# Optimizing a Trainium2 kernel written in Bass

```python
import numpy as np
import jax
import jax.numpy as jnp

def _softmax(x, axis=-1):
    return jax.nn.softmax(x, axis=axis)

def _gelu(x):
    return jax.nn.gelu(x, approximate=True)

def _silu(x):
    return jax.nn.silu(x)

def _sigmoid(x):
    return jax.nn.sigmoid(x)

def _layernorm(x, axis=-1, eps=1e-05):
    m = jnp.mean(x, axis=axis, keepdims=True)
    v = jnp.var(x, axis=axis, keepdims=True)
    return (x - m) / jnp.sqrt(v + eps)

def _scatter_add(tgt, idx, src, axis=0):
    return tgt.at[idx].add(src)

def _segment_sum(src, seg, n):
    return jax.ops.segment_sum(src, seg, n)
kernel_name = 'mk_vit_tower_d1_tok_img768_r4_33a39f'

def setup_inputs(seed: int=0):
    np.random.seed(seed)
    _w = jnp.asarray

    def _rec_inputs():
        import jax
        import jax.numpy as jnp
        _rk = jax.random.key(seed)
        x = 127.472 + 73.6052 * jax.random.normal(jax.random.fold_in(_rk, 1), (64, 224, 224, 3), jnp.float32)
        return x
    x = _rec_inputs()

    def _L0_tok_setup():
        import jax, jax.numpy as jnp
        import numpy as np
        B, H, W_IMG, C = (128, 224, 224, 3)
        P = 16
        NP = H // P * (W_IMG // P)
        D = P * P * C
        PROJ = 192

        def _img2patch(images):
            b = images.shape[0]
            x = images.reshape(b, H // P, P, W_IMG // P, P, C)
            x = x.transpose(0, 1, 3, 2, 4, 5)
            return x.reshape(b, NP, D)
        key = jax.random.key(seed)
        k1, k2, k3, k4 = jax.random.split(key, 4)
        images = jax.random.uniform(k1, (B, H, W_IMG, C), dtype=jnp.float32) * 255.0
        W = jax.random.normal(k2, (D, PROJ), dtype=jnp.float32) * 0.02
        b = jnp.zeros((PROJ,), dtype=jnp.float32)
        class_token = jax.random.normal(k3, (PROJ,), dtype=jnp.float32) * 0.02
        pos_emb = jax.random.normal(k4, (NP + 1, PROJ), dtype=jnp.float32) * 0.02
        return {'images': images, 'W': W, 'b': b, 'class_token': class_token, 'pos_emb': pos_emb}
    _L0_tok_all = _L0_tok_setup()
    _L0_tok_in = {k: v for k, v in _L0_tok_all.items() if k in ('W', 'b', 'class_token', 'pos_emb')}
    del _L0_tok_all

    def _L0_attn_setup():
        import jax, jax.numpy as jnp
        import numpy as np
        B, T, C = (2, 1024, 192)
        H = 12
        D = C // H
        SCALE = np.sqrt(D).astype(np.float32)
        key = jax.random.key(seed)
        ks = jax.random.split(key, 5)
        s = 0.02
        return {'x': jax.random.normal(ks[0], (B, T, C), dtype=jnp.float32), 'Wqkv': jax.random.normal(ks[1], (C, 3 * C), dtype=jnp.float32) * s, 'bqkv': jnp.zeros((3 * C,), dtype=jnp.float32), 'Wout': jax.random.normal(ks[2], (C, C), dtype=jnp.float32) * s, 'bout': jnp.zeros((C,), dtype=jnp.float32)}
    _L0_attn_all = _L0_attn_setup()
    _L0_attn_in = {k: v for k, v in _L0_attn_all.items() if k in ('Wqkv', 'bqkv', 'Wout', 'bout')}
    del _L0_attn_all

    def _L0_ffn_setup():
        import math
        import jax, jax.numpy as jnp
        import numpy as np
        B, L, D = (8, 1024, 192)
        E = 16
        TOP_K = 2
        F_EXP = 4 * D
        F_SH = F_EXP * 2 // 4
        key = jax.random.key(seed)
        ks = jax.random.split(key, 8)
        s = lambda fan_in: 1.0 / math.sqrt(fan_in)
        return {'hidden_states': jax.random.normal(ks[0], (B, L, D), jnp.float32), 'gate_weight': jax.random.uniform(ks[1], (E, D), jnp.float32, -s(D), s(D)), 'Wg': jax.random.uniform(ks[2], (E, F_EXP, D), jnp.float32, -s(D), s(D)), 'Wu': jax.random.uniform(ks[3], (E, F_EXP, D), jnp.float32, -s(D), s(D)), 'Wd': jax.random.uniform(ks[4], (E, D, F_EXP), jnp.float32, -s(F_EXP), s(F_EXP)), 'Ws_g': jax.random.uniform(ks[5], (F_SH, D), jnp.float32, -s(D), s(D)), 'Ws_u': jax.random.uniform(ks[6], (F_SH, D), jnp.float32, -s(D), s(D)), 'Ws_d': jax.random.uniform(ks[7], (D, F_SH), jnp.float32, -s(F_SH), s(F_SH))}
    _L0_ffn_all = _L0_ffn_setup()
    _L0_ffn_in = {k: v for k, v in _L0_ffn_all.items() if k in ('gate_weight', 'Wg', 'Wu', 'Wd', 'Ws_g', 'Ws_u', 'Ws_d')}
    del _L0_ffn_all
    return {'x': x, 'L0_tok_W': _L0_tok_in['W'], 'L0_tok_b': _L0_tok_in['b'], 'L0_tok_class_token': _L0_tok_in['class_token'], 'L0_tok_pos_emb': _L0_tok_in['pos_emb'], 'L0_attn_Wqkv': _L0_attn_in['Wqkv'], 'L0_attn_bqkv': _L0_attn_in['bqkv'], 'L0_attn_Wout': _L0_attn_in['Wout'], 'L0_attn_bout': _L0_attn_in['bout'], 'L0_ffn_gate_weight': _L0_ffn_in['gate_weight'], 'L0_ffn_Wg': _L0_ffn_in['Wg'], 'L0_ffn_Wu': _L0_ffn_in['Wu'], 'L0_ffn_Wd': _L0_ffn_in['Wd'], 'L0_ffn_Ws_g': _L0_ffn_in['Ws_g'], 'L0_ffn_Ws_u': _L0_ffn_in['Ws_u'], 'L0_ffn_Ws_d': _L0_ffn_in['Ws_d']}

def reference(x, L0_tok_W, L0_tok_b, L0_tok_class_token, L0_tok_pos_emb, L0_attn_Wqkv, L0_attn_bqkv, L0_attn_Wout, L0_attn_bout, L0_ffn_gate_weight, L0_ffn_Wg, L0_ffn_Wu, L0_ffn_Wd, L0_ffn_Ws_g, L0_ffn_Ws_u, L0_ffn_Ws_d):
    import jax
    import jax.numpy as jnp

    def _L0_tok_ref(images, W, b, class_token, pos_emb):
        import jax, jax.numpy as jnp
        import numpy as np
        B, H, W_IMG, C = (128, 224, 224, 3)
        P = 16
        NP = H // P * (W_IMG // P)
        D = P * P * C
        PROJ = 192

        def _img2patch(images):
            b = images.shape[0]
            x = images.reshape(b, H // P, P, W_IMG // P, P, C)
            x = x.transpose(0, 1, 3, 2, 4, 5)
            return x.reshape(b, NP, D)
        x = images / 255.0
        patches = _img2patch(x)
        proj = jnp.einsum('bnd,de->bne', patches, W) + b
        cls = jnp.broadcast_to(class_token, (images.shape[0], 1, PROJ))
        emb = jnp.concatenate([cls, proj], axis=1) + pos_emb
        return emb

    def _L0_attn_ref(x, Wqkv, bqkv, Wout, bout):
        import jax, jax.numpy as jnp
        import numpy as np
        B, T, C = (2, 1024, 192)
        H = 12
        D = C // H
        SCALE = np.sqrt(D).astype(np.float32)
        Bx, Tx, Cx = x.shape
        qkv = x @ Wqkv + bqkv
        qkv = qkv.reshape(Bx, Tx, 3, H, D)
        q, k, v = [jnp.moveaxis(qkv[:, :, i], 2, 1) for i in range(3)]
        attn = jnp.einsum('bhqd,bhkd->bhqk', q, k) / SCALE
        causal = jnp.tril(jnp.ones((Tx, Tx), dtype=bool))
        attn = jnp.where(causal, attn, jnp.float32(-jnp.inf))
        attn = jax.nn.softmax(attn, axis=-1)
        out = jnp.einsum('bhqk,bhkd->bhqd', attn, v)
        out = jnp.moveaxis(out, 1, 2).reshape(Bx, Tx, Cx)
        return out @ Wout + bout

    def _L0_ffn_ref(hidden_states, gate_weight, Wg, Wu, Wd, Ws_g, Ws_u, Ws_d):
        import math
        import jax, jax.numpy as jnp
        import numpy as np
        B, L, D = (8, 1024, 192)
        E = 16
        TOP_K = 2
        F_EXP = 4 * D
        F_SH = F_EXP * 2 // 4
        b, l, d = hidden_states.shape
        n = b * l
        x = hidden_states.reshape(n, d)
        scores = jax.nn.sigmoid(x @ gate_weight.T)
        capacity = math.ceil(n / E * TOP_K)
        topk_score, topk_ids = jax.lax.top_k(scores.T, capacity)
        xg = x[topk_ids]
        gate = jax.nn.silu(jnp.einsum('ecd,efd->ecf', xg, Wg))
        up = jnp.einsum('ecd,efd->ecf', xg, Wu)
        out = jnp.einsum('ecf,edf->ecd', gate * up, Wd)
        out = out * topk_score[..., None]
        y = jnp.zeros((n, d), x.dtype).at[topk_ids.reshape(-1)].add(out.reshape(-1, d))
        y = y.reshape(b, l, d)
        shared = jax.nn.silu(hidden_states @ Ws_g.T) * (hidden_states @ Ws_u.T) @ Ws_d.T
        return y + shared
    h = _L0_tok_ref(x, L0_tok_W, L0_tok_b, L0_tok_class_token, L0_tok_pos_emb)
    h = h + _L0_attn_ref(_layernorm(h, axis=-1), L0_attn_Wqkv, L0_attn_bqkv, L0_attn_Wout, L0_attn_bout)
    h = h + _L0_ffn_ref(_layernorm(h, axis=-1), L0_ffn_gate_weight, L0_ffn_Wg, L0_ffn_Wu, L0_ffn_Wd, L0_ffn_Ws_g, L0_ffn_Ws_u, L0_ffn_Ws_d)
    return h

_drawn_inputs = setup_inputs


def setup_inputs(seed=0):
    import zlib

    import numpy as np

    out = dict(_drawn_inputs(seed))
    spreads = {'L0_tok_b': (0.0, 0.1), 'L0_attn_bqkv': (0.0, 0.1), 'L0_attn_bout': (0.0, 0.1)}
    factors = {}
    for name, (base, spread) in spreads.items():
        noise = np.random.default_rng([zlib.crc32(name.encode()), seed]).standard_normal(out[name].shape)
        drawn = base * np.exp(spread * noise) if base else spread * noise
        out[name] = jnp.asarray(drawn.astype(out[name].dtype))
    for name, factor in factors.items():
        out[name] = (out[name] * factor).astype(out[name].dtype)
    return out
```

```python
from contextlib import ExitStack

import concourse.bass as bass
from concourse import mybir

ALU = mybir.AluOpType
ACT = mybir.ActivationFunctionType
AX = mybir.AxisListType
F32 = mybir.dt.float32
BF16 = mybir.dt.bfloat16
F16 = mybir.dt.float16
I32 = mybir.dt.int32

P = 128
IMAGES = 64
PATCH = 16
GRID = 14
TOK = GRID * GRID + 1
T1 = TOK - P
TILES = ((0, P), (P, T1))
D = 192
KH = D // 2
DPATCH = PATCH * PATCH * 3
KC = DPATCH // P
HEADS = 12
HH = HEADS // 2
DH = D // HEADS
VW = KH + HH
EPS = 1e-5
N = IMAGES * TOK
E = 16
CAP = (N * 2 + E - 1) // E
NBLK = (N + P - 1) // P
NPAD = NBLK * P
CHUNKS = 8
F_EXP = 4 * D
FT = F_EXP // P
F_SH = F_EXP // 2
FS = F_SH // P
ROW = D + E
BIG = -1.0e30
ST_N = 2 * TOK
assert CAP * CHUNKS == N and CAP == 4 * ST_N


def wait(eng, sem, value):
    if isinstance(value, int) and value <= 0:
        return
    eng.wait_ge(sem, value)


def stage_a(nc, dram):
    ctx = ExitStack()
    with ctx:
        def sb(name, shape, dt=F32):
            return ctx.enter_context(nc.sbuf_tensor(name, shape, dt))

        def sem(name):
            return ctx.enter_context(nc.semaphore(name))

        w_tok = sb("w_tok", [P, KC, D])
        w_qkv = sb("w_qkv", [KH, 2, 3 * D])
        w_out = sb("w_out", [KH, 2, D])
        w_gate = sb("w_gate", [KH, 2, E])
        bq = sb("bq", [KH, 2])
        bq_scaled = sb("bq_scaled", [KH, 2])
        bk = sb("bk", [KH, 2])
        bv = sb("bv", [P, D])
        bout = sb("bout", [P, D])
        pos = sb("pos", [P, 2, D])
        tokb = sb("tokb", [P, 2, D])
        ident = sb("ident", [P, P])
        ident_bf = sb("ident_bf", [P, P], BF16)
        mask0 = sb("mask0", [P, 4, P], BF16)
        mask1 = sb("mask1", [P, 2, TOK], BF16)
        sel_sum = sb("sel_sum", [VW, KH])
        minus_half = sb("minus_half", [P, 2])
        pad_scores = sb("pad_scores", [E, NPAD - N])

        patches = [sb(f"patches{u}", [P, KC, TOK]) for u in range(2)]
        h = [sb(f"h{u}", [P, 2, D]) for u in range(2)]
        h_res = [sb(f"h_res{u}", [P, 2, D]) for u in range(2)]
        stats1 = sb("stats1", [P, 2, 6])
        mv1 = sb("mv1", [P, 2, 2])
        var1 = sb("var1", [P, 2])
        rstd1 = sb("rstd1", [P, 2])
        xn = sb("xn", [P, 2, D])
        xnT = [sb(f"xnT{u}", [KH, 2, TOK]) for u in range(2)]
        qT = [sb(f"qT{u}", [KH, 2, TOK]) for u in range(2)]
        kT = [sb(f"kT{u}", [KH + 1, 2, TOK]) for u in range(2)]
        qz = [sb(f"qz{u}", [KH + 1, 2, HH, TOK]) for u in range(2)]
        vz = [sb(f"vz{u}", [P, 2, HEADS, VW]) for u in range(2)]
        mx = sb("mx", [P, 2, HEADS])
        mT = [sb(f"mT{u}", [HEADS, TOK]) for u in range(2)]
        pt0 = [sb(f"pt0_{u}", [P, HEADS, TOK]) for u in range(2)]
        pt1 = [sb(f"pt1_{u}", [P, HEADS, T1]) for u in range(2)]
        o_raw = [sb(f"o_raw{u}", [VW, 2, TOK]) for u in range(2)]
        rec = sb("rec", [VW, 2, TOK])
        oT = [sb(f"oT{u}", [KH, 2, TOK]) for u in range(2)]
        h2 = [sb(f"h2_{u}", [P, 2, D]) for u in range(2)]
        stats2 = sb("stats2", [P, 2, 6])
        mv2 = sb("mv2", [P, 2, 2])
        var2 = sb("var2", [P, 2])
        rstd2 = sb("rstd2", [P, 2])
        tab = [sb(f"tab{u}", [P, 2, ROW]) for u in range(2)]
        x2T = [sb(f"x2T{u}", [KH, 2, TOK]) for u in range(2)]
        ex = sb("ex", [P, 2, E])
        ex1 = sb("ex1", [P, 2, E])
        sT = [sb(f"sT{u}", [E, TOK]) for u in range(2)]

        ps_max = [ctx.enter_context(nc.psum_tensor(f"ps_max{i}", [P, 512], F32)) for i in range(3)]
        ps_st = [ctx.enter_context(nc.psum_tensor(f"ps_st{i}", [P, 512], F32)) for i in range(2)]
        ps5 = ctx.enter_context(nc.psum_tensor("ps5", [P, 512], F32))
        ps6 = ctx.enter_context(nc.psum_tensor("ps6", [P, 512], F32))
        ps7 = ctx.enter_context(nc.psum_tensor("ps7", [P, 512], F32))

        const_ld = sem("const_ld")
        const_pool = sem("const_pool")
        const_dve = sem("const_dve")
        const_act = sem("const_act")
        pad_out = sem("pad_out")
        cls_ld = sem("cls_ld")
        passed = sem("passed")
        pat_ld = [sem(f"pat_ld{u}") for u in range(2)]
        tok_ps = sem("tok_ps")
        h_ready = sem("h_ready")
        st1 = sem("st1")
        mv1_s = sem("mv1_s")
        var1_s = sem("var1_s")
        rstd1_s = sem("rstd1_s")
        xn_ready = sem("xn_ready")
        xnT_ps = sem("xnT_ps")
        xnT_ready = sem("xnT_ready")
        q_ps = sem("q_ps")
        q_ready = sem("q_ready")
        qz_ld = [sem(f"qz_ld{u}") for u in range(2)]
        k_ps = sem("k_ps")
        k_ready = sem("k_ready")
        v_ps = sem("v_ps")
        v_ready = sem("v_ready")
        hres_ready = sem("hres_ready")
        mx_ps = sem("mx_ps")
        mx_red = sem("mx_red")
        mT_ps = sem("mT_ps")
        mT_ready = sem("mT_ready")
        mrow_ld = [sem(f"mrow_ld{u}") for u in range(2)]
        st_ps = sem("st_ps")
        exp_done = sem("exp_done")
        sel_done = sem("sel_done")
        pv_ps = sem("pv_ps")
        pv_used = sem("pv_used")
        rec_ready = sem("rec_ready")
        bc_ps = sem("bc_ps")
        oT_ready = sem("oT_ready")
        wo_ps = sem("wo_ps")
        h2_ready = sem("h2_ready")
        st2 = sem("st2")
        mv2_s = sem("mv2_s")
        var2_s = sem("var2_s")
        rstd2_s = sem("rstd2_s")
        xn2_ready = sem("xn2_ready")
        x2T_ps = sem("x2T_ps")
        x2T_ready = sem("x2T_ready")
        lg_ps = sem("lg_ps")
        lg_used = sem("lg_used")
        ex1_s = sem("ex1_s")
        sc_ready = sem("sc_ready")
        sT_ps = sem("sT_ps")
        sT_ready = sem("sT_ready")
        h2_out = [sem(f"h2_out{u}") for u in range(2)]
        x2T_out = [sem(f"x2T_out{u}") for u in range(2)]
        tab_out = [sem(f"tab_out{u}") for u in range(2)]
        sT_out = [sem(f"sT_out{u}") for u in range(2)]

        CONST_LOADS = 12
        CONST_POOL = 22

        def slots(eng, slot):
            def parts(s):
                return dict(a=s + 1 < IMAGES, b=0 <= s < IMAGES, c=s >= 1)
            for s in range(-1, 3):
                slot(s, s % 2, **parts(s))
            with eng.Fori(0, (IMAGES - 6) // 2) as it:
                for u in range(2):
                    slot(it * 2 + (3 + u), (3 + u) % 2, a=True, b=True, c=True)
            for s in range(IMAGES - 3, IMAGES + 1):
                slot(s, s % 2, **parts(s))

        def wait_apart(eng, s, value):
            wait(eng, s, value)
            if not isinstance(value, int):
                eng.sem_inc(passed, 1)

        block = ctx.enter_context(nc.Block())

        @block.sync
        def _(sp):
            for dst, src in ((w_tok[:], dram["tok_W"].rearrange("(c p) n -> p c n", p=P)),
                             (w_qkv[:], dram["Wqkv"].rearrange("(c p) n -> p c n", p=KH)),
                             (w_out[:], dram["Wout"].rearrange("(c p) n -> p c n", p=KH)),
                             (w_gate[:], dram["gateT"].rearrange("(c p) n -> p c n", p=KH)),
                             (bv[:], dram["bqkv"][None, 2 * D:3 * D].to_broadcast([P, D])),
                             (bout[:], dram["bout"][None, :].to_broadcast([P, D])),
                             (pos[:, 0, :], dram["pos"][0:P, :]),
                             (pos[0:T1, 1, :], dram["pos"][P:TOK, :]),
                             (tokb[:, 0, :], dram["tok_b"][None, :].to_broadcast([P, D])),
                             (tokb[:, 1, :], dram["tok_b"][None, :].to_broadcast([P, D]))):
                sp.dma_start(dst, src).then_inc(const_ld, 16)
            with nc.allow_non_contiguous_dma(reason="two short bias columns"):
                sp.dma_start(bq[:], dram["bqkv"][0:D].rearrange("(c p) -> p c", p=KH)).then_inc(const_ld, 16)
                sp.dma_start(bk[:], dram["bqkv"][D:2 * D].rearrange("(c p) -> p c", p=KH)).then_inc(const_ld, 16)
            sp.wait_ge(const_ld, 16 * CONST_LOADS)
            sp.dma_start(tokb[0:1, 0, :], dram["cls"][None, :]).then_inc(cls_ld, 16)
            sp.wait_ge(const_pool, CONST_POOL)
            sp.dma_start(dram["sT"][:, N:NPAD], pad_scores[:]).then_inc(pad_out, 16)
            sp.wait_ge(pad_out, 16)
            for u in range(2):
                sp.dma_start(patches[u][:], dram["patches"][u]).then_inc(pat_ld[u], 16)

            def slot(s, u, a, b, c):
                v = 1 - u
                if b and not (isinstance(s, int) and s + 2 >= IMAGES):
                    wait_apart(sp, tok_ps, s + 1)
                    sp.dma_start(patches[u][:], dram["patches"][s + 2]).then_inc(pat_ld[u], 16)
                if a:
                    wait_apart(sp, q_ready, s + 2)
                    wait_apart(sp, st_ps, 8 * s)
                    for j in range(HH):
                        r = slice(DH * j, DH * (j + 1))
                        sp.dma_start(qz[v][r, :, j, :], qT[v][r, :, :]).then_inc(qz_ld[v], 16)
                if b:
                    wait(sp, mT_ready, s + 1)
                    sp.dma_start(qz[u][KH:KH + 1, :, :, :].rearrange("p a j t -> p (a j) t"),
                                 mT[u][:, :]).then_inc(mrow_ld[u], 16)
                if c:
                    wait_apart(sp, h2_ready, s)
                    base = (s - 1) * TOK
                    sp.dma_start(dram["h2"][bass.ds(base, P), :], h2[v][:, 0, :]).then_inc(h2_out[v], 16)
                    sp.dma_start(dram["h2"][bass.ds(base + P, T1), :], h2[v][0:T1, 1, :]).then_inc(h2_out[v], 16)
                    wait_apart(sp, x2T_ready, s)
                    sp.dma_start(dram["x2T"][:, :, bass.ds(base, TOK)], x2T[v][:]).then_inc(x2T_out[v], 16)
                    wait_apart(sp, sc_ready, s)
                    sp.dma_start(dram["tab"][bass.ds(base, P), :], tab[v][:, 0, :]).then_inc(tab_out[v], 16)
                    sp.dma_start(dram["tab"][bass.ds(base + P, T1), :], tab[v][0:T1, 1, :]).then_inc(tab_out[v], 16)
                    wait_apart(sp, sT_ready, s)
                    sp.dma_start(dram["sT"][:, bass.ds(base, TOK)], sT[v][:]).then_inc(sT_out[v], 16)

            slots(sp, slot)
            for u in range(2):
                sp.wait_ge(h2_out[u], 32 * IMAGES // 2)
                sp.wait_ge(x2T_out[u], 16 * IMAGES // 2)
                sp.wait_ge(tab_out[u], 32 * IMAGES // 2)
                sp.wait_ge(sT_out[u], 16 * IMAGES // 2)

        @block.gpsimd
        def _(pool):
            made = [0]

            def made_one(ins):
                made[0] += 1
                ins.then_inc(const_pool, 1)
                pool.wait_ge(const_pool, made[0])

            for t, val in ((ident, 0.0), (sel_sum, 0.0), (mask0, 0.0), (mask1, 0.0), (minus_half, -0.5),
                           (pad_scores, -1.0), (mv1, 0.0), (mv2, 0.0), (rec, 0.0),
                           (qz[0], 0.0), (qz[1], 0.0), (vz[0], 0.0), (vz[1], 0.0)):
                made_one(pool.memset(t[:], val))
            for u in range(2):
                made_one(pool.memset(kT[u][KH:KH + 1, :, :], 1.0))
            made_one(pool.affine_select(out=ident[:], in_=ident[:], compare_op=ALU.not_equal, fill=1.0, base=0,
                                        pattern=[[-1, P]], channel_multiplier=1))
            made_one(pool.affine_select(out=sel_sum[:].rearrange("p (j d) -> p j d", j=HH),
                                        in_=sel_sum[:].rearrange("p (j d) -> p j d", j=HH),
                                        compare_op=ALU.not_equal, fill=1.0, base=-KH,
                                        pattern=[[-1, HH], [0, DH]], channel_multiplier=1))
            made_one(pool.affine_select(out=mask0[:], in_=mask0[:], compare_op=ALU.is_ge, fill=BIG, base=0,
                                        pattern=[[0, 4], [-1, P]], channel_multiplier=1))
            made_one(pool.affine_select(out=mask1[:], in_=mask1[:], compare_op=ALU.is_ge, fill=BIG, base=P,
                                        pattern=[[0, 2], [-1, TOK]], channel_multiplier=1))
            for u in range(2):
                ones = vz[u][:, :, :, KH:VW].rearrange("p t (a j) c -> p (t a) j c", a=2)
                made_one(pool.affine_select(out=ones, in_=ones, compare_op=ALU.not_equal, fill=1.0, base=0,
                                            pattern=[[0, 4], [1, HH], [-1, HH]], channel_multiplier=0))
            made_one(pool.tensor_copy(ident_bf[:], ident[:]))
            assert made[0] == CONST_POOL, made[0]
            pool.wait_ge(const_ld, 16 * CONST_LOADS)

            def slot(s, u, a, b, c):
                v = 1 - u
                if a:
                    wait(pool, var1_s, s + 2)
                    pool.tensor_tensor(rstd1[:], var1[:], minus_half[:], ALU.pow).then_inc(rstd1_s, 1)
                if b:
                    wait(pool, h_ready, s + 1)
                    wait(pool, h2_ready, s - 1)
                    bo = bout[:, None, :].to_broadcast([P, 2, D])
                    pool.tensor_tensor(h_res[u][:, 0, :], h[u][:, 0, :], bout[:], ALU.add)
                    pool.tensor_tensor(h_res[u][0:T1, 1, :], h[u][0:T1, 1, :], bout[0:T1, :], ALU.add)\
                        .then_inc(hres_ready, 1)
                if c:
                    wait(pool, var2_s, s)
                    pool.tensor_tensor(rstd2[:], var2[:], minus_half[:], ALU.pow).then_inc(rstd2_s, 1)
                if b:
                    for unit in range(8):
                        half, part = divmod(unit, 4)
                        wait_apart(pool, exp_done, 8 * s + unit + 1)
                        if part < 3:
                            hd = half * HH + 2 * part
                            x = pt0[u][:, hd:hd + 2, 0:P]
                            n, w = 2, P
                        else:
                            x = pt1[u][0:T1, half * HH:(half + 1) * HH, :]
                            n, w = HH, T1
                        pool.affine_select(out=x, in_=x, compare_op=ALU.is_ge, fill=0.0, base=0,
                                           pattern=[[0, n], [1, w]], channel_multiplier=-1).then_inc(sel_done, 1)

            slots(pool, slot)

        @block.scalar
        def _(act):
            act.wait_ge(const_ld, 16 * CONST_LOADS)
            act.activation(bq_scaled[:], bq[:], ACT.Copy, scale=DH ** -0.5).then_inc(const_act, 1)
            act.wait_ge(const_act, 1)

            def slot(s, u, a, b, c):
                v = 1 - u
                if a:
                    wait(act, xnT_ps, s + 2)
                    wait(act, v_ps, s)
                    act.activation(xnT[v][:], ps7[0:KH, 0:ST_N].rearrange("p (a t) -> p a t", a=2), ACT.Copy)\
                        .then_inc(xnT_ready, 1)
                    wait(act, q_ps, s + 2)
                    if not isinstance(s, int) or s >= 1:
                        wait(act, qz_ld[v], (s + 1 - v) * (16 * HH // 2))
                    for half in range(2):
                        last = act.activation(qT[v][:, half, :], ps6[0:KH, half * TOK:(half + 1) * TOK], ACT.Identity,
                                       scale=DH ** -0.5, bias=bq_scaled[:, half:half + 1])
                    last.then_inc(q_ready, 1)
                    wait(act, k_ps, s + 2)
                    wait(act, st_ps, 8 * s)
                    for half in range(2):
                        last = act.activation(kT[v][0:KH, half, :], ps7[0:KH, half * TOK:(half + 1) * TOK], ACT.Identity,
                                       bias=bk[:, half:half + 1])
                    last.then_inc(k_ready, 1)
                if b:
                    wait(act, mT_ps, s + 1)
                    if not isinstance(s, int) or s >= 2:
                        wait(act, mrow_ld[u], (s - u) * 8)
                    act.activation(mT[u][:], ps6[0:HEADS, 0:TOK], ACT.Copy, scale=-1.0).then_inc(mT_ready, 1)
                if c:
                    wait(act, x2T_ps, s)
                    if not isinstance(s, int) or s >= 3:
                        wait(act, x2T_out[v], (s - 1 - v) * 8)
                    act.activation(x2T[v][:], ps7[0:KH, 0:ST_N].rearrange("p (a t) -> p a t", a=2), ACT.Copy)\
                        .then_inc(x2T_ready, 1)

                def exps(half):
                    if half == 0:
                        wait(act, pv_ps, s - 1)
                    for part in range(4):
                        unit = 4 * half + part
                        wait(act, st_ps, 8 * s + unit + 1)
                        if part < 3:
                            hd = half * HH + 2 * part
                            act.activation(pt0[u][:, hd:hd + 2, :],
                                           ps_st[unit % 2][:, 0:ST_N].rearrange("p (j t) -> p j t", j=2), ACT.Exp)\
                                .then_inc(exp_done, 1)
                        else:
                            act.activation(pt1[u][0:T1, half * HH:(half + 1) * HH, :],
                                           ps_st[unit % 2][0:T1, 0:HH * T1].rearrange("p (j t) -> p j t", j=HH),
                                           ACT.Exp).then_inc(exp_done, 1)
                if b:
                    exps(0)
                if c:
                    wait(act, lg_ps, s)
                    wait(act, ex1_s, s - 1)
                    act.activation(ex[:, 0, :], ps5[:, 0:E], ACT.Exp, scale=-1.0)
                    act.activation(ex[0:T1, 1, :], ps5[0:T1, E:2 * E], ACT.Exp, scale=-1.0).then_inc(lg_used, 1)
                if b:
                    exps(1)
                if c:
                    wait(act, sT_ps, s)
                    if not isinstance(s, int) or s >= 3:
                        wait(act, sT_out[v], (s - 1 - v) * 8)
                    act.activation(sT[v][:], ps6[0:E, 0:TOK], ACT.Copy).then_inc(sT_ready, 1)
                if b:
                    wait(act, pv_ps, s + 1)
                    wait(act, oT_ready, s - 1)
                    act.activation(o_raw[u][:], ps7[0:VW, 0:ST_N].rearrange("p (a t) -> p a t", a=2), ACT.Copy)\
                        .then_inc(pv_used, 1)

            slots(act, slot)

        @block.vector
        def _(dve):
            vec = nc.vector
            dve.wait_ge(const_ld, 16 * CONST_LOADS)
            dve.wait_ge(cls_ld, 16)
            dve.wait_ge(const_pool, CONST_POOL)
            vec.tensor_tensor(pos[:, 0, :], pos[:, 0, :], tokb[:, 0, :], ALU.add).then_inc(const_dve, 1)
            vec.tensor_tensor(pos[0:T1, 1, :], pos[0:T1, 1, :], tokb[0:T1, 1, :], ALU.add).then_inc(const_dve, 1)
            dve.wait_ge(const_dve, 2)

            def stats(x, st, st_s, mv, mv_s, var, var_s, i):
                for t, (_, n) in enumerate(TILES):
                    last = vec.bn_stats(st[0:n, t, :], x[0:n, t, :])
                last.then_inc(st_s, 1)
                wait_apart(dve, st_s, i + 1)
                for t, (_, n) in enumerate(TILES):
                    last = vec.bn_aggr(mv[0:n, t, :], st[0:n, t, :])
                last.then_inc(mv_s, 1)
                wait(dve, mv_s, i + 1)
                vec.tensor_scalar(var[:], mv[:, :, 1], EPS, None, ALU.add).then_inc(var_s, 1)

            def slot(s, u, a, b, c):
                v = 1 - u
                if c:
                    wait(dve, pv_used, s)
                    wait(dve, bc_ps, s - 1)
                    vec.reciprocal(rec[KH:VW, :, :], o_raw[v][KH:VW, :, :]).then_inc(rec_ready, 1)
                if a:
                    wait(dve, tok_ps, s + 2)
                    wait(dve, hres_ready, s)
                    for t, (_, n) in enumerate(TILES):
                        last = vec.scalar_tensor_tensor(h[v][0:n, t, :], ps5[0:n, t * D:(t + 1) * D], 1.0 / 255.0,
                                                 pos[0:n, t, :], ALU.mult, ALU.add)
                    last.then_inc(h_ready, 1)
                    wait(dve, h_ready, s + 2)
                    wait(dve, xn_ready, s + 1)
                    stats(h[v], stats1, st1, mv1, mv1_s, var1, var1_s, s + 1)

                def maxima(lo, hi):
                    for m in range(lo, hi):
                        wait(dve, mx_ps, 9 * s + m + 1)
                        if m == 0:
                            wait(dve, mT_ps, s)
                        if m < 3:
                            vec.tensor_reduce(mx[:, 0, 4 * m:4 * m + 4],
                                              ps_max[m % 3][:, :].rearrange("p (j t) -> p j t", j=4),
                                              AX.X, ALU.max).then_inc(mx_red, 1)
                        else:
                            hd = 2 * (m - 3)
                            vec.tensor_reduce(mx[0:T1, 1, hd:hd + 2],
                                              ps_max[m % 3][0:T1, 0:ST_N].rearrange("p (j t) -> p j t", j=2),
                                              AX.X, ALU.max).then_inc(mx_red, 1)
                if b:
                    maxima(0, 3)
                if a:
                    wait(dve, rstd1_s, s + 2)
                    wait(dve, xnT_ps, s + 1)
                    for t, (_, n) in enumerate(TILES):
                        last = vec.tensor_scalar(xn[0:n, t, :], h[v][0:n, t, :], mv1[0:n, t, 0:1], rstd1[0:n, t:t + 1],
                                          ALU.subtract, ALU.mult)
                    last.then_inc(xn_ready, 1)
                if b:
                    maxima(3, 9)
                if c:
                    wait(dve, bc_ps, s)
                    wait(dve, wo_ps, s - 2)
                    vec.tensor_tensor(oT[v][:], o_raw[v][0:KH, :, :],
                                      ps6[0:KH, 0:ST_N].rearrange("p (a t) -> p a t", a=2), ALU.mult)\
                        .then_inc(oT_ready, 1)
                    wait(dve, wo_ps, s)
                    if not isinstance(s, int) or s >= 3:
                        wait(dve, h2_out[v], (s - 1 - v) * 16)
                    wait(dve, hres_ready, s)
                    for t, (_, n) in enumerate(TILES):
                        last = vec.tensor_tensor(h2[v][0:n, t, :], ps5[0:n, t * D:(t + 1) * D], h_res[v][0:n, t, :],
                                          ALU.add)
                    last.then_inc(h2_ready, 1)
                    wait(dve, h2_ready, s)
                    wait(dve, xn2_ready, s - 1)
                    stats(h2[v], stats2, st2, mv2, mv2_s, var2, var2_s, s - 1)
                if a:
                    wait(dve, v_ps, s + 2)
                    wait(dve, pv_ps, s)
                    for t, (_, n) in enumerate(TILES):
                        for half in range(2):
                            dst = vz[v][0:n, t, half * HH:(half + 1) * HH, :].rearrange("p j c -> p (j c)")
                            dst = bass.AP(tensor=dst.tensor, offset=dst.offset,
                                          ap=[list(dst.ap[0]), [VW + DH, HH], [1, DH]])
                            col = t * D + half * KH
                            last = vec.tensor_tensor(dst, ps5[0:n, col:col + KH].rearrange("p (j d) -> p j d", j=HH),
                                                    bv[0:n, half * KH:(half + 1) * KH]
                                                    .rearrange("p (j d) -> p j d", j=HH), ALU.add)
                    last.then_inc(v_ready, 1)
                if c:
                    wait(dve, rstd2_s, s)
                    if not isinstance(s, int) or s >= 3:
                        wait(dve, tab_out[v], (s - 1 - v) * 16)
                    for t, (_, n) in enumerate(TILES):
                        last = vec.tensor_scalar(tab[v][0:n, t, 0:D], h2[v][0:n, t, :], mv2[0:n, t, 0:1],
                                          rstd2[0:n, t:t + 1], ALU.subtract, ALU.mult)
                    last.then_inc(xn2_ready, 1)
                    wait(dve, lg_used, s)
                    wait(dve, sc_ready, s - 1)
                    vec.tensor_scalar(ex1[:, 0, :], ex[:, 0, :], 1.0, None, ALU.add)
                    vec.tensor_scalar(ex1[0:T1, 1, :], ex[0:T1, 1, :], 1.0, None, ALU.add).then_inc(ex1_s, 1)
                    wait(dve, ex1_s, s)
                    vec.reciprocal(tab[v][:, 0, D:ROW], ex1[:, 0, :])
                    vec.reciprocal(tab[v][0:T1, 1, D:ROW], ex1[0:T1, 1, :]).then_inc(sc_ready, 1)

            slots(dve, slot)

        @block.tensor
        def _(pe):
            mm = nc.tensor.matmul
            pe.wait_ge(const_ld, 16 * CONST_LOADS)
            pe.wait_ge(const_pool, CONST_POOL)

            def transposes(dst, src, n_of):
                for t, (t0, n) in enumerate(TILES):
                    for half in range(2):
                        last = nc.tensor.transpose(dst[0:KH, half * TOK + t0:half * TOK + t0 + n],
                                                   src[0:n, t, half * KH:(half + 1) * KH], ident[0:n, 0:n])
                return last

            def slot(s, u, a, b, c):
                v = 1 - u
                if a:
                    wait(pe, pat_ld[v], (s + 1 - v) * 8 + 16)
                    if isinstance(s, int) and s <= 1:
                        wait(pe, v_ready, s + 1)
                    else:
                        wait(pe, lg_used, s - 1)
                    for t, (t0, n) in enumerate(TILES):
                        for k in range(KC):
                            last = mm(ps5[0:n, t * D:(t + 1) * D], patches[v][:, k, t0:t0 + n], w_tok[:, k, :],
                                      start=k == 0, stop=k == KC - 1)
                    last.then_inc(tok_ps, 1)
                if b:
                    wait(pe, qz_ld[u], (s - u) * (16 * HH // 2) + 16 * HH)
                    wait(pe, k_ready, s + 1)
                    for m in range(9):
                        bank = ps_max[m % 3]
                        wait(pe, mx_red, 9 * s + m - 2)
                        if m < 3:
                            mm(bank[:, :], ident_bf[:], mask0[:].rearrange("p j t -> p (j t)"), start=True, stop=False)
                            for j in range(4):
                                half, hd = divmod(4 * m + j, HH)
                                last = mm(bank[:, j * P:(j + 1) * P], qz[u][0:KH, half, hd, 0:P],
                                          kT[u][0:KH, half, 0:P], start=False, stop=j == 3)
                        else:
                            mm(bank[0:T1, 0:ST_N], ident_bf[0:T1, 0:T1], mask1[0:T1].rearrange("p j t -> p (j t)"),
                               start=True, stop=False)
                            for j in range(2):
                                half, hd = divmod(2 * (m - 3) + j, HH)
                                last = mm(bank[0:T1, j * TOK:(j + 1) * TOK], qz[u][0:KH, half, hd, P:TOK],
                                          kT[u][0:KH, half, :], start=False, stop=j == 1)
                        last.then_inc(mx_ps, 1)
                if c:
                    wait(pe, rec_ready, s)
                    if isinstance(s, int) and s == 1:
                        wait(pe, mT_ready, s)
                    else:
                        wait(pe, sT_ready, s - 1)
                    mm(ps6[0:KH, 0:ST_N], sel_sum[:], rec[:].rearrange("p a t -> p (a t)"), start=True, stop=True)\
                        .then_inc(bc_ps, 1)
                if a:
                    wait(pe, xn_ready, s + 2)
                    if isinstance(s, int) and s == 0:
                        wait(pe, k_ready, s + 1)
                    else:
                        wait(pe, pv_used, s)
                    transposes(ps7, xn, TILES).then_inc(xnT_ps, 1)
                if c:
                    wait(pe, oT_ready, s)
                    if a:
                        wait(pe, h_ready, s + 2)
                    else:
                        wait(pe, lg_used, s - 1)
                    for t, (t0, n) in enumerate(TILES):
                        for half in range(2):
                            last = mm(ps5[0:n, t * D:(t + 1) * D], oT[v][:, half, t0:t0 + n], w_out[:, half, :],
                                      start=half == 0, stop=half == 1)
                    last.then_inc(wo_ps, 1)
                if a:
                    wait(pe, xnT_ready, s + 2)
                    if c:
                        wait(pe, oT_ready, s)
                    else:
                        wait(pe, q_ready, s + 1)
                    for which, bank, done in ((0, ps6, q_ps), (1, ps7, k_ps)):
                        for half in range(2):
                            for k in range(2):
                                col = which * D + half * KH
                                last = mm(bank[0:KH, half * TOK:(half + 1) * TOK], w_qkv[:, k, col:col + KH],
                                          xnT[v][:, k, :], start=k == 0, stop=k == 1)
                        last.then_inc(done, 1)
                    if c:
                        wait(pe, h2_ready, s)
                    else:
                        wait(pe, h_ready, s + 2)
                    for t, (t0, n) in enumerate(TILES):
                        for k in range(2):
                            last = mm(ps5[0:n, t * D:(t + 1) * D], xnT[v][:, k, t0:t0 + n], w_qkv[:, k, 2 * D:3 * D],
                                      start=k == 0, stop=k == 1)
                    last.then_inc(v_ps, 1)
                if b:
                    wait(pe, mx_red, 9 * s + 9)
                    if a:
                        wait(pe, q_ready, s + 2)
                    else:
                        wait(pe, oT_ready, s)
                    for t, (t0, n) in enumerate(TILES):
                        last = nc.tensor.transpose(ps6[0:HEADS, t0:t0 + n], mx[0:n, t, :], ident[0:n, 0:n])
                    last.then_inc(mT_ps, 1)
                if c:
                    wait(pe, xn2_ready, s)
                    if a:
                        wait(pe, k_ready, s + 2)
                    else:
                        wait(pe, pv_used, s)
                    transposes(ps7, tab[v], TILES).then_inc(x2T_ps, 1)

                def scores(half):
                    for part in range(4):
                        unit = 4 * half + part
                        bank = ps_st[unit % 2]
                        wait(pe, exp_done, 8 * s + unit - 1)
                        if part < 3:
                            last = mm(bank[:, 0:ST_N], kT[u][:, half, 0:P],
                                      qz[u][:, half, 2 * part:2 * part + 2, :], start=True, stop=True)
                        else:
                            last = mm(bank[0:T1, 0:HH * T1], kT[u][:, half, P:TOK], qz[u][:, half, :, P:TOK],
                                      start=True, stop=True)
                        last.then_inc(st_ps, 1)
                if b:
                    wait(pe, mrow_ld[u], (s - u) * 8 + 16)
                    scores(0)
                if c:
                    wait(pe, x2T_ready, s)
                    if a:
                        wait(pe, v_ready, s + 2)
                    else:
                        wait(pe, h2_ready, s)
                    for t, (t0, n) in enumerate(TILES):
                        for k in range(2):
                            last = mm(ps5[0:n, t * E:(t + 1) * E], x2T[v][:, k, t0:t0 + n], w_gate[:, k, :],
                                      start=k == 0, stop=k == 1)
                    last.then_inc(lg_ps, 1)
                if b:
                    scores(1)
                if c:
                    wait(pe, sc_ready, s)
                    if b:
                        wait(pe, mT_ready, s + 1)
                    else:
                        wait(pe, oT_ready, s)
                    for t, (t0, n) in enumerate(TILES):
                        last = nc.tensor.transpose(ps6[0:E, t0:t0 + n], tab[v][0:n, t, D:ROW], ident[0:n, 0:n])
                    last.then_inc(sT_ps, 1)
                if b:
                    wait(pe, v_ready, s + 1)
                    if c:
                        wait(pe, x2T_ready, s)
                    else:
                        wait(pe, k_ready, s + 2)
                    for half in range(2):
                        wait(pe, sel_done, 8 * s + 4 * half + 4)
                        for j in range(HH):
                            hd = half * HH + j
                            mm(ps7[0:VW, half * TOK:(half + 1) * TOK], vz[u][:, 0, hd, :], pt0[u][:, hd, :],
                               start=j == 0, stop=False)
                            last = mm(ps7[0:VW, half * TOK + P:(half + 1) * TOK], vz[u][0:T1, 1, hd, :],
                                      pt1[u][0:T1, hd, :], start=False, stop=j == HH - 1)
                    last.then_inc(pv_ps, 1)

            slots(pe, slot)




CH = ST_N
SH_CHUNKS = N // CH
STEPS = 32
GT = (CAP + P - 1) // P
LAST = CAP - (GT - 1) * P
IDX_GROUPS = ((0, 3), (3, 6), (6, 9), (9, 12), (12, GT))
assert SH_CHUNKS == 2 * E and STEPS == 4 * (SH_CHUNKS // 4)


def rows_of(t):
    return P if t < GT - 1 else LAST


def stage_s(nc, dram, idx_all):
    ctx = ExitStack()
    with ctx:
        def sb(name, shape, dt=F32):
            return ctx.enter_context(nc.sbuf_tensor(name, shape, dt))

        def sem(name):
            return ctx.enter_context(nc.semaphore(name))

        wsg = sb("wsg", [KH, 2, F_SH])
        wsu = sb("wsu", [KH, 2, F_SH])
        wsd = sb("wsd", [P, FS, D])
        xs = [sb(f"xs{u}", [KH, 2, CH]) for u in range(2)]
        hs = [sb(f"hs{u}", [P, 4, D]) for u in range(2)]
        sg = [sb(f"sg{u}", [P, CH]) for u in range(2)]
        hid = [sb(f"hid{u}", [P, FS, CH]) for u in range(2)]
        os_ = [sb(f"os{u}", [P, 4, D]) for u in range(2)]

        s1 = sb("s1", [P, CAP])
        hits = sb("hits", [P, CAP], BF16)
        cnt = sb("cnt", [P, 1])
        thr = sb("thr", [P, 1], I32)
        cand = sb("cand", [P, 1], I32)
        inc = sb("inc", [P, 1], I32)
        bitf = sb("bitf", [P, 1])
        biti = sb("biti", [P, 1], I32)
        same_expert = sb("same_expert", [P, P])
        s2 = sb("s2", [NBLK, E, P])
        thr_b = sb("thr_b", [NBLK, E])
        mask = sb("mask", [NBLK, E * P])
        keep_run = sb("keep_run", [NBLK, E * P])
        g_run = sb("g_run", [NBLK, E * P])
        e_run = sb("e_run", [NBLK, E * P])
        tots = sb("tots", [NBLK, 2 * E])
        before = sb("before", [NBLK, 2 * E])
        need = sb("need", [NBLK, E])
        lo = sb("lo", [NBLK, E])
        hi = sb("hi", [NBLK, E])
        earlier = sb("earlier", [NBLK, NBLK])
        ones = sb("ones", [NBLK, NBLK])
        rank = sb("rank", [NBLK, E, P + 1], F16)
        slot_no = sb("slot_no", [NBLK, CAP], F16)
        ge = sb("ge", [NBLK, CAP], F16)
        onehot = sb("onehot", [NBLK, CAP], F16)
        jcol = sb("jcol", [P, GT])
        junk = sb("junk", [P, GT, P], BF16)
        bcol = sb("bcol", [P, GT])
        acol = sb("acol", [P, GT])

        ps_g = [ctx.enter_context(nc.psum_tensor(f"ps_g{i}", [P, 512], F32)) for i in range(2)]
        ps_u = [ctx.enter_context(nc.psum_tensor(f"ps_u{i}", [P, 512], F32)) for i in range(2)]
        ps_d = [ctx.enter_context(nc.psum_tensor(f"ps_d{i}", [P, 512], F32)) for i in range(2)]
        ps_i = [ctx.enter_context(nc.psum_tensor(f"ps_i{i}", [P, 512], F32)) for i in range(2)]

        wld = sem("wld")
        s_ld = sem("s_ld")
        cst = sem("cst")
        xs_ld = [sem(f"xs_ld{u}") for u in range(2)]
        hs_ld = [sem(f"hs_ld{u}") for u in range(2)]
        g_ps = sem("g_ps")
        sg_ready = sem("sg_ready")
        hid_ready = sem("hid_ready")
        dn_ps = sem("dn_ps")
        os_ready = sem("os_ready")
        os_out = [sem(f"os_out{u}") for u in range(2)]
        thr_init = sem("thr_init")
        cand_s = sem("cand_s")
        cnt_s = sem("cnt_s")
        cnt_ps = sem("cnt_ps")
        inc_s = sem("inc_s")
        bit_s = sem("bit_s")
        bitf_s = sem("bitf_s")
        thr_s = sem("thr_s")
        thr_st = sem("thr_st")
        thr_ld = sem("thr_ld")
        rk = sem("rk")
        rk_ps = sem("rk_ps")
        oh_ge = sem("oh_ge")
        oh_s = sem("oh_s")
        ix_ps = sem("ix_ps")
        ix_used = sem("ix_used")
        list_s = sem("list_s")
        passed = sem("passed_s")
        CST = 12
        NG = len(IDX_GROUPS)

        def wait_apart(eng, s, value):
            wait(eng, s, value)
            if not isinstance(value, int):
                eng.sem_inc(passed, 1)

        def chunks(eng, chunk, middle):
            half = SH_CHUNKS // 2
            for lo_c, hi_c, second in ((0, half, False), (half, SH_CHUNKS, True)):
                start = lo_c
                if not second:
                    for c in range(2):
                        chunk(c, c % 2, False)
                    start = lo_c + 2
                stop = hi_c - 2 if second else hi_c
                with eng.Fori(0, (stop - start) // 2) as it:
                    for u in range(2):
                        chunk(it * 2 + (start + u), (start + u) % 2, second)
                if second:
                    for c in range(hi_c - 2, hi_c):
                        chunk(c, c % 2, True)
                else:
                    middle()

        block = ctx.enter_context(nc.Block())

        @block.sync
        def _(sp):
            for e in range(E):
                sp.dma_start(s1[e * CHUNKS:(e + 1) * CHUNKS, :],
                             dram["sT"][e, 0:N].rearrange("(c t) -> c t", c=CHUNKS)).then_inc(s_ld, 16)
            for dst, src in ((wsg, "WsgT"), (wsu, "WsuT"), (wsd, "WsdT")):
                sp.dma_start(dst[:], dram[src]).then_inc(wld, 16)
            sp.dma_start(s2[:], dram["sT"].rearrange("e (a b) -> a e b", b=P)).then_inc(wld, 16)

            def load_x(c, u):
                sp.dma_start(xs[u][:], dram["x2T"][:, :, bass.ds(c * CH, CH)]).then_inc(xs_ld[u], 16)

            def load_h(c, u):
                for i in range(2):
                    sp.dma_start(hs[u][:, 2 * i, :], dram["h2"][bass.ds(c * CH + i * TOK, P), :])\
                        .then_inc(hs_ld[u], 16)
                    sp.dma_start(hs[u][0:T1, 2 * i + 1, :], dram["h2"][bass.ds(c * CH + i * TOK + P, T1), :])\
                        .then_inc(hs_ld[u], 16)

            load_x(0, 0)
            load_h(0, 0)

            def chunk(c, u, second):
                more = not (isinstance(c, int) and c + 1 >= SH_CHUNKS)
                if more:
                    wait_apart(sp, g_ps, FS * c)
                    load_x(c + 1, 1 - u)
                if not (isinstance(c, int) and c == 0):
                    for i in range(2):
                        store(c - 1, 1 - u, i)
                if more:
                    load_h(c + 1, 1 - u)

            def store(c, u, i):
                wait_apart(sp, os_ready, 2 * c + i + 1)
                sp.dma_start(dram["out"][bass.ds(c * CH + i * TOK, P), :], os_[u][:, 2 * i, :])\
                    .then_inc(os_out[u], 16)
                sp.dma_start(dram["out"][bass.ds(c * CH + i * TOK + P, T1), :], os_[u][0:T1, 2 * i + 1, :])\
                    .then_inc(os_out[u], 16)

            def middle():
                sp.wait_ge(thr_s, STEPS)
                sp.dma_start(dram["thr"], thr[0:P:CHUNKS, :].bitcast(F32)).then_inc(thr_st, 16)
                sp.wait_ge(thr_st, 16)
                sp.dma_start(thr_b[:], dram["thr"].rearrange("e one -> one e").to_broadcast([NBLK, E]))\
                    .then_inc(thr_ld, 16)

            chunks(sp, chunk, middle)
            for i in range(2):
                store(SH_CHUNKS - 1, 1, i)
            for u in range(2):
                sp.wait_ge(os_out[u], 64 * SH_CHUNKS // 2)

        @block.gpsimd
        def _(pool):
            made = [0]

            def made_one(ins):
                made[0] += 1
                ins.then_inc(cst, 1)
                pool.wait_ge(cst, made[0])

            made_one(pool.memset(same_expert[:], 1.0))
            v = same_expert[:].rearrange("p (e c) -> p e c", e=E)
            made_one(pool.affine_select(out=v, in_=v, compare_op=ALU.is_ge, fill=0.0, base=0,
                                        pattern=[[-CHUNKS, E], [0, CHUNKS]], channel_multiplier=1))
            made_one(pool.affine_select(out=v, in_=v, compare_op=ALU.is_ge, fill=0.0, base=CHUNKS - 1,
                                        pattern=[[CHUNKS, E], [0, CHUNKS]], channel_multiplier=-1))
            made_one(pool.memset(ones[:], 1.0))
            made_one(pool.memset(earlier[:], 1.0))
            made_one(pool.affine_select(out=earlier[:], in_=earlier[:], compare_op=ALU.is_gt, fill=0.0, base=0,
                                        pattern=[[1, NBLK]], channel_multiplier=-1))
            made_one(pool.memset(keep_run[:], 1.0))
            k = keep_run[:].rearrange("p (e b) -> p e b", e=E)
            made_one(pool.affine_select(out=k, in_=k, compare_op=ALU.not_equal, fill=0.0, base=0,
                                        pattern=[[0, E], [1, P]], channel_multiplier=0))
            made_one(pool.iota(rank[:, :, P:P + 1], pattern=[[0, E], [0, 1]], base=0, channel_multiplier=1,
                               allow_small_or_imprecise_dtypes=True))
            made_one(pool.iota(slot_no[:], pattern=[[1, CAP]], base=0, channel_multiplier=0,
                               allow_small_or_imprecise_dtypes=True))
            made_one(pool.iota(jcol[:], pattern=[[P, GT]], base=0, channel_multiplier=1,
                               allow_small_or_imprecise_dtypes=True))
            made_one(pool.memset(idx_all[:], 0))
            assert made[0] == CST

        @block.scalar
        def _(act):
            def chunk(c, u, second):
                for f in range(FS):
                    wait(act, g_ps, FS * c + f + 1)
                    wait(act, hid_ready, FS * c + f - 1)
                    act.activation(sg[(u + f) % 2][:], ps_g[(u + f) % 2][:, 0:CH], ACT.Silu).then_inc(sg_ready, 1)

            chunks(act, chunk, lambda: None)

        @block.vector
        def _(dve):
            vec = nc.vector
            vec.memset(thr[:], 0).then_inc(thr_init, 1)
            vec.memset(bitf[:], float(1 << 30)).then_inc(thr_init, 1)
            dve.wait_ge(thr_init, 2)
            vec.tensor_copy(biti[:], bitf[:]).then_inc(bit_s, 1)
            dve.wait_ge(bit_s, 1)
            dve.wait_ge(s_ld, 16 * E)
            dve.wait_ge(cst, CST)

            def count(k):
                wait(dve, thr_s, k)
                wait(dve, bit_s, k + 1)
                vec.tensor_tensor(cand[:], thr[:], biti[:], ALU.bitwise_or).then_inc(cand_s, 1)
                wait(dve, cand_s, k + 1)
                vec.tensor_scalar(hits[:], s1[:], cand[:].bitcast(F32), None, ALU.is_ge, ALU.add,
                                  accum_out=cnt[:]).then_inc(cnt_s, 1)

            def settle(k):
                wait(dve, cnt_ps, k + 1)
                vec.tensor_scalar(inc[:], ps_i[0][:, 0:1], CAP - 0.5, bitf[:], ALU.is_ge, ALU.mult)\
                    .then_inc(inc_s, 1)
                wait(dve, inc_s, k + 1)
                vec.tensor_tensor(thr[:], thr[:], inc[:], ALU.bitwise_or).then_inc(thr_s, 1)
                vec.tensor_scalar(bitf[:], bitf[:], 0.5, None, ALU.mult).then_inc(bitf_s, 1)

            def halve(k):
                wait(dve, bitf_s, k + 1)
                vec.tensor_copy(biti[:], bitf[:]).then_inc(bit_s, 1)

            def product(c, u, f):
                wait(dve, sg_ready, FS * c + f + 1)
                if f == 0:
                    wait(dve, dn_ps, 2 * (c - 1))
                vec.tensor_tensor(hid[u][:, f, :], sg[(u + f) % 2][:], ps_u[(u + f) % 2][:, 0:CH], ALU.mult)\
                    .then_inc(hid_ready, 1)

            def outputs(c, u, i):
                wait(dve, dn_ps, 2 * c + i + 1)
                if i == 0:
                    wait(dve, hs_ld[u], (c - u) * 32 + 64)
                    if not isinstance(c, int) or c >= 2:
                        wait(dve, os_out[u], (c - u) * 32)
                vec.tensor_tensor(os_[u][:, 2 * i, :], ps_d[i][:, 0:D], hs[u][:, 2 * i, :], ALU.add)
                vec.tensor_tensor(os_[u][0:T1, 2 * i + 1, :], ps_d[i][0:T1, D:2 * D], hs[u][0:T1, 2 * i + 1, :],
                                  ALU.add).then_inc(os_ready, 1)

            def make_list(j):
                wait(dve, ix_ps, NG * j)
                wait(dve, list_s, j)
                vec.tensor_scalar(ge[:], slot_no[:], lo[:, bass.ds(j, 1)], None, ALU.is_ge).then_inc(oh_ge, 1)
                wait(dve, oh_ge, j + 1)
                vec.scalar_tensor_tensor(onehot[:], slot_no[:], hi[:, bass.ds(j, 1)], ge[:], ALU.is_lt, ALU.mult)\
                    .then_inc(oh_s, 1)

            def take(j, u, g):
                t0, t1 = IDX_GROUPS[g]
                wait(dve, ix_ps, NG * j + g + 1)
                bank = ps_i[(u + g) % 2]
                for t in range(t0, t1):
                    n, c0 = rows_of(t), (t - t0) * (P + 1)
                    vec.tensor_scalar(junk[0:n, t, :], bank[0:n, c0:c0 + P], jcol[0:n, t:t + 1], None, ALU.is_le,
                                      ALU.add, accum_out=bcol[0:n, t:t + 1])
                n = rows_of(t1 - 1)
                vec.tensor_copy(acol[0:n, t0:t1],
                                bank[0:n, 0:(t1 - t0) * (P + 1)].rearrange("p (t b) -> p t b", b=P + 1)[:, :, P])\
                    .then_inc(ix_used, 1)

            def write_list(j):
                wait(dve, ix_used, NG * (j + 1) + 1)
                vec.scalar_tensor_tensor(idx_all[:, bass.ds(j * GT, GT)], acol[:], float(P), bcol[:], ALU.mult,
                                         ALU.add).then_inc(list_s, 1)

            def chunk(c, u, second):
                has_out = not (isinstance(c, int) and c == 0)
                product(c, u, 0)
                if second:
                    j = c - E
                    make_list(j)
                    take(j, u, 0)
                    product(c, u, 1)
                    take(j, u, 1)
                    product(c, u, 2)
                    take(j, u, 2)
                    outputs(c - 1, 1 - u, 0)
                    take(j, u, 3)
                    outputs(c - 1, 1 - u, 1)
                    take(j, u, 4)
                    write_list(j)
                else:
                    count(2 * c)
                    product(c, u, 1)
                    settle(2 * c)
                    halve(2 * c)
                    count(2 * c + 1)
                    product(c, u, 2)
                    if has_out:
                        outputs(c - 1, 1 - u, 0)
                    settle(2 * c + 1)
                    halve(2 * c + 1)
                    if has_out:
                        outputs(c - 1, 1 - u, 1)

            def middle():
                n = [0]

                def step(ins):
                    n[0] += 1
                    ins.then_inc(rk, 1)
                    dve.wait_ge(rk, n[0])

                s2v = s2[:].rearrange("p e b -> p (e b)")
                dve.wait_ge(wld, 64)
                dve.wait_ge(thr_ld, 16)
                per_block = thr_b[:, :, None].to_broadcast([NBLK, E, P])
                m3 = mask[:].rearrange("p (e b) -> p e b", e=E)
                for run, op, o in ((g_run, ALU.is_gt, 0), (e_run, ALU.is_equal, E)):
                    step(vec.tensor_tensor(m3, s2[:], per_block, op))
                    step(vec.tensor_tensor_scan(run[:], keep_run[:], mask[:], 0.0, ALU.mult, ALU.add))
                    step(vec.tensor_copy(tots[:, o:o + E], run[:].rearrange("p (e b) -> p e b", e=E)[:, :, P - 1]))
                dve.wait_ge(rk_ps, 1)
                step(vec.tensor_copy(before[:], ps_i[1][0:NBLK, 0:2 * E]))
                step(vec.tensor_scalar(need[:], ps_i[1][0:NBLK, 2 * E:3 * E], -1.0, float(CAP), ALU.mult, ALU.add))
                step(vec.tensor_tensor(lo[:], before[:, E:2 * E], need[:], ALU.min))
                step(vec.tensor_tensor(lo[:], lo[:], before[:, 0:E], ALU.add))
                g3 = g_run[:].rearrange("p (e b) -> p e b", e=E)
                e3 = e_run[:].rearrange("p (e b) -> p e b", e=E)
                step(vec.tensor_tensor(g3, g3, before[:, 0:E, None].to_broadcast([NBLK, E, P]), ALU.add))
                step(vec.tensor_tensor(e3, e3, before[:, E:2 * E, None].to_broadcast([NBLK, E, P]), ALU.add))
                step(vec.tensor_tensor(e3, e3, need[:, :, None].to_broadcast([NBLK, E, P]), ALU.min))
                step(vec.tensor_tensor(rank[:, :, 0:P], g3, e3, ALU.add))
                step(vec.tensor_copy(hi[:], rank[:, :, P - 1]))
                step(vec.memset(bcol[:], 0.0))
                vec.memset(acol[:], 0.0).then_inc(ix_used, 1)
                dve.wait_ge(ix_used, 1)

            chunks(dve, chunk, middle)
            for i in range(2):
                outputs(SH_CHUNKS - 1, 1, i)

        @block.tensor
        def _(pe):
            mm = nc.tensor.matmul
            pe.wait_ge(wld, 64)
            pe.wait_ge(cst, CST)

            def hidden(c, u, f):
                if f == 0:
                    wait(pe, xs_ld[u], (c - u) * 8 + 16)
                wait(pe, hid_ready, FS * c + f - 1)
                for w, bank in ((wsg, ps_g), (wsu, ps_u)):
                    for k in range(2):
                        last = mm(bank[(u + f) % 2][:, 0:CH], w[:, k, f * P:(f + 1) * P], xs[u][:, k, :],
                                  start=k == 0, stop=k == 1)
                last.then_inc(g_ps, 1)

            def down(c, u, i):
                wait(pe, hid_ready, FS * c + FS)
                wait(pe, os_ready, 2 * c + i - 1)
                for t, (t0, n) in enumerate(TILES):
                    for k in range(FS):
                        last = mm(ps_d[i][0:n, t * D:(t + 1) * D], hid[u][:, k, i * TOK + t0:i * TOK + t0 + n],
                                  wsd[:, k, :], start=k == 0, stop=k == FS - 1)
                last.then_inc(dn_ps, 1)

            def count(k):
                wait(pe, cnt_s, k + 1)
                mm(ps_i[0][:, 0:1], same_expert[:], cnt[:], start=True, stop=True).then_inc(cnt_ps, 1)

            def lists(j, u, g):
                t0, t1 = IDX_GROUPS[g]
                if g == 0:
                    wait(pe, oh_s, j + 1)
                (wait if g < NG - 1 else wait_apart)(pe, ix_used, NG * j + g)
                for t in range(t0, t1):
                    n, c0 = rows_of(t), (t - t0) * (P + 1)
                    last = mm(ps_i[(u + g) % 2][0:n, c0:c0 + P + 1], onehot[:, t * P:t * P + n],
                              rank[:, bass.ds(j, 1), :].rearrange("p e b -> p (e b)"), start=True, stop=True)
                last.then_inc(ix_ps, 1)

            def chunk(c, u, second):
                has_out = not (isinstance(c, int) and c == 0)
                hidden(c, u, 0)
                hidden(c, u, 1)
                if second:
                    j = c - E
                    lists(j, u, 0)
                    lists(j, u, 1)
                    hidden(c, u, 2)
                    lists(j, u, 2)
                    down(c - 1, 1 - u, 0)
                    lists(j, u, 3)
                    down(c - 1, 1 - u, 1)
                    lists(j, u, 4)
                else:
                    count(2 * c)
                    hidden(c, u, 2)
                    if has_out:
                        down(c - 1, 1 - u, 0)
                    count(2 * c + 1)
                    if has_out:
                        down(c - 1, 1 - u, 1)

            def middle():
                pe.wait_ge(rk, 6)
                mm(ps_i[1][0:NBLK, 0:2 * E], earlier[:], tots[:], start=True, stop=True)
                mm(ps_i[1][0:NBLK, 2 * E:4 * E], ones[:], tots[:], start=True, stop=True).then_inc(rk_ps, 1)
                pe.wait_ge(rk, 16)

            chunks(pe, chunk, middle)
            for i in range(2):
                down(SH_CHUNKS - 1, 1, i)


def stage_e(nc, dram, idx_all):
    ctx = ExitStack()
    with ctx:
        def sb(name, shape, dt=F32):
            return ctx.enter_context(nc.sbuf_tensor(name, shape, dt))

        def sem(name):
            return ctx.enter_context(nc.semaphore(name))

        wg = [sb(f"wg{u}", [KH, 2, F_EXP]) for u in range(2)]
        wu = [sb(f"wu{u}", [KH, 2, F_EXP]) for u in range(2)]
        wd = [sb(f"wd{u}", [P, FT, D]) for u in range(2)]
        xg = [sb(f"xg{u}", [P, GT, ROW]) for u in range(2)]
        xgT = [sb(f"xgT{u}", [KH, 2, CAP]) for u in range(2)]
        score = [sb(f"score{u}", [P, GT]) for u in range(2)]
        idx_g = [sb(f"idx_g{u}", [P, GT], I32) for u in range(2)]
        idx_s = [sb(f"idx_s{u}", [P, GT], I32) for u in range(2)]
        sg = [sb(f"esg{u}", [P, CH]) for u in range(2)]
        hid = sb("ehid", [P, FT, CAP])
        y = sb("y", [P, GT, D])
        ident = sb("eident", [P, P])

        ps_g = [ctx.enter_context(nc.psum_tensor(f"eps_g{i}", [P, 512], F32)) for i in range(2)]
        ps_u = [ctx.enter_context(nc.psum_tensor(f"eps_u{i}", [P, 512], F32)) for i in range(2)]
        ps_d = [ctx.enter_context(nc.psum_tensor(f"eps_d{i}", [P, 512], F32)) for i in range(2)]
        ps_t = [ctx.enter_context(nc.psum_tensor(f"eps_t{i}", [P, 512], F32)) for i in range(2)]

        cst = sem("e_cst")
        gu_ld = [sem(f"gu_ld{u}") for u in range(2)]
        d_ld = [sem(f"d_ld{u}") for u in range(2)]
        gathered = [sem(f"gathered{u}") for u in range(2)]
        scattered = [sem(f"scattered{u}") for u in range(2)]
        idxg_ready = sem("idxg_ready")
        idxs_ready = sem("idxs_ready")
        score_ready = sem("score_ready")
        tr_ps = sem("tr_ps")
        xgT_ready = sem("xgT_ready")
        gu_ps = sem("gu_ps")
        sg_ready = sem("esg_ready")
        hid_ready = sem("ehid_ready")
        dn_ps = sem("edn_ps")
        y_ready = sem("y_ready")
        passed = sem("passed_e")
        CHN = CAP // CH
        UNITS = CHN * FT

        def wait_apart(eng, s, value):
            wait(eng, s, value)
            if not isinstance(value, int):
                eng.sem_inc(passed, 1)

        def order():
            downs = [[(1, t) for t in range(9, GT)]] + [[(0, t) for t in range(3 * c, 3 * c + 3)] for c in range(3)]
            nxt = 0
            for c in range(CHN):
                for f in range(FT):
                    yield "gu", c, f
                    if 1 <= f <= len(downs[c]):
                        yield ("dn", *downs[c][f - 1])
                    if c >= 1 and f < 5 and nxt < GT:
                        yield "tr", 0, nxt
                        nxt += 1
            assert nxt == GT

        def experts(eng, expert):
            for e in range(2):
                expert(e, e % 2, True)
            with eng.Fori(0, (E - 4) // 2) as it:
                for u in range(2):
                    expert(it * 2 + (2 + u), u, True)
            for e in range(E - 2, E):
                expert(e, e % 2, e + 1 < E)

        block = ctx.enter_context(nc.Block())

        @block.sync
        def _(sp):
            def load_gu(e, u):
                sp.dma_start(wg[u][:], dram["WgT"][bass.ds(e, 1)].rearrange("e p k f -> (e p) k f"))\
                    .then_inc(gu_ld[u], 16)
                sp.dma_start(wu[u][:], dram["WuT"][bass.ds(e, 1)].rearrange("e p k f -> (e p) k f"))\
                    .then_inc(gu_ld[u], 16)

            def load_d(e, u):
                sp.dma_start(wd[u][:], dram["WdT"][bass.ds(e, 1)].rearrange("e p k f -> (e p) k f"))\
                    .then_inc(d_ld[u], 16)

            load_gu(0, 0)
            load_d(0, 0)

            def expert(e, u, more):
                if more:
                    wait_apart(sp, gu_ps, UNITS * e)
                    load_gu(e + 1, 1 - u)
                    wait_apart(sp, dn_ps, GT * e)
                    load_d(e + 1, 1 - u)

            experts(sp, expert)

        @block.gpsimd
        def _(pool):
            made = [0]

            def made_one(ins):
                made[0] += 1
                ins.then_inc(cst, 1)
                pool.wait_ge(cst, made[0])

            made_one(pool.memset(ident[:], 0.0))
            made_one(pool.affine_select(out=ident[:], in_=ident[:], compare_op=ALU.not_equal, fill=1.0, base=0,
                                        pattern=[[-1, P]], channel_multiplier=1))
            made_one(pool.memset(xg[0][:, GT - 1, :], 0.0))
            made_one(pool.memset(xg[1][:, GT - 1, :], 0.0))

            def gather(u):
                for t in range(GT):
                    n = rows_of(t)
                    pool.indirect_dma_start(
                        out=xg[u][0:n, t, :], out_offset=None, in_=dram["tab"],
                        in_offset=bass.IndirectOffsetOnAxis(ap=idx_g[u][0:n, t:t + 1], axis=0))\
                        .then_inc(gathered[u], 16)

            pool.wait_ge(idxg_ready, 1)
            gather(0)

            def expert(e, u, more):
                if more:
                    wait(pool, idxg_ready, e + 2)
                    wait(pool, tr_ps, GT * e)
                    wait_apart(pool, score_ready, e)
                    gather(1 - u)
                for t in range(GT):
                    if t == 0:
                        wait(pool, idxs_ready, e + 1)
                        if not isinstance(e, int) or e >= 1:
                            wait(pool, scattered[1 - u], (e - (1 - u) + 1) * (16 * GT // 2))
                    wait_apart(pool, y_ready, GT * e + t + 1)
                    n = rows_of(t)
                    pool.indirect_dma_start(
                        out=dram["out"], out_offset=bass.IndirectOffsetOnAxis(ap=idx_s[u][0:n, t:t + 1], axis=0),
                        in_=y[0:n, t, :], in_offset=None, compute_op=ALU.add).then_inc(scattered[u], 16)

            experts(pool, expert)
            for u in range(2):
                pool.wait_ge(scattered[u], 16 * GT * E // 2)

        @block.scalar
        def _(act):
            def evacuate(e, u, t):
                wait(act, tr_ps, GT * e + t + 1)
                n = rows_of(t)
                act.activation(xgT[u][:, :, t * P:t * P + n],
                               ps_t[(u + t) % 2][0:KH, 0:2 * P].rearrange("p (k t) -> p k t", k=2)[:, :, 0:n], ACT.Copy)\
                    .then_inc(xgT_ready, 1)

            for t in range(GT):
                evacuate(0, 0, t)

            def expert(e, u, more):
                for kind, c, t in order():
                    if kind == "gu":
                        n = UNITS * e + FT * c + t
                        wait(act, gu_ps, n + 1)
                        wait(act, hid_ready, n - 1)
                        act.activation(sg[t % 2][:], ps_g[t % 2][:, 0:CH], ACT.Silu).then_inc(sg_ready, 1)
                    elif kind == "tr" and more:
                        evacuate(e + 1, 1 - u, t)

            experts(act, expert)

        @block.vector
        def _(dve):
            vec = nc.vector

            def copy_g(e, u):
                if not isinstance(e, int) or e >= 2:
                    wait_apart(dve, gathered[u], (e - u) * (16 * GT // 2))
                vec.tensor_copy(idx_g[u][:], idx_all[:, bass.ds(e * GT, GT)]).then_inc(idxg_ready, 1)

            def copy_score(e, u):
                wait_apart(dve, gathered[u], (e - u) * (16 * GT // 2) + 16 * GT)
                vec.tensor_copy(score[u][:, :], xg[u][:, :, bass.ds(e + D, 1)].rearrange("p t one -> p (t one)"))\
                    .then_inc(score_ready, 1)

            def scaled(e, u, t):
                n = rows_of(t)
                if t == 0:
                    wait(dve, score_ready, e + 1)
                    if not isinstance(e, int) or e >= 1:
                        wait(dve, scattered[1 - u], (e - (1 - u) + 1) * (16 * GT // 2))
                wait(dve, dn_ps, GT * e + t + 1)
                vec.tensor_scalar(y[0:n, t, :], ps_d[(u + t) % 2][0:n, 0:D], score[u][0:n, t:t + 1], None, ALU.mult)\
                    .then_inc(y_ready, 1)

            copy_g(0, 0)
            dve.wait_ge(cst, 4)
            copy_score(0, 0)

            def expert(e, u, more):
                if more:
                    copy_g(e + 1, 1 - u)
                if not isinstance(e, int) or e >= 2:
                    wait_apart(dve, scattered[u], (e - u) * (16 * GT // 2))
                vec.tensor_copy(idx_s[u][:], idx_all[:, bass.ds(e * GT, GT)]).then_inc(idxs_ready, 1)
                for kind, c, t in order():
                    if kind == "gu":
                        n = UNITS * e + FT * c + t
                        wait(dve, sg_ready, n + 1)
                        vec.tensor_tensor(hid[:, t, c * CH:(c + 1) * CH], sg[t % 2][:], ps_u[t % 2][:, 0:CH],
                                          ALU.mult).then_inc(hid_ready, 1)
                    elif kind == "dn" and c == 0:
                        scaled(e, u, t)
                    elif kind == "dn" and not (isinstance(e, int) and e == 0):
                        scaled(e - 1, 1 - u, t)
                    elif kind == "tr" and t == 0 and more:
                        copy_score(e + 1, 1 - u)

            experts(dve, expert)
            for t in range(9, GT):
                scaled(E - 1, (E - 1) % 2, t)

        @block.tensor
        def _(pe):
            mm = nc.tensor.matmul
            pe.wait_ge(cst, 4)

            def transposes(e, u, t):
                if t == 0:
                    wait(pe, gathered[u], (e - u) * (16 * GT // 2) + 16 * GT)
                (wait if t < GT - 1 else wait_apart)(pe, xgT_ready, GT * e + t - 1)
                n = rows_of(t)
                for k in range(2):
                    last = nc.tensor.transpose(ps_t[(u + t) % 2][0:KH, k * P:k * P + n], xg[u][0:n, t, k * KH:(k + 1) * KH],
                                               ident[0:n, 0:n])
                last.then_inc(tr_ps, 1)

            def down(e, u, t):
                chunk = (min((t + 1) * P, CAP) - 1) // CH
                wait(pe, hid_ready, UNITS * e + FT * (chunk + 1))
                if t == 0:
                    wait(pe, d_ld[u], (e - u) * 8 + 16)
                wait(pe, y_ready, GT * e + t - 1)
                n = rows_of(t)
                for k in range(FT):
                    last = mm(ps_d[(u + t) % 2][0:n, 0:D], hid[:, k, t * P:t * P + n], wd[u][:, k, :],
                              start=k == 0, stop=k == FT - 1)
                last.then_inc(dn_ps, 1)

            for t in range(GT):
                transposes(0, 0, t)

            def expert(e, u, more):
                for kind, c, t in order():
                    if kind == "gu":
                        n = UNITS * e + FT * c + t
                        if c == 0 and t == 0:
                            wait(pe, gu_ld[u], (e - u) * 16 + 32)
                            wait(pe, xgT_ready, GT * (e + 1))
                        wait(pe, hid_ready, n - 1)
                        for w, bank in ((wg[u], ps_g), (wu[u], ps_u)):
                            for k in range(2):
                                last = mm(bank[t % 2][:, 0:CH], w[:, k, t * P:(t + 1) * P],
                                          xgT[u][:, k, c * CH:(c + 1) * CH], start=k == 0, stop=k == 1)
                        last.then_inc(gu_ps, 1)
                    elif kind == "dn" and c == 0:
                        down(e, u, t)
                    elif kind == "dn" and not (isinstance(e, int) and e == 0):
                        down(e - 1, 1 - u, t)
                    elif kind == "tr" and more:
                        transposes(e + 1, 1 - u, t)

            experts(pe, expert)
            for t in range(9, GT):
                down(E - 1, (E - 1) % 2, t)


SCRATCH = {"h2": (N, D), "tab": (N, ROW), "x2T": (KH, 2, N), "sT": (E, NPAD), "thr": (E, 1)}


def program(nc, dram):
    stage_a(nc, dram)
    with nc.sbuf_tensor("idx_all", [P, E * GT], I32) as idx_all:
        stage_s(nc, dram, idx_all)
        stage_e(nc, dram, idx_all)


def layouts(i):
    import numpy as np
    x = np.asarray(i["x"]).reshape(IMAGES, GRID, PATCH, GRID, PATCH, 3).transpose(0, 2, 4, 5, 1, 3)
    patches = np.zeros((IMAGES, KC * P, TOK), x.dtype)
    patches[:, :, 1:] = x.reshape(IMAGES, DPATCH, GRID * GRID)
    a = {k: np.asarray(v) for k, v in i.items()}
    return {
        "patches": patches.reshape(IMAGES, KC, P, TOK).transpose(0, 2, 1, 3),
        "tok_W": a["L0_tok_W"], "tok_b": a["L0_tok_b"], "cls": a["L0_tok_class_token"],
        "pos": a["L0_tok_pos_emb"], "Wqkv": a["L0_attn_Wqkv"], "bqkv": a["L0_attn_bqkv"],
        "Wout": a["L0_attn_Wout"], "bout": a["L0_attn_bout"], "gateT": a["L0_ffn_gate_weight"].T,
        "WgT": a["L0_ffn_Wg"].reshape(E, F_EXP, 2, KH).transpose(0, 3, 2, 1),
        "WuT": a["L0_ffn_Wu"].reshape(E, F_EXP, 2, KH).transpose(0, 3, 2, 1),
        "WdT": a["L0_ffn_Wd"].reshape(E, D, FT, P).transpose(0, 3, 2, 1),
        "WsgT": a["L0_ffn_Ws_g"].reshape(F_SH, 2, KH).transpose(2, 1, 0),
        "WsuT": a["L0_ffn_Ws_u"].reshape(F_SH, 2, KH).transpose(2, 1, 0),
        "WsdT": a["L0_ffn_Ws_d"].reshape(D, FS, P).transpose(2, 1, 0),
    }


def kernel(**inputs):
    import numpy as np
    import concourse.bacc as bacc
    from concourse.bass_utils import run_bass_kernel_spmd

    nc = bacc.Bacc("TRN2", target_bir_lowering=False, num_devices=1)
    arrays, dram = {}, {}
    for name, a in layouts(inputs).items():
        arrays[f"in_{name}"] = np.ascontiguousarray(a)
        dram[name] = nc.dram_tensor(f"in_{name}", a.shape, mybir.dt.from_np(a.dtype), kind="ExternalInput").ap()
    for name, shape in SCRATCH.items():
        dram[name] = nc.dram_tensor(f"scratch_{name}", shape, F32, kind="Internal").ap()
    dram["out"] = nc.dram_tensor("out", (N, D), F32, kind="ExternalOutput").ap()
    program(nc, dram)
    got = run_bass_kernel_spmd(nc, [arrays], core_ids=[0]).results[0]["out"]
    return got.reshape(IMAGES, TOK, D)
```

```python
from contextlib import ExitStack

import concourse.bass as bass
from concourse import mybir

ALU = mybir.AluOpType
ACT = mybir.ActivationFunctionType
AX = mybir.AxisListType
F32 = mybir.dt.float32
F32R = mybir.dt.float32r
BF16 = mybir.dt.bfloat16
F16 = mybir.dt.float16
I32 = mybir.dt.int32

P = 128
IMAGES = 64
PATCH = 16
GRID = 14
TOK = GRID * GRID + 1
T1 = TOK - P
TILES = ((0, P), (P, T1))
D = 192
KH = D // 2
DPATCH = PATCH * PATCH * 3
KC = DPATCH // P
HEADS = 12
HH = HEADS // 2
DH = D // HEADS
VW = KH + HH
EPS = 1e-5
N = IMAGES * TOK
E = 16
CAP = (N * 2 + E - 1) // E
NBLK = (N + P - 1) // P
NPAD = NBLK * P
CHUNKS = 8
F_EXP = 4 * D
FT = F_EXP // P
F_SH = F_EXP // 2
FS = F_SH // P
SC0 = D + 64
ROW = SC0 + E
BIG = -1.0e30
ST_N = 2 * TOK
assert CAP * CHUNKS == N and CAP == 4 * ST_N


def wait(eng, sem, value):
    if isinstance(value, int) and value <= 0:
        return
    eng.wait_ge(sem, value)


def stage_a(nc, dram):
    ctx = ExitStack()
    with ctx:
        def sb(name, shape, dt=F32):
            return ctx.enter_context(nc.sbuf_tensor(name, shape, dt))

        def sem(name):
            return ctx.enter_context(nc.semaphore(name))

        w_tok = sb("w_tok", [P, KC, D])
        w_qkv = sb("w_qkv", [KH, 2, 3 * D])
        w_out = sb("w_out", [KH, 2, D])
        w_gate = sb("w_gate", [KH, 2, E])
        bq = sb("bq", [KH, 2])
        bq_scaled = sb("bq_scaled", [KH, 2])
        bk = sb("bk", [KH, 2])
        bv = sb("bv", [P, D])
        bout = sb("bout", [P, D])
        pos = sb("pos", [P, 2, D])
        tokb = sb("tokb", [P, 2, D])
        ident = sb("ident", [P, P])
        ident_bf = sb("ident_bf", [P, P], BF16)
        mask0 = sb("mask0", [P, 4, P], BF16)
        mask1 = sb("mask1", [P, 2, TOK], BF16)
        sel_sum = sb("sel_sum", [VW, KH])
        minus_half = sb("minus_half", [P, 2])
        pad_scores = sb("pad_scores", [E, NPAD - N])

        patches = [sb(f"patches{u}", [P, KC, TOK]) for u in range(2)]
        h = [sb(f"h{u}", [P, 2, D]) for u in range(2)]
        h_res = [sb(f"h_res{u}", [P, 2, D]) for u in range(2)]
        stats1 = sb("stats1", [P, 2, 6])
        mv1 = sb("mv1", [P, 2, 2])
        var1 = sb("var1", [P, 2])
        rstd1 = sb("rstd1", [P, 2])
        xn = sb("xn", [P, 2, D])
        xnT = [sb(f"xnT{u}", [KH, 2, TOK]) for u in range(2)]
        qT = [sb(f"qT{u}", [KH, 2, TOK]) for u in range(2)]
        kT = [sb(f"kT{u}", [KH + 1, 2, TOK]) for u in range(2)]
        qz = [sb(f"qz{u}", [KH + 1, 2, HH, TOK]) for u in range(2)]
        vz = [sb(f"vz{u}", [P, 2, HEADS, VW]) for u in range(2)]
        mx = sb("mx", [P, 2, HEADS])
        mT = [sb(f"mT{u}", [HEADS, TOK]) for u in range(2)]
        pt0 = [sb(f"pt0_{u}", [P, HEADS, TOK]) for u in range(2)]
        pt1 = [sb(f"pt1_{u}", [P, HEADS, T1]) for u in range(2)]
        o_raw = [sb(f"o_raw{u}", [VW, 2, TOK]) for u in range(2)]
        rec = sb("rec", [VW, 2, TOK])
        oT = [sb(f"oT{u}", [KH, 2, TOK]) for u in range(2)]
        h2 = [sb(f"h2_{u}", [P, 2, D]) for u in range(2)]
        stats2 = sb("stats2", [P, 2, 6])
        mv2 = sb("mv2", [P, 2, 2])
        var2 = sb("var2", [P, 2])
        rstd2 = sb("rstd2", [P, 2])
        tab = [sb(f"tab{u}", [P, 2, ROW]) for u in range(2)]
        x2T = [sb(f"x2T{u}", [KH, 2, TOK]) for u in range(2)]
        ex = sb("ex", [P, 2, E])
        ex1 = sb("ex1", [P, 2, E])
        sT = [sb(f"sT{u}", [E, TOK]) for u in range(2)]

        ps_max = [ctx.enter_context(nc.psum_tensor(f"ps_max{i}", [P, 512], F32)) for i in range(3)]
        ps_st = [ctx.enter_context(nc.psum_tensor(f"ps_st{i}", [P, 512], F32)) for i in range(2)]
        ps5 = ctx.enter_context(nc.psum_tensor("ps5", [P, 512], F32))
        ps6 = ctx.enter_context(nc.psum_tensor("ps6", [P, 512], F32))
        ps7 = ctx.enter_context(nc.psum_tensor("ps7", [P, 512], F32))

        const_ld = sem("const_ld")
        const_pool = sem("const_pool")
        const_dve = sem("const_dve")
        const_act = sem("const_act")
        pad_out = sem("pad_out")
        cls_ld = sem("cls_ld")
        passed = sem("passed")
        pat_ld = [sem(f"pat_ld{u}") for u in range(2)]
        tok_ps = sem("tok_ps")
        h_ready = sem("h_ready")
        st1 = sem("st1")
        mv1_s = sem("mv1_s")
        var1_s = sem("var1_s")
        rstd1_s = sem("rstd1_s")
        xn_ready = sem("xn_ready")
        xnT_ps = sem("xnT_ps")
        xnT_ready = sem("xnT_ready")
        q_ps = sem("q_ps")
        q_ready = sem("q_ready")
        qz_ld = [sem(f"qz_ld{u}") for u in range(2)]
        k_ps = sem("k_ps")
        k_ready = sem("k_ready")
        v_ps = sem("v_ps")
        v_ready = sem("v_ready")
        hres_ready = sem("hres_ready")
        mx_ps = sem("mx_ps")
        mx_red = sem("mx_red")
        mT_ps = sem("mT_ps")
        mT_ready = sem("mT_ready")
        mrow_ld = [sem(f"mrow_ld{u}") for u in range(2)]
        st_ps = sem("st_ps")
        exp_done = sem("exp_done")
        sel_done = sem("sel_done")
        pv_ps = sem("pv_ps")
        pv_used = sem("pv_used")
        rec_ready = sem("rec_ready")
        bc_ps = sem("bc_ps")
        oT_ready = sem("oT_ready")
        wo_ps = sem("wo_ps")
        h2_ready = sem("h2_ready")
        st2 = sem("st2")
        mv2_s = sem("mv2_s")
        var2_s = sem("var2_s")
        rstd2_s = sem("rstd2_s")
        xn2_ready = sem("xn2_ready")
        x2T_ps = sem("x2T_ps")
        x2T_ready = sem("x2T_ready")
        lg_ps = sem("lg_ps")
        lg_used = sem("lg_used")
        ex1_s = sem("ex1_s")
        sc_ready = sem("sc_ready")
        sT_ps = sem("sT_ps")
        sT_ready = sem("sT_ready")
        h2_out = [sem(f"h2_out{u}") for u in range(2)]
        x2T_out = [sem(f"x2T_out{u}") for u in range(2)]
        tab_out = [sem(f"tab_out{u}") for u in range(2)]
        sT_out = [sem(f"sT_out{u}") for u in range(2)]

        CONST_LOADS = 12
        CONST_POOL = 22

        def slots(eng, slot):
            def parts(s):
                return dict(a=s + 1 < IMAGES, b=0 <= s < IMAGES, c=s >= 1)
            for s in range(-1, 3):
                slot(s, s % 2, **parts(s))
            with eng.Fori(0, (IMAGES - 6) // 2) as it:
                for u in range(2):
                    slot(it * 2 + (3 + u), (3 + u) % 2, a=True, b=True, c=True)
            for s in range(IMAGES - 3, IMAGES + 1):
                slot(s, s % 2, **parts(s))

        def wait_apart(eng, s, value):
            wait(eng, s, value)
            if not isinstance(value, int):
                eng.sem_inc(passed, 1)

        block = ctx.enter_context(nc.Block())

        @block.sync
        def _(sp):
            for dst, src in ((w_tok[:], dram["tok_W"].rearrange("(c p) n -> p c n", p=P)),
                             (w_qkv[:], dram["Wqkv"].rearrange("(c p) n -> p c n", p=KH)),
                             (w_out[:], dram["Wout"].rearrange("(c p) n -> p c n", p=KH)),
                             (w_gate[:], dram["gateT"].rearrange("(c p) n -> p c n", p=KH)),
                             (bv[:], dram["bqkv"][None, 2 * D:3 * D].to_broadcast([P, D])),
                             (bout[:], dram["bout"][None, :].to_broadcast([P, D])),
                             (pos[:, 0, :], dram["pos"][0:P, :]),
                             (pos[0:T1, 1, :], dram["pos"][P:TOK, :]),
                             (tokb[:, 0, :], dram["tok_b"][None, :].to_broadcast([P, D])),
                             (tokb[:, 1, :], dram["tok_b"][None, :].to_broadcast([P, D]))):
                sp.dma_start(dst, src).then_inc(const_ld, 16)
            with nc.allow_non_contiguous_dma(reason="two short bias columns"):
                sp.dma_start(bq[:], dram["bqkv"][0:D].rearrange("(c p) -> p c", p=KH)).then_inc(const_ld, 16)
                sp.dma_start(bk[:], dram["bqkv"][D:2 * D].rearrange("(c p) -> p c", p=KH)).then_inc(const_ld, 16)
            sp.wait_ge(const_ld, 16 * CONST_LOADS)
            sp.dma_start(tokb[0:1, 0, :], dram["cls"][None, :]).then_inc(cls_ld, 16)
            sp.wait_ge(const_pool, CONST_POOL)
            sp.dma_start(dram["sT"][:, N:NPAD], pad_scores[:]).then_inc(pad_out, 16)
            sp.wait_ge(pad_out, 16)
            for u in range(2):
                sp.dma_start(patches[u][:], dram["patches"][u]).then_inc(pat_ld[u], 16)

            def slot(s, u, a, b, c):
                v = 1 - u
                if b and not (isinstance(s, int) and s + 2 >= IMAGES):
                    wait_apart(sp, tok_ps, s + 1)
                    sp.dma_start(patches[u][:], dram["patches"][s + 2]).then_inc(pat_ld[u], 16)
                if a:
                    wait_apart(sp, q_ready, s + 2)
                    wait_apart(sp, st_ps, 8 * s)
                    for j in range(HH):
                        r = slice(DH * j, DH * (j + 1))
                        sp.dma_start(qz[v][r, :, j, :], qT[v][r, :, :]).then_inc(qz_ld[v], 16)
                if b:
                    wait(sp, mT_ready, s + 1)
                    sp.dma_start(qz[u][KH:KH + 1, :, :, :].rearrange("p a j t -> p (a j) t"),
                                 mT[u][:, :]).then_inc(mrow_ld[u], 16)
                if c:
                    wait_apart(sp, h2_ready, s)
                    base = (s - 1) * TOK
                    sp.dma_start(dram["h2"][bass.ds(base, P), :], h2[v][:, 0, :]).then_inc(h2_out[v], 16)
                    sp.dma_start(dram["h2"][bass.ds(base + P, T1), :], h2[v][0:T1, 1, :]).then_inc(h2_out[v], 16)
                    wait_apart(sp, x2T_ready, s)
                    sp.dma_start(dram["x2T"].rearrange("(k p) n -> p k n", p=KH)[:, :, bass.ds(base, TOK)], x2T[v][:]).then_inc(x2T_out[v], 16)
                    wait_apart(sp, sc_ready, s)
                    sp.dma_start(dram["tab"][bass.ds(base, P), :], tab[v][:, 0, :]).then_inc(tab_out[v], 16)
                    sp.dma_start(dram["tab"][bass.ds(base + P, T1), :], tab[v][0:T1, 1, :]).then_inc(tab_out[v], 16)
                    wait_apart(sp, sT_ready, s)
                    sp.dma_start(dram["sT"][:, bass.ds(base, TOK)], sT[v][:]).then_inc(sT_out[v], 16)

            slots(sp, slot)
            for u in range(2):
                sp.wait_ge(h2_out[u], 32 * IMAGES // 2)
                sp.wait_ge(x2T_out[u], 16 * IMAGES // 2)
                sp.wait_ge(tab_out[u], 32 * IMAGES // 2)
                sp.wait_ge(sT_out[u], 16 * IMAGES // 2)

        @block.gpsimd
        def _(pool):
            made = [0]

            def made_one(ins):
                made[0] += 1
                ins.then_inc(const_pool, 1)
                pool.wait_ge(const_pool, made[0])

            for t, val in ((ident, 0.0), (sel_sum, 0.0), (mask0, 0.0), (mask1, 0.0), (minus_half, -0.5),
                           (pad_scores, -1.0), (mv1, 0.0), (mv2, 0.0), (rec, 0.0),
                           (qz[0], 0.0), (qz[1], 0.0), (vz[0], 0.0), (vz[1], 0.0)):
                made_one(pool.memset(t[:], val))
            for u in range(2):
                made_one(pool.memset(kT[u][KH:KH + 1, :, :], 1.0))
            made_one(pool.affine_select(out=ident[:], in_=ident[:], compare_op=ALU.not_equal, fill=1.0, base=0,
                                        pattern=[[-1, P]], channel_multiplier=1))
            made_one(pool.affine_select(out=sel_sum[:].rearrange("p (j d) -> p j d", j=HH),
                                        in_=sel_sum[:].rearrange("p (j d) -> p j d", j=HH),
                                        compare_op=ALU.not_equal, fill=1.0, base=-KH,
                                        pattern=[[-1, HH], [0, DH]], channel_multiplier=1))
            made_one(pool.affine_select(out=mask0[:], in_=mask0[:], compare_op=ALU.is_ge, fill=BIG, base=0,
                                        pattern=[[0, 4], [-1, P]], channel_multiplier=1))
            made_one(pool.affine_select(out=mask1[:], in_=mask1[:], compare_op=ALU.is_ge, fill=BIG, base=P,
                                        pattern=[[0, 2], [-1, TOK]], channel_multiplier=1))
            for u in range(2):
                ones = vz[u][:, :, :, KH:VW].rearrange("p t (a j) c -> p (t a) j c", a=2)
                made_one(pool.affine_select(out=ones, in_=ones, compare_op=ALU.not_equal, fill=1.0, base=0,
                                            pattern=[[0, 4], [1, HH], [-1, HH]], channel_multiplier=0))
            made_one(pool.tensor_copy(ident_bf[:], ident[:]))
            assert made[0] == CONST_POOL, made[0]
            pool.wait_ge(const_ld, 16 * CONST_LOADS)

            def slot(s, u, a, b, c):
                v = 1 - u
                if a:
                    wait(pool, var1_s, s + 2)
                    pool.tensor_tensor(rstd1[:], var1[:], minus_half[:], ALU.pow).then_inc(rstd1_s, 1)
                if b:
                    wait(pool, h_ready, s + 1)
                    wait(pool, h2_ready, s - 1)
                    bo = bout[:, None, :].to_broadcast([P, 2, D])
                    pool.tensor_tensor(h_res[u][:, 0, :], h[u][:, 0, :], bout[:], ALU.add)
                    pool.tensor_tensor(h_res[u][0:T1, 1, :], h[u][0:T1, 1, :], bout[0:T1, :], ALU.add)\
                        .then_inc(hres_ready, 1)
                if c:
                    wait(pool, var2_s, s)
                    pool.tensor_tensor(rstd2[:], var2[:], minus_half[:], ALU.pow).then_inc(rstd2_s, 1)
                if b:
                    for unit in range(8):
                        half, part = divmod(unit, 4)
                        wait_apart(pool, exp_done, 8 * s + unit + 1)
                        if part < 3:
                            hd = half * HH + 2 * part
                            x = pt0[u][:, hd:hd + 2, 0:P]
                            n, w = 2, P
                        else:
                            x = pt1[u][0:T1, half * HH:(half + 1) * HH, :]
                            n, w = HH, T1
                        pool.affine_select(out=x, in_=x, compare_op=ALU.is_ge, fill=0.0, base=0,
                                           pattern=[[0, n], [1, w]], channel_multiplier=-1).then_inc(sel_done, 1)

            slots(pool, slot)

        @block.scalar
        def _(act):
            act.wait_ge(const_ld, 16 * CONST_LOADS)
            act.activation(bq_scaled[:], bq[:], ACT.Copy, scale=DH ** -0.5).then_inc(const_act, 1)
            act.wait_ge(const_act, 1)

            def slot(s, u, a, b, c):
                v = 1 - u
                if a:
                    wait(act, xnT_ps, s + 2)
                    wait(act, v_ps, s)
                    act.activation(xnT[v][:], ps7[0:KH, 0:ST_N].rearrange("p (a t) -> p a t", a=2), ACT.Copy)\
                        .then_inc(xnT_ready, 1)
                    wait(act, q_ps, s + 2)
                    if not isinstance(s, int) or s >= 1:
                        wait(act, qz_ld[v], (s + 1 - v) * (16 * HH // 2))
                    for half in range(2):
                        last = act.activation(qT[v][:, half, :], ps6[0:KH, half * TOK:(half + 1) * TOK], ACT.Identity,
                                       scale=DH ** -0.5, bias=bq_scaled[:, half:half + 1])
                    last.then_inc(q_ready, 1)
                    wait(act, k_ps, s + 2)
                    wait(act, st_ps, 8 * s)
                    for half in range(2):
                        last = act.activation(kT[v][0:KH, half, :], ps7[0:KH, half * TOK:(half + 1) * TOK], ACT.Identity,
                                       bias=bk[:, half:half + 1])
                    last.then_inc(k_ready, 1)
                if b:
                    wait(act, mT_ps, s + 1)
                    if not isinstance(s, int) or s >= 2:
                        wait(act, mrow_ld[u], (s - u) * 8)
                    act.activation(mT[u][:], ps6[0:HEADS, 0:TOK], ACT.Copy, scale=-1.0).then_inc(mT_ready, 1)
                if c:
                    wait(act, x2T_ps, s)
                    if not isinstance(s, int) or s >= 3:
                        wait(act, x2T_out[v], (s - 1 - v) * 8)
                    act.activation(x2T[v][:], ps7[0:KH, 0:ST_N].rearrange("p (a t) -> p a t", a=2), ACT.Copy)\
                        .then_inc(x2T_ready, 1)

                def exps(half):
                    if half == 0:
                        wait(act, pv_ps, s - 1)
                    for part in range(4):
                        unit = 4 * half + part
                        wait(act, st_ps, 8 * s + unit + 1)
                        if part < 3:
                            hd = half * HH + 2 * part
                            act.activation(pt0[u][:, hd:hd + 2, :],
                                           ps_st[unit % 2][:, 0:ST_N].rearrange("p (j t) -> p j t", j=2), ACT.Exp)\
                                .then_inc(exp_done, 1)
                        else:
                            act.activation(pt1[u][0:T1, half * HH:(half + 1) * HH, :],
                                           ps_st[unit % 2][0:T1, 0:HH * T1].rearrange("p (j t) -> p j t", j=HH),
                                           ACT.Exp).then_inc(exp_done, 1)
                if b:
                    exps(0)
                if c:
                    wait(act, lg_ps, s)
                    wait(act, ex1_s, s - 1)
                    act.activation(ex[:, 0, :], ps5[:, 0:E], ACT.Exp, scale=-1.0)
                    act.activation(ex[0:T1, 1, :], ps5[0:T1, E:2 * E], ACT.Exp, scale=-1.0).then_inc(lg_used, 1)
                if b:
                    exps(1)
                if c:
                    wait(act, sT_ps, s)
                    if not isinstance(s, int) or s >= 3:
                        wait(act, sT_out[v], (s - 1 - v) * 8)
                    act.activation(sT[v][:], ps6[0:E, 0:TOK], ACT.Copy).then_inc(sT_ready, 1)
                if b:
                    wait(act, pv_ps, s + 1)
                    wait(act, oT_ready, s - 1)
                    act.activation(o_raw[u][:], ps7[0:VW, 0:ST_N].rearrange("p (a t) -> p a t", a=2), ACT.Copy)\
                        .then_inc(pv_used, 1)

            slots(act, slot)

        @block.vector
        def _(dve):
            vec = nc.vector
            dve.wait_ge(const_ld, 16 * CONST_LOADS)
            dve.wait_ge(cls_ld, 16)
            dve.wait_ge(const_pool, CONST_POOL)
            vec.tensor_tensor(pos[:, 0, :], pos[:, 0, :], tokb[:, 0, :], ALU.add).then_inc(const_dve, 1)
            vec.tensor_tensor(pos[0:T1, 1, :], pos[0:T1, 1, :], tokb[0:T1, 1, :], ALU.add).then_inc(const_dve, 1)
            dve.wait_ge(const_dve, 2)

            def stats(x, st, st_s, mv, mv_s, var, var_s, i):
                for t, (_, n) in enumerate(TILES):
                    last = vec.bn_stats(st[0:n, t, :], x[0:n, t, :])
                last.then_inc(st_s, 1)
                wait_apart(dve, st_s, i + 1)
                for t, (_, n) in enumerate(TILES):
                    last = vec.bn_aggr(mv[0:n, t, :], st[0:n, t, :])
                last.then_inc(mv_s, 1)
                wait(dve, mv_s, i + 1)
                vec.tensor_scalar(var[:], mv[:, :, 1], EPS, None, ALU.add).then_inc(var_s, 1)

            def slot(s, u, a, b, c):
                v = 1 - u
                if c:
                    wait(dve, pv_used, s)
                    wait(dve, bc_ps, s - 1)
                    vec.reciprocal(rec[KH:VW, :, :], o_raw[v][KH:VW, :, :]).then_inc(rec_ready, 1)
                if a:
                    wait(dve, tok_ps, s + 2)
                    wait(dve, hres_ready, s)
                    for t, (_, n) in enumerate(TILES):
                        last = vec.scalar_tensor_tensor(h[v][0:n, t, :], ps5[0:n, t * D:(t + 1) * D], 1.0 / 255.0,
                                                 pos[0:n, t, :], ALU.mult, ALU.add)
                    last.then_inc(h_ready, 1)
                    wait(dve, h_ready, s + 2)
                    wait(dve, xn_ready, s + 1)
                    stats(h[v], stats1, st1, mv1, mv1_s, var1, var1_s, s + 1)

                def maxima(lo, hi):
                    for m in range(lo, hi):
                        wait(dve, mx_ps, 9 * s + m + 1)
                        if m == 0:
                            wait(dve, mT_ps, s)
                        if m < 3:
                            vec.tensor_reduce(mx[:, 0, 4 * m:4 * m + 4],
                                              ps_max[m % 3][:, :].rearrange("p (j t) -> p j t", j=4),
                                              AX.X, ALU.max).then_inc(mx_red, 1)
                        else:
                            hd = 2 * (m - 3)
                            vec.tensor_reduce(mx[0:T1, 1, hd:hd + 2],
                                              ps_max[m % 3][0:T1, 0:ST_N].rearrange("p (j t) -> p j t", j=2),
                                              AX.X, ALU.max).then_inc(mx_red, 1)
                if b:
                    maxima(0, 3)
                if a:
                    wait(dve, rstd1_s, s + 2)
                    wait(dve, xnT_ps, s + 1)
                    for t, (_, n) in enumerate(TILES):
                        last = vec.tensor_scalar(xn[0:n, t, :], h[v][0:n, t, :], mv1[0:n, t, 0:1], rstd1[0:n, t:t + 1],
                                          ALU.subtract, ALU.mult)
                    last.then_inc(xn_ready, 1)
                if b:
                    maxima(3, 9)
                if c:
                    wait(dve, bc_ps, s)
                    wait(dve, wo_ps, s - 2)
                    vec.tensor_tensor(oT[v][:], o_raw[v][0:KH, :, :],
                                      ps6[0:KH, 0:ST_N].rearrange("p (a t) -> p a t", a=2), ALU.mult)\
                        .then_inc(oT_ready, 1)
                    wait(dve, wo_ps, s)
                    if not isinstance(s, int) or s >= 3:
                        wait(dve, h2_out[v], (s - 1 - v) * 16)
                    wait(dve, hres_ready, s)
                    for t, (_, n) in enumerate(TILES):
                        last = vec.tensor_tensor(h2[v][0:n, t, :], ps5[0:n, t * D:(t + 1) * D], h_res[v][0:n, t, :],
                                          ALU.add)
                    last.then_inc(h2_ready, 1)
                    wait(dve, h2_ready, s)
                    wait(dve, xn2_ready, s - 1)
                    stats(h2[v], stats2, st2, mv2, mv2_s, var2, var2_s, s - 1)
                if a:
                    wait(dve, v_ps, s + 2)
                    wait(dve, pv_ps, s)
                    for t, (_, n) in enumerate(TILES):
                        for half in range(2):
                            dst = vz[v][0:n, t, half * HH:(half + 1) * HH, :].rearrange("p j c -> p (j c)")
                            dst = bass.AP(tensor=dst.tensor, offset=dst.offset,
                                          ap=[list(dst.ap[0]), [VW + DH, HH], [1, DH]])
                            col = t * D + half * KH
                            last = vec.tensor_tensor(dst, ps5[0:n, col:col + KH].rearrange("p (j d) -> p j d", j=HH),
                                                    bv[0:n, half * KH:(half + 1) * KH]
                                                    .rearrange("p (j d) -> p j d", j=HH), ALU.add)
                    last.then_inc(v_ready, 1)
                if c:
                    wait(dve, rstd2_s, s)
                    if not isinstance(s, int) or s >= 3:
                        wait(dve, tab_out[v], (s - 1 - v) * 16)
                    for t, (_, n) in enumerate(TILES):
                        last = vec.tensor_scalar(tab[v][0:n, t, 0:D], h2[v][0:n, t, :], mv2[0:n, t, 0:1],
                                          rstd2[0:n, t:t + 1], ALU.subtract, ALU.mult)
                    last.then_inc(xn2_ready, 1)
                    for t, (_, n) in enumerate(TILES):
                        last = vec.tensor_scalar(tab[v][0:n, t, D:SC0], h2[v][0:n, t, 0:SC0 - D], mv2[0:n, t, 0:1],
                                                 rstd2[0:n, t:t + 1], ALU.subtract, ALU.mult)
                    wait(dve, lg_used, s)
                    wait(dve, sc_ready, s - 1)
                    vec.tensor_scalar(ex1[:, 0, :], ex[:, 0, :], 1.0, None, ALU.add)
                    vec.tensor_scalar(ex1[0:T1, 1, :], ex[0:T1, 1, :], 1.0, None, ALU.add).then_inc(ex1_s, 1)
                    wait(dve, ex1_s, s)
                    vec.reciprocal(tab[v][:, 0, SC0:ROW], ex1[:, 0, :])
                    vec.reciprocal(tab[v][0:T1, 1, SC0:ROW], ex1[0:T1, 1, :]).then_inc(sc_ready, 1)

            slots(dve, slot)

        @block.tensor
        def _(pe):
            mm = nc.tensor.matmul
            pe.wait_ge(const_ld, 16 * CONST_LOADS)
            pe.wait_ge(const_pool, CONST_POOL)

            def transposes(dst, src, n_of):
                for t, (t0, n) in enumerate(TILES):
                    for half in range(2):
                        last = nc.tensor.transpose(dst[0:KH, half * TOK + t0:half * TOK + t0 + n],
                                                   src[0:n, t, half * KH:(half + 1) * KH], ident[0:n, 0:n])
                return last

            def slot(s, u, a, b, c):
                v = 1 - u
                if a:
                    wait(pe, pat_ld[v], (s + 1 - v) * 8 + 16)
                    if isinstance(s, int) and s <= 1:
                        wait(pe, v_ready, s + 1)
                    else:
                        wait(pe, lg_used, s - 1)
                    for t, (t0, n) in enumerate(TILES):
                        for k in range(KC):
                            last = mm(ps5[0:n, t * D:(t + 1) * D], patches[v][:, k, t0:t0 + n], w_tok[:, k, :],
                                      start=k == 0, stop=k == KC - 1)
                    last.then_inc(tok_ps, 1)
                if b:
                    wait(pe, qz_ld[u], (s - u) * (16 * HH // 2) + 16 * HH)
                    wait(pe, k_ready, s + 1)
                    for m in range(9):
                        bank = ps_max[m % 3]
                        wait(pe, mx_red, 9 * s + m - 2)
                        if m < 3:
                            mm(bank[:, :], ident_bf[:], mask0[:].rearrange("p j t -> p (j t)"), start=True, stop=False)
                            for j in range(4):
                                half, hd = divmod(4 * m + j, HH)
                                last = mm(bank[:, j * P:(j + 1) * P], qz[u][0:KH, half, hd, 0:P],
                                          kT[u][0:KH, half, 0:P], start=False, stop=j == 3)
                        else:
                            mm(bank[0:T1, 0:ST_N], ident_bf[0:T1, 0:T1], mask1[0:T1].rearrange("p j t -> p (j t)"),
                               start=True, stop=False)
                            for j in range(2):
                                half, hd = divmod(2 * (m - 3) + j, HH)
                                last = mm(bank[0:T1, j * TOK:(j + 1) * TOK], qz[u][0:KH, half, hd, P:TOK],
                                          kT[u][0:KH, half, :], start=False, stop=j == 1)
                        last.then_inc(mx_ps, 1)
                if c:
                    wait(pe, rec_ready, s)
                    if isinstance(s, int) and s == 1:
                        wait(pe, mT_ready, s)
                    else:
                        wait(pe, sT_ready, s - 1)
                    mm(ps6[0:KH, 0:ST_N], sel_sum[:], rec[:].rearrange("p a t -> p (a t)"), start=True, stop=True)\
                        .then_inc(bc_ps, 1)
                if a:
                    wait(pe, xn_ready, s + 2)
                    if isinstance(s, int) and s == 0:
                        wait(pe, k_ready, s + 1)
                    else:
                        wait(pe, pv_used, s)
                    transposes(ps7, xn, TILES).then_inc(xnT_ps, 1)
                if c:
                    wait(pe, oT_ready, s)
                    if a:
                        wait(pe, h_ready, s + 2)
                    else:
                        wait(pe, lg_used, s - 1)
                    for t, (t0, n) in enumerate(TILES):
                        for half in range(2):
                            last = mm(ps5[0:n, t * D:(t + 1) * D], oT[v][:, half, t0:t0 + n], w_out[:, half, :],
                                      start=half == 0, stop=half == 1)
                    last.then_inc(wo_ps, 1)
                if a:
                    wait(pe, xnT_ready, s + 2)
                    if c:
                        wait(pe, oT_ready, s)
                    else:
                        wait(pe, q_ready, s + 1)
                    for which, bank, done in ((0, ps6, q_ps), (1, ps7, k_ps)):
                        for half in range(2):
                            for k in range(2):
                                col = which * D + half * KH
                                last = mm(bank[0:KH, half * TOK:(half + 1) * TOK], w_qkv[:, k, col:col + KH],
                                          xnT[v][:, k, :], start=k == 0, stop=k == 1)
                        last.then_inc(done, 1)
                    if c:
                        wait(pe, h2_ready, s)
                    else:
                        wait(pe, h_ready, s + 2)
                    for t, (t0, n) in enumerate(TILES):
                        for k in range(2):
                            last = mm(ps5[0:n, t * D:(t + 1) * D], xnT[v][:, k, t0:t0 + n], w_qkv[:, k, 2 * D:3 * D],
                                      start=k == 0, stop=k == 1)
                    last.then_inc(v_ps, 1)
                if b:
                    wait(pe, mx_red, 9 * s + 9)
                    if a:
                        wait(pe, q_ready, s + 2)
                    else:
                        wait(pe, oT_ready, s)
                    for t, (t0, n) in enumerate(TILES):
                        last = nc.tensor.transpose(ps6[0:HEADS, t0:t0 + n], mx[0:n, t, :], ident[0:n, 0:n])
                    last.then_inc(mT_ps, 1)
                if c:
                    wait(pe, xn2_ready, s)
                    if a:
                        wait(pe, k_ready, s + 2)
                    else:
                        wait(pe, pv_used, s)
                    transposes(ps7, tab[v], TILES).then_inc(x2T_ps, 1)

                def scores(half):
                    for part in range(4):
                        unit = 4 * half + part
                        bank = ps_st[unit % 2]
                        wait(pe, exp_done, 8 * s + unit - 1)
                        if part < 3:
                            last = mm(bank[:, 0:ST_N], kT[u][:, half, 0:P],
                                      qz[u][:, half, 2 * part:2 * part + 2, :], start=True, stop=True)
                        else:
                            last = mm(bank[0:T1, 0:HH * T1], kT[u][:, half, P:TOK], qz[u][:, half, :, P:TOK],
                                      start=True, stop=True)
                        last.then_inc(st_ps, 1)
                if b:
                    wait(pe, mrow_ld[u], (s - u) * 8 + 16)
                    scores(0)
                if c:
                    wait(pe, x2T_ready, s)
                    if a:
                        wait(pe, v_ready, s + 2)
                    else:
                        wait(pe, h2_ready, s)
                    for t, (t0, n) in enumerate(TILES):
                        for k in range(2):
                            last = mm(ps5[0:n, t * E:(t + 1) * E], x2T[v][:, k, t0:t0 + n], w_gate[:, k, :],
                                      start=k == 0, stop=k == 1)
                    last.then_inc(lg_ps, 1)
                if b:
                    scores(1)
                if c:
                    wait(pe, sc_ready, s)
                    if b:
                        wait(pe, mT_ready, s + 1)
                    else:
                        wait(pe, oT_ready, s)
                    for t, (t0, n) in enumerate(TILES):
                        last = nc.tensor.transpose(ps6[0:E, t0:t0 + n], tab[v][0:n, t, SC0:ROW], ident[0:n, 0:n])
                    last.then_inc(sT_ps, 1)
                if b:
                    wait(pe, v_ready, s + 1)
                    if c:
                        wait(pe, x2T_ready, s)
                    else:
                        wait(pe, k_ready, s + 2)
                    for half in range(2):
                        wait(pe, sel_done, 8 * s + 4 * half + 4)
                        for j in range(HH):
                            hd = half * HH + j
                            mm(ps7[0:VW, half * TOK:(half + 1) * TOK], vz[u][:, 0, hd, :], pt0[u][:, hd, :],
                               start=j == 0, stop=False)
                            last = mm(ps7[0:VW, half * TOK + P:(half + 1) * TOK], vz[u][0:T1, 1, hd, :],
                                      pt1[u][0:T1, hd, :], start=False, stop=j == HH - 1)
                    last.then_inc(pv_ps, 1)

            slots(pe, slot)


CH = ST_N
SH_CHUNKS = N // CH
STEPS = 32
GT = (CAP + P - 1) // P
LAST = CAP - (GT - 1) * P
IDX_GROUPS = ((0, 3), (3, 6), (6, 9), (9, 12), (12, GT))
assert SH_CHUNKS == 2 * E and STEPS == 4 * (SH_CHUNKS // 4)


def rows_of(t):
    return P if t < GT - 1 else LAST


XT = 3
WT = 5
PASSES = ((0, 0), (1, 1), (2, 2), (3, 0), (4, 1))
W64 = D - P


def stage_s(nc, dram, idx_all):
    ctx = ExitStack()
    with ctx:
        def sb(name, shape, dt=F32):
            return ctx.enter_context(nc.sbuf_tensor(name, shape, dt))

        def sem(name):
            return ctx.enter_context(nc.semaphore(name))

        w_raw = sb("w_raw", [P, 2, XT, F_SH])
        w_gu = sb("w_gu", [P, 2, WT, F_SH], F32R)
        wd_raw = sb("wd_raw", [P, FS, D])
        w_d = sb("w_d", [P, FS, 2, D], F32R)
        xr = [sb(f"xr{u}", [P, XT, CH]) for u in range(2)]
        xs = [sb(f"xs{u}", [P, XT, CH], F32R) for u in range(2)]
        hs = [sb(f"hs{u}", [P, 4, D]) for u in range(2)]
        sg = [sb(f"sg{u}", [P, CH]) for u in range(2)]
        prod = [sb(f"prod{u}", [P, CH]) for u in range(2)]
        hidh = [sb(f"hidh{u}", [P, FS, CH], F32R) for u in range(2)]
        hidl = [sb(f"hidl{u}", [P, FS, CH], F32R) for u in range(2)]
        os_ = [sb(f"os{u}", [P, 4, D]) for u in range(2)]

        s1 = sb("s1", [P, CAP])
        hits = sb("hits", [P, CAP], BF16)
        cnt = sb("cnt", [P, 1])
        thr = sb("thr", [P, 1], I32)
        cand = sb("cand", [P, 1], I32)
        inc = sb("inc", [P, 1], I32)
        bitf = sb("bitf", [P, 1])
        biti = sb("biti", [P, 1], I32)
        same_expert = sb("same_expert", [P, P])
        s2 = sb("s2", [NBLK, E, P])
        thr_b = sb("thr_b", [NBLK, E])
        mask = sb("mask", [NBLK, E * P])
        keep_run = sb("keep_run", [NBLK, E * P])
        g_run = sb("g_run", [NBLK, E * P])
        e_run = sb("e_run", [NBLK, E * P])
        tots = sb("tots", [NBLK, 2 * E])
        before = sb("before", [NBLK, 2 * E])
        need = sb("need", [NBLK, E])
        lo = sb("lo", [NBLK, E])
        hi = sb("hi", [NBLK, E])
        earlier = sb("earlier", [NBLK, NBLK])
        ones = sb("ones", [NBLK, NBLK])
        rank = sb("rank", [NBLK, E, P + 1], F16)
        slot_no = sb("slot_no", [NBLK, CAP], F16)
        ge = sb("ge", [NBLK, CAP], F16)
        onehot = sb("onehot", [NBLK, CAP], F16)
        jcol = sb("jcol", [P, GT])
        junk = sb("junk", [P, GT, P], BF16)
        bcol = sb("bcol", [P, GT])
        acol = sb("acol", [P, GT])

        ps_g = [ctx.enter_context(nc.psum_tensor(f"ps_g{i}", [P, 512], F32)) for i in range(2)]
        ps_u = [ctx.enter_context(nc.psum_tensor(f"ps_u{i}", [P, 512], F32)) for i in range(2)]
        ps_d = [ctx.enter_context(nc.psum_tensor(f"ps_d{i}", [P, 512], F32)) for i in range(2)]
        ps_i = [ctx.enter_context(nc.psum_tensor(f"ps_i{i}", [P, 512], F32)) for i in range(2)]

        wld = sem("wld")
        s_ld = sem("s_ld")
        cst = sem("cst")
        xs_ld = [sem(f"xs_ld{u}") for u in range(2)]
        hs_ld = [sem(f"hs_ld{u}") for u in range(2)]
        g_ps = sem("g_ps")
        sg_ready = sem("sg_ready")
        w_high = sem("w_high")
        w_low = sem("w_low")
        wd_low = sem("wd_low")
        x1_ready = sem("x1_ready")
        xh_ready = sem("xh_ready")
        xl_ready = sem("xl_ready")
        prod_ready = sem("prod_ready")
        hh_ready = sem("hh_ready")
        hl_ready = sem("hl_ready")
        os_half = sem("os_half")
        dn_ps = sem("dn_ps")
        os_ready = sem("os_ready")
        os_out = [sem(f"os_out{u}") for u in range(2)]
        thr_init = sem("thr_init")
        cand_s = sem("cand_s")
        cnt_s = sem("cnt_s")
        cnt_ps = sem("cnt_ps")
        inc_s = sem("inc_s")
        bit_s = sem("bit_s")
        bitf_s = sem("bitf_s")
        thr_s = sem("thr_s")
        thr_st = sem("thr_st")
        thr_ld = sem("thr_ld")
        rk = sem("rk")
        rk_ps = sem("rk_ps")
        oh_ge = sem("oh_ge")
        oh_s = sem("oh_s")
        ix_ps = sem("ix_ps")
        ix_used = sem("ix_used")
        list_s = sem("list_s")
        passed = sem("passed_s")
        CST = 12
        NG = len(IDX_GROUPS)

        def wait_apart(eng, s, value):
            wait(eng, s, value)
            if not isinstance(value, int):
                eng.sem_inc(passed, 1)

        def chunks(eng, chunk, middle):
            half = SH_CHUNKS // 2
            for lo_c, hi_c, second in ((0, half, False), (half, SH_CHUNKS, True)):
                start = lo_c
                if not second:
                    for c in range(2):
                        chunk(c, c % 2, False)
                    start = lo_c + 2
                stop = hi_c - 2 if second else hi_c
                with eng.Fori(0, (stop - start) // 2) as it:
                    for u in range(2):
                        chunk(it * 2 + (start + u), (start + u) % 2, second)
                if second:
                    for c in range(hi_c - 2, hi_c):
                        chunk(c, c % 2, True)
                else:
                    middle()

        block = ctx.enter_context(nc.Block())

        @block.sync
        def _(sp):
            for e in range(E):
                sp.dma_start(s1[e * CHUNKS:(e + 1) * CHUNKS, :],
                             dram["sT"][e, 0:N].rearrange("(c t) -> c t", c=CHUNKS)).then_inc(s_ld, 16)
            for dst, src in ((w_raw[:, 0], "WsgT"), (w_raw[:, 1], "WsuT"), (wd_raw[:], "WsdT")):
                sp.dma_start(dst, dram[src]).then_inc(wld, 16)
            sp.dma_start(s2[:], dram["sT"].rearrange("e (a b) -> a e b", b=P)).then_inc(wld, 16)

            def load_x(c, u):
                for dst, r0, r1 in ((xr[u][:, 0, :], 0, P), (xr[u][0:W64, 1, :], P, D), (xr[u][W64:P, 1, :], 0, W64),
                                    (xr[u][:, 2, :], W64, D)):
                    sp.dma_start(dst, dram["x2T"][r0:r1, bass.ds(c * CH, CH)]).then_inc(xs_ld[u], 16)

            def load_h(c, u):
                for i in range(2):
                    sp.dma_start(hs[u][:, 2 * i, :], dram["h2"][bass.ds(c * CH + i * TOK, P), :])\
                        .then_inc(hs_ld[u], 16)
                    sp.dma_start(hs[u][0:T1, 2 * i + 1, :], dram["h2"][bass.ds(c * CH + i * TOK + P, T1), :])\
                        .then_inc(hs_ld[u], 16)

            load_x(0, 0)
            load_h(0, 0)

            def chunk(c, u, second):
                more = not (isinstance(c, int) and c + 1 >= SH_CHUNKS)
                if more:
                    wait_apart(sp, xl_ready, c)
                    load_x(c + 1, 1 - u)
                if not (isinstance(c, int) and c == 0):
                    for i in range(2):
                        store(c - 1, 1 - u, i)
                if more:
                    load_h(c + 1, 1 - u)

            def store(c, u, i):
                wait_apart(sp, os_ready, 4 * c + 2 * i + 2)
                sp.dma_start(dram["out"][bass.ds(c * CH + i * TOK, P), :], os_[u][:, 2 * i, :])\
                    .then_inc(os_out[u], 16)
                sp.dma_start(dram["out"][bass.ds(c * CH + i * TOK + P, T1), :], os_[u][0:T1, 2 * i + 1, :])\
                    .then_inc(os_out[u], 16)

            def middle():
                sp.wait_ge(thr_s, STEPS)
                sp.dma_start(dram["thr"], thr[0:P:CHUNKS, :].bitcast(F32)).then_inc(thr_st, 16)
                sp.wait_ge(thr_st, 16)
                sp.dma_start(thr_b[:], dram["thr"].rearrange("e one -> one e").to_broadcast([NBLK, E]))\
                    .then_inc(thr_ld, 16)

            chunks(sp, chunk, middle)
            for i in range(2):
                store(SH_CHUNKS - 1, 1, i)
            for u in range(2):
                sp.wait_ge(os_out[u], 64 * SH_CHUNKS // 2)

        @block.gpsimd
        def _(pool):
            made = [0]

            def made_one(ins):
                made[0] += 1
                ins.then_inc(cst, 1)
                pool.wait_ge(cst, made[0])

            made_one(pool.memset(same_expert[:], 1.0))
            v = same_expert[:].rearrange("p (e c) -> p e c", e=E)
            made_one(pool.affine_select(out=v, in_=v, compare_op=ALU.is_ge, fill=0.0, base=0,
                                        pattern=[[-CHUNKS, E], [0, CHUNKS]], channel_multiplier=1))
            made_one(pool.affine_select(out=v, in_=v, compare_op=ALU.is_ge, fill=0.0, base=CHUNKS - 1,
                                        pattern=[[CHUNKS, E], [0, CHUNKS]], channel_multiplier=-1))
            made_one(pool.memset(ones[:], 1.0))
            made_one(pool.memset(earlier[:], 1.0))
            made_one(pool.affine_select(out=earlier[:], in_=earlier[:], compare_op=ALU.is_gt, fill=0.0, base=0,
                                        pattern=[[1, NBLK]], channel_multiplier=-1))
            made_one(pool.memset(keep_run[:], 1.0))
            k = keep_run[:].rearrange("p (e b) -> p e b", e=E)
            made_one(pool.affine_select(out=k, in_=k, compare_op=ALU.not_equal, fill=0.0, base=0,
                                        pattern=[[0, E], [1, P]], channel_multiplier=0))
            made_one(pool.iota(rank[:, :, P:P + 1], pattern=[[0, E], [0, 1]], base=0, channel_multiplier=1,
                               allow_small_or_imprecise_dtypes=True))
            made_one(pool.iota(slot_no[:], pattern=[[1, CAP]], base=0, channel_multiplier=0,
                               allow_small_or_imprecise_dtypes=True))
            made_one(pool.iota(jcol[:], pattern=[[P, GT]], base=0, channel_multiplier=1,
                               allow_small_or_imprecise_dtypes=True))
            made_one(pool.memset(idx_all[:], 0))
            assert made[0] == CST
            pool.wait_ge(w_high, 2)
            pool.tensor_tensor(w_d[:, :, 1, :], wd_raw[:], w_d[:, :, 0, :].bitcast(F32), ALU.subtract)\
                .then_inc(wd_low, 1)

            def split_x(c, u):
                wait(pool, xh_ready, c + 1)
                if isinstance(c, int) and c == 0:
                    pool.wait_ge(wd_low, 1)
                else:
                    wait(pool, hl_ready, FS * (c - 1) + 2)
                pool.tensor_tensor(xs[u][W64:P, 1, :], xr[u][W64:P, 1, :], xs[u][W64:P, 1, :].bitcast(F32),
                                   ALU.subtract).then_inc(x1_ready, 1)
                wait(pool, x1_ready, c + 1)
                pool.tensor_tensor(xs[u][:, 2, :], xr[u][:, 2, :], xs[u][:, 2, :].bitcast(F32), ALU.subtract)\
                    .then_inc(xl_ready, 1)

            def low(c, u, f):
                wait(pool, hh_ready, FS * c + f + 1)
                pool.tensor_tensor(hidl[u][:, f, :], prod[(u + f) % 2][:], hidh[u][:, f, :].bitcast(F32),
                                   ALU.subtract).then_inc(hl_ready, 1)

            split_x(0, 0)

            def chunk(c, u, second):
                low(c, u, 0)
                low(c, u, 1)
                if not (isinstance(c, int) and c + 1 >= SH_CHUNKS):
                    split_x(c + 1, 1 - u)
                low(c, u, 2)

            chunks(pool, chunk, lambda: None)

        @block.scalar
        def _(act):
            act.wait_ge(wld, 64)
            act.activation(w_gu[:, :, 0:XT, :], w_raw[:], ACT.Copy).then_inc(w_high, 1)
            act.activation(w_d[:, :, 0, :], wd_raw[:], ACT.Copy).then_inc(w_high, 1)

            def high_x(c, u):
                wait(act, xs_ld[u], (c - u) * 32 + 64)
                wait(act, g_ps, FS * (c - 1))
                act.activation(xs[u][:], xr[u][:], ACT.Copy).then_inc(xh_ready, 1)

            def silu(c, u, f):
                wait(act, g_ps, FS * c + f + 1)
                wait(act, prod_ready, FS * c + f - 1)
                act.activation(sg[(u + f) % 2][:], ps_g[(u + f) % 2][:, 0:CH], ACT.Silu).then_inc(sg_ready, 1)

            def high(c, u, f):
                wait(act, prod_ready, FS * c + f + 1)
                if f == 0:
                    wait(act, dn_ps, 4 * (c - 1))
                act.activation(hidh[u][:, f, :], prod[(u + f) % 2][:], ACT.Copy).then_inc(hh_ready, 1)

            high_x(0, 0)

            def chunk(c, u, second):
                silu(c, u, 0)
                silu(c, u, 1)
                high(c, u, 0)
                if not (isinstance(c, int) and c + 1 >= SH_CHUNKS):
                    high_x(c + 1, 1 - u)
                silu(c, u, 2)
                high(c, u, 1)
                high(c, u, 2)

            chunks(act, chunk, lambda: None)

        @block.vector
        def _(dve):
            vec = nc.vector
            dve.wait_ge(w_high, 2)
            vec.tensor_tensor(w_gu[:, :, XT:WT, :], w_raw[:, :, 0:2, :], w_gu[:, :, 0:2, :].bitcast(F32),
                              ALU.subtract).then_inc(w_low, 1)
            vec.memset(thr[:], 0).then_inc(thr_init, 1)
            vec.memset(bitf[:], float(1 << 30)).then_inc(thr_init, 1)
            dve.wait_ge(thr_init, 2)
            vec.tensor_copy(biti[:], bitf[:]).then_inc(bit_s, 1)
            dve.wait_ge(bit_s, 1)
            dve.wait_ge(s_ld, 16 * E)
            dve.wait_ge(cst, CST)

            def count(k):
                wait(dve, thr_s, k)
                wait(dve, bit_s, k + 1)
                vec.tensor_tensor(cand[:], thr[:], biti[:], ALU.bitwise_or).then_inc(cand_s, 1)
                wait(dve, cand_s, k + 1)
                vec.tensor_scalar(hits[:], s1[:], cand[:].bitcast(F32), None, ALU.is_ge, ALU.add,
                                  accum_out=cnt[:]).then_inc(cnt_s, 1)

            def settle(k):
                wait(dve, cnt_ps, k + 1)
                vec.tensor_scalar(inc[:], ps_i[0][:, 0:1], CAP - 0.5, bitf[:], ALU.is_ge, ALU.mult)\
                    .then_inc(inc_s, 1)
                wait(dve, inc_s, k + 1)
                vec.tensor_tensor(thr[:], thr[:], inc[:], ALU.bitwise_or).then_inc(thr_s, 1)
                vec.tensor_scalar(bitf[:], bitf[:], 0.5, None, ALU.mult).then_inc(bitf_s, 1)

            def halve(k):
                wait(dve, bitf_s, k + 1)
                vec.tensor_copy(biti[:], bitf[:]).then_inc(bit_s, 1)

            def product(c, u, f):
                wait(dve, sg_ready, FS * c + f + 1)
                wait(dve, hl_ready, FS * c + f - 1)
                vec.tensor_tensor(prod[(u + f) % 2][:], sg[(u + f) % 2][:], ps_u[(u + f) % 2][:, 0:CH], ALU.mult)\
                    .then_inc(prod_ready, 1)

            def outputs(c, u, i):
                for t in range(2 * i, 2 * i + 2):
                    n = TILES[t % 2][1]
                    wait(dve, dn_ps, 4 * c + t + 1)
                    if t == 0:
                        wait(dve, hs_ld[u], (c - u) * 32 + 64)
                        if not isinstance(c, int) or c >= 2:
                            wait(dve, os_out[u], (c - u) * 32)
                    vec.tensor_tensor(os_[u][0:n, t, :], ps_d[t % 2][0:n, D:2 * D], hs[u][0:n, t, :], ALU.add)\
                        .then_inc(os_half, 1)
                    wait(dve, os_half, 4 * c + t + 1)
                    vec.tensor_tensor(os_[u][0:n, t, :], ps_d[t % 2][0:n, 0:D], os_[u][0:n, t, :], ALU.add)\
                        .then_inc(os_ready, 1)

            def make_list(j):
                wait(dve, ix_ps, NG * j)
                wait(dve, list_s, j)
                vec.tensor_scalar(ge[:], slot_no[:], lo[:, bass.ds(j, 1)], None, ALU.is_ge).then_inc(oh_ge, 1)
                wait(dve, oh_ge, j + 1)
                vec.scalar_tensor_tensor(onehot[:], slot_no[:], hi[:, bass.ds(j, 1)], ge[:], ALU.is_lt, ALU.mult)\
                    .then_inc(oh_s, 1)

            def take(j, u, g):
                t0, t1 = IDX_GROUPS[g]
                wait(dve, ix_ps, NG * j + g + 1)
                bank = ps_i[(u + g) % 2]
                for t in range(t0, t1):
                    n, c0 = rows_of(t), (t - t0) * (P + 1)
                    vec.tensor_scalar(junk[0:n, t, :], bank[0:n, c0:c0 + P], jcol[0:n, t:t + 1], None, ALU.is_le,
                                      ALU.add, accum_out=bcol[0:n, t:t + 1])
                n = rows_of(t1 - 1)
                vec.tensor_copy(acol[0:n, t0:t1],
                                bank[0:n, 0:(t1 - t0) * (P + 1)].rearrange("p (t b) -> p t b", b=P + 1)[:, :, P])\
                    .then_inc(ix_used, 1)

            def write_list(j):
                wait(dve, ix_used, NG * (j + 1) + 1)
                vec.scalar_tensor_tensor(idx_all[:, bass.ds(j * GT, GT)], acol[:], float(P), bcol[:], ALU.mult,
                                         ALU.add).then_inc(list_s, 1)

            def chunk(c, u, second):
                has_out = not (isinstance(c, int) and c == 0)
                product(c, u, 0)
                if second:
                    j = c - E
                    make_list(j)
                    take(j, u, 0)
                    product(c, u, 1)
                    take(j, u, 1)
                    product(c, u, 2)
                    take(j, u, 2)
                    outputs(c - 1, 1 - u, 0)
                    take(j, u, 3)
                    outputs(c - 1, 1 - u, 1)
                    take(j, u, 4)
                    write_list(j)
                else:
                    count(2 * c)
                    product(c, u, 1)
                    settle(2 * c)
                    halve(2 * c)
                    count(2 * c + 1)
                    product(c, u, 2)
                    if has_out:
                        outputs(c - 1, 1 - u, 0)
                    settle(2 * c + 1)
                    halve(2 * c + 1)
                    if has_out:
                        outputs(c - 1, 1 - u, 1)

            def middle():
                n = [0]

                def step(ins):
                    n[0] += 1
                    ins.then_inc(rk, 1)
                    dve.wait_ge(rk, n[0])

                s2v = s2[:].rearrange("p e b -> p (e b)")
                dve.wait_ge(wld, 64)
                dve.wait_ge(thr_ld, 16)
                per_block = thr_b[:, :, None].to_broadcast([NBLK, E, P])
                m3 = mask[:].rearrange("p (e b) -> p e b", e=E)
                for run, op, o in ((g_run, ALU.is_gt, 0), (e_run, ALU.is_equal, E)):
                    step(vec.tensor_tensor(m3, s2[:], per_block, op))
                    step(vec.tensor_tensor_scan(run[:], keep_run[:], mask[:], 0.0, ALU.mult, ALU.add))
                    step(vec.tensor_copy(tots[:, o:o + E], run[:].rearrange("p (e b) -> p e b", e=E)[:, :, P - 1]))
                dve.wait_ge(rk_ps, 1)
                step(vec.tensor_copy(before[:], ps_i[1][0:NBLK, 0:2 * E]))
                step(vec.tensor_scalar(need[:], ps_i[1][0:NBLK, 2 * E:3 * E], -1.0, float(CAP), ALU.mult, ALU.add))
                step(vec.tensor_tensor(lo[:], before[:, E:2 * E], need[:], ALU.min))
                step(vec.tensor_tensor(lo[:], lo[:], before[:, 0:E], ALU.add))
                g3 = g_run[:].rearrange("p (e b) -> p e b", e=E)
                e3 = e_run[:].rearrange("p (e b) -> p e b", e=E)
                step(vec.tensor_tensor(g3, g3, before[:, 0:E, None].to_broadcast([NBLK, E, P]), ALU.add))
                step(vec.tensor_tensor(e3, e3, before[:, E:2 * E, None].to_broadcast([NBLK, E, P]), ALU.add))
                step(vec.tensor_tensor(e3, e3, need[:, :, None].to_broadcast([NBLK, E, P]), ALU.min))
                step(vec.tensor_tensor(rank[:, :, 0:P], g3, e3, ALU.add))
                step(vec.tensor_copy(hi[:], rank[:, :, P - 1]))
                step(vec.memset(bcol[:], 0.0))
                vec.memset(acol[:], 0.0).then_inc(ix_used, 1)
                dve.wait_ge(ix_used, 1)

            chunks(dve, chunk, middle)
            for i in range(2):
                outputs(SH_CHUNKS - 1, 1, i)

        @block.tensor
        def _(pe):
            mm = nc.tensor.matmul
            pe.wait_ge(w_low, 1)
            pe.wait_ge(wd_low, 1)
            pe.wait_ge(cst, CST)

            def hidden(c, u, f):
                if f == 0:
                    wait(pe, xl_ready, c + 1)
                wait(pe, prod_ready, FS * c + f - 1)
                for m, bank in ((0, ps_g), (1, ps_u)):
                    for wt, xt in PASSES:
                        last = mm(bank[(u + f) % 2][:, 0:CH], w_gu[:, m, wt, f * P:(f + 1) * P], xs[u][:, xt, :],
                                  start=wt == 0, stop=wt == WT - 1)
                last.then_inc(g_ps, 1)

            def down(c, u, i):
                for t in range(2 * i, 2 * i + 2):
                    t0, n = TILES[t % 2]
                    cols = slice(i * TOK + t0, i * TOK + t0 + n)
                    wait(pe, hl_ready, FS * c + FS)
                    wait(pe, os_ready, 4 * c + t - 1)
                    for k in range(FS):
                        mm(ps_d[t % 2][0:n, 0:2 * D], hidh[u][:, k, cols], w_d[:, k].rearrange("p h n -> p (h n)"),
                           start=k == 0, stop=False)
                        last = mm(ps_d[t % 2][0:n, 0:D], hidl[u][:, k, cols], w_d[:, k, 0, :],
                                  start=False, stop=k == FS - 1)
                    last.then_inc(dn_ps, 1)

            def count(k):
                wait(pe, cnt_s, k + 1)
                mm(ps_i[0][:, 0:1], same_expert[:], cnt[:], start=True, stop=True).then_inc(cnt_ps, 1)

            def lists(j, u, g):
                t0, t1 = IDX_GROUPS[g]
                if g == 0:
                    wait(pe, oh_s, j + 1)
                (wait if g < NG - 1 else wait_apart)(pe, ix_used, NG * j + g)
                for t in range(t0, t1):
                    n, c0 = rows_of(t), (t - t0) * (P + 1)
                    last = mm(ps_i[(u + g) % 2][0:n, c0:c0 + P + 1], onehot[:, t * P:t * P + n],
                              rank[:, bass.ds(j, 1), :].rearrange("p e b -> p (e b)"), start=True, stop=True)
                last.then_inc(ix_ps, 1)

            def chunk(c, u, second):
                has_out = not (isinstance(c, int) and c == 0)
                hidden(c, u, 0)
                hidden(c, u, 1)
                if second:
                    j = c - E
                    lists(j, u, 0)
                    lists(j, u, 1)
                    hidden(c, u, 2)
                    lists(j, u, 2)
                    down(c - 1, 1 - u, 0)
                    lists(j, u, 3)
                    down(c - 1, 1 - u, 1)
                    lists(j, u, 4)
                else:
                    count(2 * c)
                    hidden(c, u, 2)
                    if has_out:
                        down(c - 1, 1 - u, 0)
                    count(2 * c + 1)
                    if has_out:
                        down(c - 1, 1 - u, 1)

            def middle():
                pe.wait_ge(rk, 6)
                mm(ps_i[1][0:NBLK, 0:2 * E], earlier[:], tots[:], start=True, stop=True)
                mm(ps_i[1][0:NBLK, 2 * E:4 * E], ones[:], tots[:], start=True, stop=True).then_inc(rk_ps, 1)
                pe.wait_ge(rk, 16)

            chunks(pe, chunk, middle)
            for i in range(2):
                down(SH_CHUNKS - 1, 1, i)


def stage_e(nc, dram, idx_all):
    ctx = ExitStack()
    with ctx:
        def sb(name, shape, dt=F32):
            return ctx.enter_context(nc.sbuf_tensor(name, shape, dt))

        def sem(name):
            return ctx.enter_context(nc.semaphore(name))

        CT = 3
        CHN = GT // CT
        FIRST = [c * CT * P for c in range(CHN)] + [CAP]
        CMAX = CAP - FIRST[CHN - 1]
        UNITS = CHN * FT
        TAIL = (CHN - 1) * CT

        w_raw = sb("ew_raw", [P, 2, XT, F_EXP])
        w_gu = sb("ew_gu", [P, 2, WT, F_EXP], F32R)
        wd_raw = sb("ewd_raw", [P, FT, D])
        w_d = [sb(f"ew_d{u}", [P, FT, 2, D], F32R) for u in range(2)]
        xg = [sb(f"xg{u}", [P, GT, ROW]) for u in range(2)]
        xT = [sb(f"xT{u}", [P, XT, CAP], F32R) for u in range(2)]
        score = [sb(f"score{u}", [P, GT]) for u in range(2)]
        idx_g = [sb(f"idx_g{u}", [P, GT], I32) for u in range(2)]
        idx_s = [sb(f"idx_s{u}", [P, GT], I32) for u in range(2)]
        sg = [sb(f"esg{u}", [P, CMAX]) for u in range(2)]
        prod = [sb(f"eprod{u}", [P, CMAX]) for u in range(2)]
        hidh = [sb(f"ehidh{u}", [P, FT, CMAX], F32R) for u in range(2)]
        hidl = [sb(f"ehidl{u}", [P, FT, CMAX], F32R) for u in range(2)]
        y_low = [sb(f"y_low{u}", [P, D]) for u in range(2)]
        y = sb("y", [P, GT, D])
        ident = sb("eident", [P, P])

        ps_g = [ctx.enter_context(nc.psum_tensor(f"eps_g{i}", [P, 512], F32)) for i in range(2)]
        ps_u = [ctx.enter_context(nc.psum_tensor(f"eps_u{i}", [P, 512], F32)) for i in range(2)]
        ps_d = [ctx.enter_context(nc.psum_tensor(f"eps_d{i}", [P, 512], F32)) for i in range(2)]
        ps_t = [ctx.enter_context(nc.psum_tensor(f"eps_t{i}", [P, 512], F32)) for i in range(2)]

        cst = sem("e_cst")
        gu_ld = sem("gu_ld")
        d_ld = sem("d_ld")
        wh_ready = sem("wh_ready")
        wl_ready = sem("wl_ready")
        dh_ready = sem("dh_ready")
        dl_ready = sem("dl_ready")
        gathered = [sem(f"gathered{u}") for u in range(2)]
        scattered = [sem(f"scattered{u}") for u in range(2)]
        idxg_ready = sem("idxg_ready")
        idxs_ready = sem("idxs_ready")
        score_ready = sem("score_ready")
        tr_ps = sem("tr_ps")
        xh_ready = sem("exh_ready")
        xl_ready = sem("exl_ready")
        gu_ps = sem("gu_ps")
        sg_ready = sem("esg_ready")
        prod_ready = sem("eprod_ready")
        hh_ready = sem("ehh_ready")
        hl_ready = sem("ehl_ready")
        dn_ps = sem("edn_ps")
        ylow_ready = sem("ylow_ready")
        y_ready = sem("y_ready")
        passed = sem("passed_e")

        def wait_apart(eng, s, value):
            wait(eng, s, value)
            if not isinstance(value, int):
                eng.sem_inc(passed, 1)

        def order():
            downs = [[(1, t) for t in range(TAIL, GT)]] + \
                    [[(0, t) for t in range(CT * c, CT * c + CT)] for c in range(CHN - 1)]
            turn = nxt = 0
            for c in range(CHN):
                for f in range(FT):
                    yield "gu", c, f
                    if 1 <= f <= len(downs[c]):
                        yield ("dn", *downs[c][f - 1])
                    if c >= 1 and turn < GT and (f < 5 or c == 1):
                        yield "tr", 0, turn
                        turn += 1
                    if (c, f) == (2, 4):
                        yield "wd", 0, 0
                    if c >= 1 and f >= 1 and nxt < GT:
                        yield "ga", 0, nxt
                        nxt += 1
            assert turn == GT and nxt == GT

        def before(c, f):
            if f:
                return 0, c, f - 1
            return (0, c - 1, FT - 1) if c else (1, CHN - 1, FT - 1)

        def is_first(e, c, f):
            return isinstance(e, int) and e == 0 and c == 0 and f == 0

        def size(c):
            return FIRST[c + 1] - FIRST[c]

        def experts(eng, expert):
            for e in range(2):
                expert(e, e % 2, True, True)
            with eng.Fori(0, (E - 4) // 2) as it:
                for u in range(2):
                    expert(it * 2 + (2 + u), u, True, True)
            for e in range(E - 2, E):
                expert(e, e % 2, e + 1 < E, False)

        block = ctx.enter_context(nc.Block())

        @block.sync
        def _(sp):
            def load_gu(e):
                sp.dma_start(w_raw[:], dram["WguT"][bass.ds(e, 1)].rearrange("e p m k f -> (e p) m k f"))\
                    .then_inc(gu_ld, 16)

            def load_d(e):
                sp.dma_start(wd_raw[:], dram["WdT"][bass.ds(e, 1)].rearrange("e p k f -> (e p) k f"))\
                    .then_inc(d_ld, 16)

            load_gu(0)
            load_d(0)

            def expert(e, u, more, more2):
                if more:
                    wait_apart(sp, wl_ready, FT * (e + 1))
                    load_gu(e + 1)
                    wait_apart(sp, dl_ready, e + 1)
                    load_d(e + 1)

            experts(sp, expert)

        @block.gpsimd
        def _(pool):
            made = [0]

            def made_one(ins):
                made[0] += 1
                ins.then_inc(cst, 1)
                pool.wait_ge(cst, made[0])

            made_one(pool.memset(ident[:], 0.0))
            made_one(pool.affine_select(out=ident[:], in_=ident[:], compare_op=ALU.not_equal, fill=1.0, base=0,
                                        pattern=[[-1, P]], channel_multiplier=1))
            made_one(pool.memset(xg[0][:, GT - 1, :], 0.0))
            made_one(pool.memset(xg[1][:, GT - 1, :], 0.0))

            def gather(e, u, t):
                if t == 0:
                    wait(pool, idxg_ready, e + 1)
                    wait(pool, tr_ps, GT * (e - 1))
                    wait_apart(pool, score_ready, e - 1)
                n = rows_of(t)
                pool.indirect_dma_start(
                    out=xg[u][0:n, t, :], out_offset=None, in_=dram["tab"],
                    in_offset=bass.IndirectOffsetOnAxis(ap=idx_g[u][0:n, t:t + 1], axis=0))\
                    .then_inc(gathered[u], 16)

            def scatter(e, u, t):
                if t == 0:
                    wait(pool, idxs_ready, e + 1)
                    if not isinstance(e, int) or e >= 1:
                        wait(pool, scattered[1 - u], (e - (1 - u) + 1) * (16 * GT // 2))
                wait_apart(pool, y_ready, GT * e + t + 1)
                n = rows_of(t)
                pool.indirect_dma_start(
                    out=dram["out"], out_offset=bass.IndirectOffsetOnAxis(ap=idx_s[u][0:n, t:t + 1], axis=0),
                    in_=y[0:n, t, :], in_offset=None, compute_op=ALU.add).then_inc(scattered[u], 16)

            def low_gu(e, f):
                cols = slice(f * P, (f + 1) * P)
                wait(pool, wh_ready, FT * e + f + 1)
                pool.tensor_tensor(w_gu[:, :, XT:WT, cols], w_raw[:, :, 0:2, cols],
                                   w_gu[:, :, 0:2, cols].bitcast(F32), ALU.subtract).then_inc(wl_ready, 1)

            def low_d(e, u):
                wait(pool, dh_ready, e + 1)
                pool.tensor_tensor(w_d[u][:, :, 1, :], wd_raw[:], w_d[u][:, :, 0, :].bitcast(F32), ALU.subtract)\
                    .then_inc(dl_ready, 1)

            for e in range(2):
                for t in range(GT):
                    gather(e, e, t)
            for f in range(FT):
                low_gu(0, f)
            low_d(0, 0)

            def expert(e, u, more, more2):
                last_down = None
                for kind, c, t in order():
                    if kind == "gu" and c == 0 and not (isinstance(e, int) and e == 0) and t == 0:
                        low_gu(e, FT - 1)
                    if kind == "gu" and c == CHN - 1 and t >= 1 and more:
                        low_gu(e + 1, t - 1)
                    if kind == "gu" and last_down is not None:
                        scatter(*last_down)
                        last_down = None
                    if kind == "dn" and c == 0:
                        last_down = (e, u, t)
                    elif kind == "dn" and not (isinstance(e, int) and e == 0):
                        last_down = (e - 1, 1 - u, t)
                    elif kind == "ga" and more2:
                        gather(e + 2, u, t)
                    elif kind == "wd" and more:
                        low_d(e + 1, 1 - u)

            experts(pool, expert)
            for t in range(TAIL, GT):
                scatter(E - 1, (E - 1) % 2, t)
            for u in range(2):
                pool.wait_ge(scattered[u], 16 * GT * E // 2)

        @block.scalar
        def _(act):
            def high_x(e, u, t):
                wait(act, tr_ps, GT * e + t + 1)
                n = rows_of(t)
                act.activation(xT[u][:, :, t * P:t * P + n],
                               ps_t[(u + t) % 2][:, 0:XT * P].rearrange("p (k t) -> p k t", k=XT)[:, :, 0:n],
                               ACT.Copy).then_inc(xh_ready, 1)

            def high_d(e, u):
                wait(act, d_ld, 16 * (e + 1))
                wait(act, dn_ps, GT * (e - 1))
                act.activation(w_d[u][:, :, 0, :], wd_raw[:], ACT.Copy).then_inc(dh_ready, 1)

            def high(back, e, c, f):
                n = UNITS * (e - back) + FT * c + f
                wait(act, prod_ready, n + 1)
                act.activation(hidh[c % 2][:, f, 0:size(c)], prod[f % 2][:, 0:size(c)], ACT.Copy)\
                    .then_inc(hh_ready, 1)

            def low_y(e, u, t):
                n = rows_of(t)
                wait(act, dn_ps, GT * e + t + 1)
                if t == 0:
                    wait(act, score_ready, e + 1)
                wait(act, y_ready, GT * e + t - 1)
                act.activation(y_low[(u + t) % 2][0:n, :], ps_d[(u + t) % 2][0:n, D:2 * D], ACT.Copy,
                               scale=score[u][0:n, t:t + 1]).then_inc(ylow_ready, 1)

            for t in range(GT):
                high_x(0, 0, t)
            high_d(0, 0)

            def expert(e, u, more, more2):
                for kind, c, t in order():
                    if kind == "gu":
                        n = UNITS * e + FT * c + t
                        wait(act, gu_ps, n + 1)
                        wait(act, prod_ready, n - 1)
                        act.activation(sg[t % 2][:, 0:size(c)], ps_g[t % 2][:, 0:size(c)], ACT.Silu)\
                            .then_inc(sg_ready, 1)
                        if not is_first(e, c, t):
                            back, pc, pf = before(c, t)
                            high(back, e, pc, pf)
                    elif kind == "dn" and c == 0:
                        low_y(e, u, t)
                    elif kind == "dn" and not (isinstance(e, int) and e == 0):
                        low_y(e - 1, 1 - u, t)
                    elif kind == "tr" and more:
                        high_x(e + 1, 1 - u, t)
                    elif kind == "wd" and more:
                        high_d(e + 1, 1 - u)

            experts(act, expert)
            high(1, E, CHN - 1, FT - 1)
            for t in range(TAIL, GT):
                low_y(E - 1, (E - 1) % 2, t)

        @block.vector
        def _(dve):
            vec = nc.vector

            def copy_g(e, u):
                if not isinstance(e, int) or e >= 2:
                    wait_apart(dve, gathered[u], (e - u) * (16 * GT // 2))
                vec.tensor_copy(idx_g[u][:], idx_all[:, bass.ds(e * GT, GT)]).then_inc(idxg_ready, 1)

            def copy_score(e, u):
                wait_apart(dve, gathered[u], (e - u) * (16 * GT // 2) + 16 * GT)
                vec.tensor_copy(score[u][:, :], xg[u][:, :, bass.ds(e + SC0, 1)].rearrange("p t one -> p (t one)"))\
                    .then_inc(score_ready, 1)

            def low_x(e, u, t):
                n = rows_of(t)
                wait(dve, xh_ready, GT * e + t + 1)
                for rows, k in ((slice(W64, P), 1), (slice(0, P), 2)):
                    dst = xT[u][rows, k, t * P:t * P + n]
                    last = vec.tensor_tensor(dst, ps_t[(u + t) % 2][rows, k * P:k * P + n], dst.bitcast(F32),
                                             ALU.subtract)
                last.then_inc(xl_ready, 1)

            def high_gu(e, f, used):
                cols = slice(f * P, (f + 1) * P)
                if f == 0:
                    wait(dve, gu_ld, 16 * (e + 1))
                wait(dve, gu_ps, used)
                vec.tensor_copy(w_gu[:, :, 0:XT, cols], w_raw[:, :, :, cols]).then_inc(wh_ready, 1)

            def product(e, c, f):
                wait(dve, sg_ready, UNITS * e + FT * c + f + 1)
                wait(dve, hl_ready, UNITS * e + FT * c + f - 1)
                vec.tensor_tensor(prod[f % 2][:, 0:size(c)], sg[f % 2][:, 0:size(c)], ps_u[f % 2][:, 0:size(c)],
                                  ALU.mult).then_inc(prod_ready, 1)

            def low(back, e, c, f):
                wait(dve, hh_ready, UNITS * (e - back) + FT * c + f + 1)
                vec.tensor_tensor(hidl[c % 2][:, f, 0:size(c)], prod[f % 2][:, 0:size(c)],
                                  hidh[c % 2][:, f, 0:size(c)].bitcast(F32), ALU.subtract).then_inc(hl_ready, 1)

            def scaled(e, u, t):
                n = rows_of(t)
                if t == 0:
                    wait(dve, score_ready, e + 1)
                    if not isinstance(e, int) or e >= 1:
                        wait(dve, scattered[1 - u], (e - (1 - u) + 1) * (16 * GT // 2))
                wait(dve, ylow_ready, GT * e + t + 1)
                vec.scalar_tensor_tensor(y[0:n, t, :], ps_d[(u + t) % 2][0:n, 0:D], score[u][0:n, t:t + 1],
                                         y_low[(u + t) % 2][0:n, :], ALU.mult, ALU.add).then_inc(y_ready, 1)

            copy_g(0, 0)
            copy_g(1, 1)
            for f in range(FT):
                high_gu(0, f, 0)
            dve.wait_ge(cst, 4)
            copy_score(0, 0)
            for t in range(GT):
                low_x(0, 0, t)

            def expert(e, u, more, more2):
                for kind, c, t in order():
                    if kind == "gu":
                        n = UNITS * e + FT * c + t
                        if c == 0 and t == 0 and not (isinstance(e, int) and e == 0):
                            high_gu(e, FT - 1, n)
                        if c == CHN - 1 and t >= 1 and more:
                            high_gu(e + 1, t - 1, n)
                        product(e, c, t)
                        if not is_first(e, c, t):
                            back, pc, pf = before(c, t)
                            low(back, e, pc, pf)
                        if (c, t) == (0, 4):
                            if more2:
                                copy_g(e + 2, u)
                            if not isinstance(e, int) or e >= 2:
                                wait_apart(dve, scattered[u], (e - u) * (16 * GT // 2))
                            vec.tensor_copy(idx_s[u][:], idx_all[:, bass.ds(e * GT, GT)]).then_inc(idxs_ready, 1)
                    elif kind == "dn" and c == 0:
                        scaled(e, u, t)
                    elif kind == "dn" and not (isinstance(e, int) and e == 0):
                        scaled(e - 1, 1 - u, t)
                    elif kind == "tr" and more:
                        if t == 0:
                            copy_score(e + 1, 1 - u)
                        low_x(e + 1, 1 - u, t)

            experts(dve, expert)
            low(1, E, CHN - 1, FT - 1)
            for t in range(TAIL, GT):
                scaled(E - 1, (E - 1) % 2, t)

        @block.tensor
        def _(pe):
            mm = nc.tensor.matmul
            pe.wait_ge(cst, 4)

            def transposes(e, u, t):
                if t == 0:
                    wait(pe, gathered[u], (e - u) * (16 * GT // 2) + 16 * GT)
                (wait if t < GT - 1 else wait_apart)(pe, xl_ready, GT * e + t - 1)
                n = rows_of(t)
                for k, c0 in enumerate((0, P, W64)):
                    last = nc.tensor.transpose(ps_t[(u + t) % 2][:, k * P:k * P + n], xg[u][0:n, t, c0:c0 + P],
                                               ident[0:n, 0:n])
                last.then_inc(tr_ps, 1)

            def down(e, u, t):
                c = min(t // CT, CHN - 1)
                wait(pe, hl_ready, UNITS * e + FT * (c + 1))
                if t == 0:
                    wait(pe, dl_ready, e + 1)
                wait(pe, y_ready, GT * e + t - 1)
                n = rows_of(t)
                cols = slice(t * P - FIRST[c], t * P - FIRST[c] + n)
                bank = ps_d[(u + t) % 2]
                for k in range(FT):
                    mm(bank[0:n, 0:2 * D], hidh[c % 2][:, k, cols], w_d[u][:, k].rearrange("p h n -> p (h n)"),
                       start=k == 0, stop=False)
                    last = mm(bank[0:n, 0:D], hidl[c % 2][:, k, cols], w_d[u][:, k, 0, :],
                              start=False, stop=k == FT - 1)
                last.then_inc(dn_ps, 1)

            for t in range(GT):
                transposes(0, 0, t)

            def expert(e, u, more, more2):
                for kind, c, t in order():
                    if kind == "gu":
                        n = UNITS * e + FT * c + t
                        if c == 0 and t == 0:
                            wait(pe, xl_ready, GT * (e + 1))
                        if c == 0:
                            wait(pe, wl_ready, FT * e + t + 1)
                        wait(pe, prod_ready, n - 1)
                        for m, bank in ((0, ps_g), (1, ps_u)):
                            for wt, xt in PASSES:
                                last = mm(bank[t % 2][:, 0:size(c)], w_gu[:, m, wt, t * P:(t + 1) * P],
                                          xT[u][:, xt, FIRST[c]:FIRST[c + 1]], start=wt == 0, stop=wt == WT - 1)
                        last.then_inc(gu_ps, 1)
                    elif kind == "dn" and c == 0:
                        down(e, u, t)
                    elif kind == "dn" and not (isinstance(e, int) and e == 0):
                        down(e - 1, 1 - u, t)
                    elif kind == "tr" and more:
                        transposes(e + 1, 1 - u, t)

            experts(pe, expert)
            for t in range(TAIL, GT):
                down(E - 1, (E - 1) % 2, t)


SCRATCH = {"h2": (N, D), "tab": (N, ROW), "x2T": (D, N), "sT": (E, NPAD), "thr": (E, 1)}


def program(nc, dram):
    stage_a(nc, dram)
    with nc.sbuf_tensor("idx_all", [P, E * GT], I32) as idx_all:
        stage_s(nc, dram, idx_all)
        stage_e(nc, dram, idx_all)


def layouts(i):
    import numpy as np

    def stacked(w):
        return np.stack([w[..., 0:P, :], np.concatenate([w[..., P:D, :], w[..., 0:D - P, :]], -2),
                         w[..., D - P:D, :]], -2)

    x = np.asarray(i["x"]).reshape(IMAGES, GRID, PATCH, GRID, PATCH, 3).transpose(0, 2, 4, 5, 1, 3)
    patches = np.zeros((IMAGES, KC * P, TOK), x.dtype)
    patches[:, :, 1:] = x.reshape(IMAGES, DPATCH, GRID * GRID)
    a = {k: np.asarray(v) for k, v in i.items()}
    return {
        "patches": patches.reshape(IMAGES, KC, P, TOK).transpose(0, 2, 1, 3),
        "tok_W": a["L0_tok_W"], "tok_b": a["L0_tok_b"], "cls": a["L0_tok_class_token"],
        "pos": a["L0_tok_pos_emb"], "Wqkv": a["L0_attn_Wqkv"], "bqkv": a["L0_attn_bqkv"],
        "Wout": a["L0_attn_Wout"], "bout": a["L0_attn_bout"], "gateT": a["L0_ffn_gate_weight"].T,
        "WguT": np.stack([stacked(a["L0_ffn_Wg"].transpose(0, 2, 1)), stacked(a["L0_ffn_Wu"].transpose(0, 2, 1))], 2),
        "WdT": a["L0_ffn_Wd"].reshape(E, D, FT, P).transpose(0, 3, 2, 1),
        "WsgT": stacked(a["L0_ffn_Ws_g"].T), "WsuT": stacked(a["L0_ffn_Ws_u"].T),
        "WsdT": a["L0_ffn_Ws_d"].reshape(D, FS, P).transpose(2, 1, 0),
    }


def kernel(**inputs):
    import numpy as np
    import concourse.bacc as bacc
    from concourse.bass_utils import run_bass_kernel_spmd

    nc = bacc.Bacc("TRN2", target_bir_lowering=False, num_devices=1)
    arrays, dram = {}, {}
    for name, a in layouts(inputs).items():
        arrays[f"in_{name}"] = np.ascontiguousarray(a)
        dram[name] = nc.dram_tensor(f"in_{name}", a.shape, mybir.dt.from_np(a.dtype), kind="ExternalInput").ap()
    for name, shape in SCRATCH.items():
        dram[name] = nc.dram_tensor(f"scratch_{name}", shape, F32, kind="Internal").ap()
    dram["out"] = nc.dram_tensor("out", (N, D), F32, kind="ExternalOutput").ap()
    program(nc, dram)
    got = run_bass_kernel_spmd(nc, [arrays], core_ids=[0]).results[0]["out"]
    return got.reshape(IMAGES, TOK, D)
```

```python
from contextlib import ExitStack

import concourse.bass as bass
from concourse import mybir

ALU = mybir.AluOpType
ACT = mybir.ActivationFunctionType
AX = mybir.AxisListType
F32 = mybir.dt.float32
F32R = mybir.dt.float32r
BF16 = mybir.dt.bfloat16
F16 = mybir.dt.float16
I32 = mybir.dt.int32

P = 128
IMAGES = 64
PATCH = 16
GRID = 14
TOK = GRID * GRID + 1
T1 = TOK - P
TILES = ((0, P), (P, T1))
D = 192
KH = D // 2
DPATCH = PATCH * PATCH * 3
KC = DPATCH // P
HEADS = 12
HH = HEADS // 2
PAIRS = HEADS // 2
PP = 3
TP = TOK + 1
DH = D // HEADS
VW = KH + HH
EPS = 1e-5
N = IMAGES * TOK
E = 16
CAP = (N * 2 + E - 1) // E
NBLK = (N + P - 1) // P
NPAD = NBLK * P
CHUNKS = 8
F_EXP = 4 * D
FT = F_EXP // P
F_SH = F_EXP // 2
FS = F_SH // P
SC0 = D + 64
ROW = SC0 + E
BIG = -1.0e30
ST_N = 2 * TOK
assert CAP * CHUNKS == N and CAP == 4 * ST_N


def wait(eng, sem, value):
    if isinstance(value, int) and value <= 0:
        return
    eng.wait_ge(sem, value)


class SharedWeights:

    def __init__(self, nc, ctx):
        def sb(name, shape, dt=F32):
            return ctx.enter_context(nc.sbuf_tensor(name, shape, dt))

        self.raw = sb("w_raw", [P, 2, XT, F_SH])
        self.gu = sb("w_gu", [P, 2, WT, F_SH], F32R)
        self.d_raw = sb("wd_raw", [P, FS, D])
        self.d = sb("w_d", [P, FS, 2, D], F32R)
        self.loaded = ctx.enter_context(nc.semaphore("w_loaded"))
        self.high = ctx.enter_context(nc.semaphore("w_high"))
        self.gu_low = ctx.enter_context(nc.semaphore("w_low"))
        self.d_low = ctx.enter_context(nc.semaphore("wd_low"))


def stage_a(nc, dram, ws):
    ctx = ExitStack()
    with ctx:
        def sb(name, shape, dt=F32):
            return ctx.enter_context(nc.sbuf_tensor(name, shape, dt))

        def sem(name):
            return ctx.enter_context(nc.semaphore(name))

        w_tok = sb("w_tok", [P, KC, D])
        w_qkv = sb("w_qkv", [KH, 2, 3 * D])
        w_out = sb("w_out", [KH, 2, D])
        w_gate = sb("w_gate", [KH, 2, E])
        bq = sb("bq", [KH, 2])
        bk = sb("bk", [KH, 2])
        bv = sb("bv", [P, D])
        bout = sb("bout", [P, D])
        pos = sb("pos", [P, 2, D])
        tokb = sb("tokb", [P, 2, D])
        ident = sb("ident", [P, P])
        ident_bf = sb("ident_bf", [P, P], BF16)
        mask0 = sb("mask0", [P, 2, P], BF16)
        sel_sum = sb("sel_sum", [VW, KH])
        minus_half = sb("minus_half", [P, 2])
        of_head = sb("of_head", [KH, HH])
        head_mask = sb("head_mask", [KH, 2])
        pad_scores = sb("pad_scores", [E, NPAD - N])

        patches = [sb(f"patches{u}", [P, KC, TOK]) for u in range(2)]
        h = [sb(f"h{u}", [P, 2, D]) for u in range(2)]
        h_res = [sb(f"h_res{u}", [P, 2, D]) for u in range(2)]
        stats1 = sb("stats1", [P, 2, 6])
        mv1 = sb("mv1", [P, 2, 2])
        var1 = sb("var1", [P, 2])
        rstd1 = sb("rstd1", [P, 2])
        xn = sb("xn", [P, 2, D])
        xnT = [sb(f"xnT{u}", [KH, 2, TOK]) for u in range(2)]
        q_h = [sb(f"q_h{u}", [KH, 2, TOK], F32R) for u in range(2)]
        q_l = [sb(f"q_l{u}", [KH, 2, TOK], F32R) for u in range(2)]
        k_h = [sb(f"k_h{u}", [KH, 2, TOK], F32R) for u in range(2)]
        k_l = [sb(f"k_l{u}", [KH, 2, TOK], F32R) for u in range(2)]
        k_rows = [sb(f"k_rows{u}", [KH + 1, 2, PP, TP], F32R) for u in range(2)]
        q_rows = [sb(f"q_rows{u}", [KH + 1, 2, PP, 2, TP], F32R) for u in range(2)]
        vz = [sb(f"vz{u}", [P, 2, HEADS, VW]) for u in range(2)]
        mx = sb("mx", [P, 2, HEADS])
        mT = [sb(f"mT{u}", [HEADS, TOK], F32R) for u in range(2)]
        pt0 = [sb(f"pt0_{u}", [P, HEADS, TOK]) for u in range(2)]
        pt1 = [sb(f"pt1_{u}", [P, HEADS, T1]) for u in range(2)]
        o_raw = [sb(f"o_raw{u}", [VW, 2, TOK]) for u in range(2)]
        rec = sb("rec", [VW, 2, TOK])
        oT = [sb(f"oT{u}", [KH, 2, TOK]) for u in range(2)]
        h2 = [sb(f"h2_{u}", [P, 2, D]) for u in range(2)]
        stats2 = sb("stats2", [P, 2, 6])
        mv2 = sb("mv2", [P, 2, 2])
        var2 = sb("var2", [P, 2])
        rstd2 = sb("rstd2", [P, 2])
        tab = [sb(f"tab{u}", [P, 2, ROW]) for u in range(2)]
        x2T = [sb(f"x2T{u}", [KH, 2, TOK]) for u in range(2)]
        ex = sb("ex", [E, TOK])
        ex1 = sb("ex1", [E, TOK])
        sT = [sb(f"sT{u}", [E, TOK]) for u in range(2)]

        ps_max = [ctx.enter_context(nc.psum_tensor(f"ps_max{i}", [P, 512], F32)) for i in range(3)]
        ps_st = [ctx.enter_context(nc.psum_tensor(f"ps_st{i}", [P, 512], F32)) for i in range(2)]
        ps5 = ctx.enter_context(nc.psum_tensor("ps5", [P, 512], F32))
        ps6 = ctx.enter_context(nc.psum_tensor("ps6", [P, 512], F32))
        ps7 = ctx.enter_context(nc.psum_tensor("ps7", [P, 512], F32))

        pv_banks = (ps_max[1], ps_st[0])
        st_banks = (ps_st[0], ps_st[1], ps_max[2])

        const_ld = sem("const_ld")
        const_pool = sem("const_pool")
        const_dve = sem("const_dve")
        pad_out = sem("pad_out")
        cls_ld = sem("cls_ld")
        passed = sem("passed")
        pat_ld = [sem(f"pat_ld{u}") for u in range(2)]
        tok_ps = sem("tok_ps")
        h_ready = sem("h_ready")
        st1 = sem("st1")
        mv1_s = sem("mv1_s")
        var1_s = sem("var1_s")
        rstd1_s = sem("rstd1_s")
        xn_ready = sem("xn_ready")
        xnT_ps = sem("xnT_ps")
        xnT_ready = sem("xnT_ready")
        q_ps = sem("q_ps")
        q_ready = sem("q_ready")
        ql_ready = sem("ql_ready")
        kl_ready = sem("kl_ready")
        qrows_ready = sem("qrows_ready")
        krows_ready = sem("krows_ready")
        rows_ld = [sem(f"rows_ld{u}") for u in range(2)]
        k_ps = sem("k_ps")
        k_ready = sem("k_ready")
        v_ps = sem("v_ps")
        v_ready = sem("v_ready")
        hres_ready = sem("hres_ready")
        mx_ps = sem("mx_ps")
        mx_red = sem("mx_red")
        mT_ps = sem("mT_ps")
        mT_ready = sem("mT_ready")
        mrow_ld = [sem(f"mrow_ld{u}") for u in range(2)]
        st_ps = sem("st_ps")
        exp_done = sem("exp_done")
        sel_done = sem("sel_done")
        pv_ps = sem("pv_ps")
        pv_used = sem("pv_used")
        rec_ready = sem("rec_ready")
        bc_ps = sem("bc_ps")
        oT_ready = sem("oT_ready")
        wo_ps = sem("wo_ps")
        h2_ready = sem("h2_ready")
        st2 = sem("st2")
        mv2_s = sem("mv2_s")
        var2_s = sem("var2_s")
        rstd2_s = sem("rstd2_s")
        xn2_ready = sem("xn2_ready")
        x2T_ps = sem("x2T_ps")
        x2T_ready = sem("x2T_ready")
        lg_ps = sem("lg_ps")
        lg_used = sem("lg_used")
        ex1_s = sem("ex1_s")
        tab_x = sem("tab_x")
        sc_ready = sem("sc_ready")
        sT_ps = sem("sT_ps")
        sT_ready = sem("sT_ready")
        h2_out = [sem(f"h2_out{u}") for u in range(2)]
        x2T_out = [sem(f"x2T_out{u}") for u in range(2)]
        tab_out = [sem(f"tab_out{u}") for u in range(2)]
        sT_out = [sem(f"sT_out{u}") for u in range(2)]

        CONST_LOADS = 12
        CONST_POOL = 23
        CONST_EARLY = 7
        ROWS = 11
        UN = 9
        MX = 2 * PAIRS
        EMBED = (0, 2, 4, 6, 8, 10, 12)

        def slots(eng, slot, before_last=None):
            def parts(s):
                return dict(a=s + 1 < IMAGES, b=0 <= s < IMAGES, c=s >= 1)
            for s in range(-1, 3):
                slot(s, s % 2, **parts(s))
            with eng.Fori(0, (IMAGES - 6) // 2) as it:
                for u in range(2):
                    slot(it * 2 + (3 + u), (3 + u) % 2, a=True, b=True, c=True)
            for s in range(IMAGES - 3, IMAGES + 1):
                if s == IMAGES and before_last is not None:
                    before_last()
                slot(s, s % 2, **parts(s))

        def wait_apart(eng, s, value):
            wait(eng, s, value)
            if not isinstance(value, int):
                eng.sem_inc(passed, 1)

        block = ctx.enter_context(nc.Block())

        @block.sync
        def _(sp):
            for u in range(2):
                sp.dma_start(patches[u][:], dram["patches"][u]).then_inc(pat_ld[u], 16)
            for dst, src in ((w_tok[:], dram["tok_W"].rearrange("(c p) n -> p c n", p=P)),
                             (w_qkv[:], dram["Wqkv"].rearrange("(c p) n -> p c n", p=KH)),
                             (w_out[:], dram["Wout"].rearrange("(c p) n -> p c n", p=KH)),
                             (w_gate[:], dram["gateT"].rearrange("(c p) n -> p c n", p=KH)),
                             (bv[:], dram["bqkv"][None, 2 * D:3 * D].to_broadcast([P, D])),
                             (bout[:], dram["bout"][None, :].to_broadcast([P, D])),
                             (pos[:, 0, :], dram["pos"][0:P, :]),
                             (pos[0:T1, 1, :], dram["pos"][P:TOK, :]),
                             (tokb[:, 0, :], dram["tok_b"][None, :].to_broadcast([P, D])),
                             (tokb[:, 1, :], dram["tok_b"][None, :].to_broadcast([P, D]))):
                sp.dma_start(dst, src).then_inc(const_ld, 16)
            with nc.allow_non_contiguous_dma(reason="two short bias columns"):
                sp.dma_start(bq[:], dram["bqkv"][0:D].rearrange("(c p) -> p c", p=KH)).then_inc(const_ld, 16)
                sp.dma_start(bk[:], dram["bqkv"][D:2 * D].rearrange("(c p) -> p c", p=KH)).then_inc(const_ld, 16)
            sp.wait_ge(const_ld, 16 * CONST_LOADS)
            sp.dma_start(tokb[0:1, 0, :], dram["cls"][None, :]).then_inc(cls_ld, 16)
            sp.wait_ge(const_pool, CONST_POOL)
            sp.dma_start(dram["sT"][:, N:NPAD], pad_scores[:]).then_inc(pad_out, 16)
            for dst, src in ((ws.raw[:, 0], "WsgT"), (ws.raw[:, 1], "WsuT"), (ws.d_raw[:], "WsdT")):
                sp.dma_start(dst, dram[src]).then_inc(ws.loaded, 16)

            def slot(s, u, a, b, c):
                v = 1 - u
                if b and not (isinstance(s, int) and s + 2 >= IMAGES):
                    wait_apart(sp, tok_ps, s + 1)
                    sp.dma_start(patches[u][:], dram["patches"][s + 2]).then_inc(pat_ld[u], 16)
                if b:
                    wait(sp, mT_ready, s + 1)
                    sp.dma_start(q_rows[u][KH:KH + 1, :, :, :, 0:TOK].rearrange("p a j h t -> p (a j h) t").bitcast(F32),
                                 mT[u][:, :].bitcast(F32)).then_inc(mrow_ld[u], 16)
                base = (s - 1) * TOK
                if c:
                    wait_apart(sp, h2_ready, s)
                    sp.dma_start(dram["h2"][bass.ds(base, P), :], h2[v][:, 0, :]).then_inc(h2_out[v], 16)
                    sp.dma_start(dram["h2"][bass.ds(base + P, T1), :], h2[v][0:T1, 1, :]).then_inc(h2_out[v], 16)
                if a:
                    wait_apart(sp, st_ps, UN * s)
                    wait_apart(sp, ql_ready, s + 2)
                    for j in range(PP):
                        for head in range(2):
                            src_rows = slice(32 * j + DH * head, 32 * j + DH * (head + 1))
                            dst_rows = slice(32 + DH * head, 32 + DH * (head + 1))
                            sp.dma_start(q_rows[v][dst_rows, :, j, head, 0:TOK].bitcast(F32),
                                         q_l[v][src_rows, :, :].bitcast(F32)).then_inc(rows_ld[v], 16)
                    wait_apart(sp, kl_ready, s + 2)
                    for j in range(PP):
                        sp.dma_start(k_rows[v][64:96, :, j, 0:TOK].bitcast(F32),
                                     k_l[v][32 * j:32 * (j + 1), :, :].bitcast(F32)).then_inc(rows_ld[v], 16)
                    wait_apart(sp, krows_ready, s + 2)
                    sp.dma_start(k_rows[v][32:64].bitcast(F32), k_rows[v][0:32].bitcast(F32)).then_inc(rows_ld[v], 16)
                if c:
                    wait_apart(sp, x2T_ready, s)
                    sp.dma_start(dram["x2T"].rearrange("(k p) n -> p k n", p=KH)[:, :, bass.ds(base, TOK)], x2T[v][:])\
                        .then_inc(x2T_out[v], 16)
                if a:
                    wait_apart(sp, qrows_ready, s + 2)
                    sp.dma_start(q_rows[v][64:96].bitcast(F32), q_rows[v][0:32].bitcast(F32)).then_inc(rows_ld[v], 16)
                if c:
                    wait_apart(sp, sT_ready, s)
                    sp.dma_start(dram["sT"][:, bass.ds(base, TOK)], sT[v][:]).then_inc(sT_out[v], 16)
                    wait_apart(sp, tab_x, s)
                    wait_apart(sp, sc_ready, s)
                    sp.dma_start(dram["tab"][bass.ds(base, P), :], tab[v][:, 0, :]).then_inc(tab_out[v], 16)
                    sp.dma_start(dram["tab"][bass.ds(base + P, T1), :], tab[v][0:T1, 1, :]).then_inc(tab_out[v], 16)

            slots(sp, slot)
            sp.wait_ge(pad_out, 16)
            for u in range(2):
                sp.wait_ge(h2_out[u], 32 * IMAGES // 2)
                sp.wait_ge(x2T_out[u], 16 * IMAGES // 2)
                sp.wait_ge(tab_out[u], 32 * IMAGES // 2)
                sp.wait_ge(sT_out[u], 16 * IMAGES // 2)

        @block.gpsimd
        def _(pool):
            made = [0]

            def made_one(ins):
                made[0] += 1
                ins.then_inc(const_pool, 1)
                pool.wait_ge(const_pool, made[0])

            for t, val in ((ident, 0.0), (minus_half, -0.5), (mv1, 0.0), (of_head, 1.0)):
                made_one(pool.memset(t[:], val))
            made_one(pool.affine_select(out=ident[:], in_=ident[:], compare_op=ALU.not_equal, fill=1.0, base=0,
                                        pattern=[[-1, P]], channel_multiplier=1))
            made_one(pool.affine_select(out=of_head[:], in_=of_head[:], compare_op=ALU.is_ge, fill=0.0, base=0,
                                        pattern=[[-DH, HH]], channel_multiplier=1))
            made_one(pool.affine_select(out=of_head[:], in_=of_head[:], compare_op=ALU.is_ge, fill=0.0,
                                        base=DH - 1, pattern=[[DH, HH]], channel_multiplier=-1))
            assert made[0] == CONST_EARLY
            for t, val in ((sel_sum, 0.0), (mask0, 0.0), (pad_scores, -1.0), (mv2, 0.0), (rec, 0.0),
                           (vz[0], 0.0), (vz[1], 0.0)):
                made_one(pool.memset(t[:], val))
            for u in range(2):
                made_one(pool.memset(q_rows[u][:].bitcast(F32), 0.0))
                made_one(pool.memset(k_rows[u][:].bitcast(F32), 1.0))
            made_one(pool.affine_select(out=sel_sum[:].rearrange("p (j d) -> p j d", j=HH),
                                        in_=sel_sum[:].rearrange("p (j d) -> p j d", j=HH),
                                        compare_op=ALU.not_equal, fill=1.0, base=-KH,
                                        pattern=[[-1, HH], [0, DH]], channel_multiplier=1))
            made_one(pool.affine_select(out=mask0[:], in_=mask0[:], compare_op=ALU.is_ge, fill=BIG, base=0,
                                        pattern=[[0, 2], [-1, P]], channel_multiplier=1))
            for u in range(2):
                ones = vz[u][:, :, :, KH:VW].rearrange("p t (a j) c -> p (t a) j c", a=2)
                made_one(pool.affine_select(out=ones, in_=ones, compare_op=ALU.not_equal, fill=1.0, base=0,
                                            pattern=[[0, 4], [1, HH], [-1, HH]], channel_multiplier=0))
            made_one(pool.tensor_copy(ident_bf[:], ident[:]))
            assert made[0] == CONST_POOL, made[0]
            pool.wait_ge(const_ld, 16 * CONST_LOADS)

            def slot(s, u, a, b, c):
                v = 1 - u
                if a:
                    wait(pool, var1_s, s + 2)
                    pool.tensor_tensor(rstd1[:], var1[:], minus_half[:], ALU.pow).then_inc(rstd1_s, 1)
                if b:
                    wait(pool, h_ready, s + 1)
                    wait(pool, h2_ready, s - 1)
                    pool.tensor_tensor(h_res[u][:, 0, :], h[u][:, 0, :], bout[:], ALU.add)
                    pool.tensor_tensor(h_res[u][0:T1, 1, :], h[u][0:T1, 1, :], bout[0:T1, :], ALU.add)\
                        .then_inc(hres_ready, 1)
                if c:
                    wait(pool, var2_s, s)
                    pool.tensor_tensor(rstd2[:], var2[:], minus_half[:], ALU.pow).then_inc(rstd2_s, 1)
                if b:
                    for unit in range(UN):
                        g, part = divmod(unit, 3)
                        wait_apart(pool, exp_done, UN * s + unit + 1)
                        if part < 2:
                            hd = 4 * g + 2 * part
                            x = pt0[u][:, hd:hd + 2, 0:P]
                            n, w = 2, P
                        else:
                            x = pt1[u][0:T1, 4 * g:4 * g + 4, :]
                            n, w = 4, T1
                        pool.affine_select(out=x, in_=x, compare_op=ALU.is_ge, fill=0.0, base=0,
                                           pattern=[[0, n], [1, w]], channel_multiplier=-1).then_inc(sel_done, 1)

            slots(pool, slot)
            pool.wait_ge(ws.high, 2)
            pool.tensor_tensor(ws.d[:, :, 1, :], ws.d_raw[:], ws.d[:, :, 0, :].bitcast(F32), ALU.subtract)\
                .then_inc(ws.d_low, 1)

        @block.scalar
        def _(act):
            act.wait_ge(const_ld, 16 * CONST_LOADS)
            def slot(s, u, a, b, c):
                v = 1 - u
                def exps(g):
                    if g == 0:
                        wait(act, pv_ps, 2 * (s - 1))
                    for part in range(3):
                        unit = 3 * g + part
                        bank = st_banks[part]
                        wait(act, st_ps, UN * s + unit + 1)
                        if part < 2:
                            hd = 4 * g + 2 * part
                            act.activation(pt0[u][:, hd:hd + 2, :],
                                           bank[:, 0:2 * TP].rearrange("p (j t) -> p j t", j=2)[:, :, 0:TOK], ACT.Exp,
                                           scale=DH ** -0.5).then_inc(exp_done, 1)
                        else:
                            act.activation(pt1[u][0:T1, 4 * g:4 * g + 4, :],
                                           bank[0:T1, :].rearrange("p (j t) -> p j t", j=4)[:, :, P - 1 - T1:P - 1],
                                           ACT.Exp, scale=DH ** -0.5).then_inc(exp_done, 1)

                if a:
                    wait(act, xnT_ps, s + 2)
                    wait(act, v_ps, s)
                    act.activation(xnT[v][:], ps7[0:KH, 0:ST_N].rearrange("p (a t) -> p a t", a=2), ACT.Copy)\
                        .then_inc(xnT_ready, 1)
                if b:
                    wait(act, mT_ps, s + 1)
                    if not isinstance(s, int) or s >= 2:
                        wait(act, mrow_ld[u], (s - u) * 8)
                    act.activation(mT[u][:], ps_max[0][0:HEADS, 0:TOK], ACT.Copy, scale=-1.0).then_inc(mT_ready, 1)
                if a:
                    wait(act, q_ps, s + 2)
                    if not isinstance(s, int) or s >= 1:
                        wait(act, rows_ld[v], (s + 1 - v) * (16 * ROWS // 2))
                    for half in range(2):
                        last = act.activation(q_h[v][:, half, :], ps6[0:KH, half * TOK:(half + 1) * TOK],
                                              ACT.Identity, bias=bq[:, half:half + 1])
                    last.then_inc(q_ready, 1)
                    wait(act, k_ps, s + 2)
                    for half in range(2):
                        last = act.activation(k_h[v][:, half, :], ps7[0:KH, half * TOK:(half + 1) * TOK],
                                              ACT.Identity, bias=bk[:, half:half + 1])
                    last.then_inc(k_ready, 1)
                if b:
                    exps(0)
                    exps(1)
                if c:
                    wait(act, x2T_ps, s)
                    if not isinstance(s, int) or s >= 3:
                        wait(act, x2T_out[v], (s - 1 - v) * 8)
                    act.activation(x2T[v][:], ps7[0:KH, 0:ST_N].rearrange("p (a t) -> p a t", a=2), ACT.Copy)\
                        .then_inc(x2T_ready, 1)
                if a:
                    if isinstance(s, int) and s == -1:
                        act.wait_ge(const_pool, CONST_POOL)
                    wait(act, k_ready, s + 2)
                    for j in range(PP):
                        last = act.activation(k_rows[v][0:32, :, j, 0:TOK], k_h[v][32 * j:32 * (j + 1)].bitcast(F32),
                                              ACT.Copy)
                    last.then_inc(krows_ready, 1)
                if b:
                    exps(2)

                def raw(half):
                    wait(act, pv_ps, 2 * s + half + 1)
                    if half == 0:
                        wait(act, oT_ready, s - 1)
                    act.activation(o_raw[u][:, half, :], pv_banks[half][0:VW, 0:TOK], ACT.Copy)\
                        .then_inc(pv_used, 1)
                if b:
                    raw(0)
                if c:
                    wait(act, lg_ps, s)
                    wait(act, ex1_s, s - 1)
                    act.activation(ex[:], ps5[0:E, 0:TOK], ACT.Exp, scale=-1.0).then_inc(lg_used, 1)
                if b:
                    raw(1)
                if c:
                    wait(act, sT_ps, s)
                    if not isinstance(s, int) or s >= 3:
                        wait(act, tab_out[v], (s - 1 - v) * 16)
                    for t, (_, n) in enumerate(TILES):
                        last = act.activation(tab[v][0:n, t, SC0:ROW], ps6[0:n, t * E:(t + 1) * E], ACT.Copy)
                    last.then_inc(sc_ready, 1)

            def split_weights():
                act.wait_ge(ws.loaded, 48)
                act.activation(ws.gu[:, :, 0:XT, :], ws.raw[:], ACT.Copy).then_inc(ws.high, 1)
                act.activation(ws.d[:, :, 0, :], ws.d_raw[:], ACT.Copy).then_inc(ws.high, 1)

            slots(act, slot, split_weights)

        @block.vector
        def _(dve):
            vec = nc.vector
            dve.wait_ge(const_ld, 16 * CONST_LOADS)
            dve.wait_ge(cls_ld, 16)
            dve.wait_ge(const_pool, CONST_EARLY)
            vec.tensor_tensor(pos[:, 0, :], pos[:, 0, :], tokb[:, 0, :], ALU.add).then_inc(const_dve, 1)
            vec.tensor_tensor(pos[0:T1, 1, :], pos[0:T1, 1, :], tokb[0:T1, 1, :], ALU.add).then_inc(const_dve, 1)
            vec.tensor_reduce(head_mask[:], of_head[:].rearrange("p (j h) -> p h j", h=2), AX.X, ALU.add)\
                .then_inc(const_dve, 1)
            dve.wait_ge(const_dve, 3)

            def stats(x, st, st_s):
                for t, (_, n) in enumerate(TILES):
                    last = vec.bn_stats(st[0:n, t, :], x[0:n, t, :])
                last.then_inc(st_s, 1)

            def moments(st, st_s, mv, mv_s, i):
                wait_apart(dve, st_s, i + 1)
                for t, (_, n) in enumerate(TILES):
                    last = vec.bn_aggr(mv[0:n, t, :], st[0:n, t, :])
                last.then_inc(mv_s, 1)

            def guarded(mv, mv_s, var, var_s, i):
                wait(dve, mv_s, i + 1)
                vec.tensor_scalar(var[:], mv[:, :, 1], EPS, None, ALU.add).then_inc(var_s, 1)

            def slot(s, u, a, b, c):
                v = 1 - u

                def reciprocals(half, i, w):
                    wait(dve, pv_used, 2 * i + half + 1)
                    if half == 0:
                        wait(dve, bc_ps, i)
                    last = vec.reciprocal(rec[KH:VW, half, :], o_raw[w][KH:VW, half, :])
                    if half == 1:
                        last.then_inc(rec_ready, 1)

                def maxima(lo, hi):
                    for m in range(lo, hi):
                        pair, t = divmod(m, 2)
                        n, keys = (P, P) if t == 0 else (T1, TOK)
                        wait(dve, mx_ps, MX * s + m + 1)
                        if m == 0:
                            wait(dve, mT_ps, s)
                        vec.tensor_reduce(mx[0:n, t, 2 * pair:2 * pair + 2],
                                          ps_max[m % 3][0:n, 0:2 * TP].rearrange("p (j t) -> p j t", j=2)[:, :, 0:keys],
                                          AX.X, ALU.max).then_inc(mx_red, 1)

                if c:
                    reciprocals(1, s - 1, v)
                if b:
                    maxima(0, 6)
                if a:
                    wait(dve, tok_ps, s + 2)
                    wait(dve, hres_ready, s)
                    for t, (_, n) in enumerate(TILES):
                        last = vec.scalar_tensor_tensor(h[v][0:n, t, :], ps5[0:n, t * D:(t + 1) * D], 1.0 / 255.0,
                                                 pos[0:n, t, :], ALU.mult, ALU.add)
                    last.then_inc(h_ready, 1)
                if a:
                    wait(dve, h_ready, s + 2)
                    wait(dve, xn_ready, s + 1)
                    stats(h[v], stats1, st1)
                if c:
                    wait(dve, bc_ps, s)
                    wait(dve, wo_ps, s - 2)
                    vec.tensor_tensor(oT[v][:], o_raw[v][0:KH, :, :],
                                      ps6[0:KH, 0:ST_N].rearrange("p (a t) -> p a t", a=2), ALU.mult)\
                        .then_inc(oT_ready, 1)
                if a:
                    moments(stats1, st1, mv1, mv1_s, s + 1)
                if b:
                    maxima(6, 7)
                if a:
                    guarded(mv1, mv1_s, var1, var1_s, s + 1)
                if b:
                    maxima(7, 9)
                if a:
                    wait(dve, rstd1_s, s + 2)
                    wait(dve, xnT_ps, s + 1)
                    for t, (_, n) in enumerate(TILES):
                        last = vec.tensor_scalar(xn[0:n, t, :], h[v][0:n, t, :], mv1[0:n, t, 0:1], rstd1[0:n, t:t + 1],
                                          ALU.subtract, ALU.mult)
                    last.then_inc(xn_ready, 1)
                if b:
                    maxima(9, MX)
                if c:
                    wait(dve, wo_ps, s)
                    if not isinstance(s, int) or s >= 3:
                        wait(dve, h2_out[v], (s - 1 - v) * 16)
                    wait(dve, hres_ready, s)
                    for t, (_, n) in enumerate(TILES):
                        last = vec.tensor_tensor(h2[v][0:n, t, :], ps5[0:n, t * D:(t + 1) * D], h_res[v][0:n, t, :],
                                          ALU.add)
                    last.then_inc(h2_ready, 1)
                    wait(dve, h2_ready, s)
                    wait(dve, xn2_ready, s - 1)
                    stats(h2[v], stats2, st2)
                    moments(stats2, st2, mv2, mv2_s, s - 1)
                    guarded(mv2, mv2_s, var2, var2_s, s - 1)

                def low_part(low_, high_, ps, bias, ready, done):
                    wait(dve, ready, s + 2)
                    for half in range(2):
                        last = vec.scalar_tensor_tensor(low_[v][:, half, :], ps[0:KH, half * TOK:(half + 1) * TOK],
                                                        bias[:, half:half + 1], high_[v][:, half, :].bitcast(F32),
                                                        ALU.add, ALU.subtract)
                    last.then_inc(done, 1)

                if a:
                    low_part(q_l, q_h, ps6, bq, q_ready, ql_ready)
                if c:
                    wait(dve, rstd2_s, s)
                    if not isinstance(s, int) or s >= 3:
                        wait(dve, tab_out[v], (s - 1 - v) * 16)
                    for t, (_, n) in enumerate(TILES):
                        last = vec.tensor_scalar(tab[v][0:n, t, 0:D], h2[v][0:n, t, :], mv2[0:n, t, 0:1],
                                          rstd2[0:n, t:t + 1], ALU.subtract, ALU.mult)
                    last.then_inc(xn2_ready, 1)
                if a:
                    low_part(k_l, k_h, ps7, bk, k_ready, kl_ready)
                    if isinstance(s, int) and s == -1:
                        dve.wait_ge(const_pool, CONST_POOL)
                    wait(dve, st_ps, UN * s)
                    for j in range(PP):
                        rows = slice(32 * j, 32 * (j + 1))
                        for head in range(2):
                            last = vec.tensor_scalar(q_rows[v][0:32, :, j, head, 0:TOK], q_h[v][rows].bitcast(F32),
                                                     head_mask[rows, head:head + 1], None, ALU.mult)
                    last.then_inc(qrows_ready, 1)
                    wait(dve, v_ps, s + 2)
                    wait(dve, pv_ps, 2 * s)
                    for t, (_, n) in enumerate(TILES):
                        for half in range(2):
                            dst = vz[v][0:n, t, half * HH:(half + 1) * HH, :].rearrange("p j c -> p (j c)")
                            dst = bass.AP(tensor=dst.tensor, offset=dst.offset,
                                          ap=[list(dst.ap[0]), [VW + DH, HH], [1, DH]])
                            col = t * D + half * KH
                            last = vec.tensor_tensor(dst, ps5[0:n, col:col + KH].rearrange("p (j d) -> p j d", j=HH),
                                                    bv[0:n, half * KH:(half + 1) * KH]
                                                    .rearrange("p (j d) -> p j d", j=HH), ALU.add)
                    last.then_inc(v_ready, 1)
                if c:
                    for t, (_, n) in enumerate(TILES):
                        last = vec.tensor_scalar(tab[v][0:n, t, D:SC0], h2[v][0:n, t, 0:SC0 - D], mv2[0:n, t, 0:1],
                                                 rstd2[0:n, t:t + 1], ALU.subtract, ALU.mult)
                    last.then_inc(tab_x, 1)
                    wait(dve, lg_used, s)
                    vec.tensor_scalar(ex1[:], ex[:], 1.0, None, ALU.add).then_inc(ex1_s, 1)
                    wait(dve, ex1_s, s)
                    if not isinstance(s, int) or s >= 3:
                        wait(dve, sT_out[v], (s - 1 - v) * 8)
                    wait(dve, sT_ps, s - 2)
                    vec.reciprocal(sT[v][:], ex1[:]).then_inc(sT_ready, 1)
                if b:
                    reciprocals(0, s, u)

            def split_weights():
                dve.wait_ge(ws.high, 1)
                vec.tensor_tensor(ws.gu[:, :, XT:WT, :], ws.raw[:, :, 0:2, :], ws.gu[:, :, 0:2, :].bitcast(F32),
                                  ALU.subtract).then_inc(ws.gu_low, 1)

            slots(dve, slot, split_weights)

        @block.tensor
        def _(pe):
            mm = nc.tensor.matmul
            pe.wait_ge(const_ld, 16 * CONST_LOADS)
            pe.wait_ge(const_pool, CONST_EARLY)

            def transposes(dst, src, n_of):
                for t, (t0, n) in enumerate(TILES):
                    for half in range(2):
                        last = nc.tensor.transpose(dst[0:KH, half * TOK + t0:half * TOK + t0 + n],
                                                   src[0:n, t, half * KH:(half + 1) * KH], ident[0:n, 0:n])
                return last

            def slot(s, u, a, b, c):
                v = 1 - u

                def embed(lo, hi):
                    for i in range(lo, hi):
                        t, k = divmod(i, KC)
                        t0, n = TILES[t]
                        if i == 0:
                            wait(pe, pat_ld[v], (s + 1 - v) * 8 + 16)
                            if isinstance(s, int) and s <= 1:
                                wait(pe, v_ready, s + 1)
                            else:
                                wait(pe, lg_used, s - 1)
                        last = mm(ps5[0:n, t * D:(t + 1) * D], patches[v][:, k, t0:t0 + n], w_tok[:, k, :],
                                  start=k == 0, stop=k == KC - 1)
                    if hi == 2 * KC:
                        last.then_inc(tok_ps, 1)

                def masked(m):
                    pair, t = divmod(m, 2)
                    half, j = divmod(pair, PP)
                    t0, n = TILES[t]
                    bank = ps_max[m % 3]
                    wait(pe, mx_red, MX * s + m - 2)
                    if m == 1:
                        wait(pe, pv_used, 2 * s - 1)
                    for head in range(2):
                        mm(bank[0:n, head * TP:(head + 1) * TP], q_rows[u][0:KH, half, j, head, t0:t0 + n],
                           k_rows[u][0:KH, half, j, :], start=head == 0, stop=False)
                    mm(bank[0:n, 0:2 * TP].rearrange("p (j t) -> p j t", j=2)[:, :, t0:t0 + n], ident_bf[0:n, 0:n],
                       mask0[0:n, :, 0:n], start=False, stop=True).then_inc(mx_ps, 1)

                def sums():
                    wait(pe, rec_ready, s)
                    if isinstance(s, int) and s == 1:
                        wait(pe, ql_ready, s + 1)
                    else:
                        wait(pe, sc_ready, s - 1)
                    mm(ps6[0:KH, 0:ST_N], sel_sum[:], rec[:].rearrange("p a t -> p (a t)"), start=True, stop=True)\
                        .then_inc(bc_ps, 1)

                def out_projection(t):
                    if t == 0:
                        wait(pe, oT_ready, s)
                        if a:
                            wait(pe, h_ready, s + 2)
                        else:
                            wait(pe, lg_used, s - 1)
                    t0, n = TILES[t]
                    for half in range(2):
                        last = mm(ps5[0:n, t * D:(t + 1) * D], oT[v][:, half, t0:t0 + n], w_out[:, half, :],
                                  start=half == 0, stop=half == 1)
                    if t == 1:
                        last.then_inc(wo_ps, 1)

                if isinstance(s, int) and s == 0:
                    pe.wait_ge(const_pool, CONST_POOL)
                if b:
                    wait(pe, rows_ld[u], (s - u) * (16 * ROWS // 2) + 16 * ROWS)
                    wait(pe, mT_ready, s)
                for m in range(MX):
                    if b:
                        masked(m)
                    if a and m < 6:
                        embed(EMBED[m], EMBED[m + 1])
                    if c and m == 6:
                        sums()
                    if c and m in (8, 10):
                        out_projection((m - 8) // 2)
                if a:
                    wait(pe, xn_ready, s + 2)
                    if isinstance(s, int) and s < 2:
                        wait(pe, kl_ready, s + 1)
                    else:
                        wait(pe, x2T_ready, s - 1)
                    transposes(ps7, xn, TILES).then_inc(xnT_ps, 1)
                if b:
                    wait(pe, mx_red, MX * (s + 1))
                    for t, (t0, n) in enumerate(TILES):
                        last = nc.tensor.transpose(ps_max[0][0:HEADS, t0:t0 + n], mx[0:n, t, :], ident[0:n, 0:n])
                    last.then_inc(mT_ps, 1)

                def project(which, bank, done):
                    for half in range(2):
                        for k in range(2):
                            col = which * D + half * KH
                            last = mm(bank[0:KH, half * TOK:(half + 1) * TOK], w_qkv[:, k, col:col + KH],
                                      xnT[v][:, k, :], start=k == 0, stop=k == 1)
                    last.then_inc(done, 1)

                def scores(g):
                    if g == 0:
                        wait(pe, mrow_ld[u], (s - u) * 8 + 16)
                        wait(pe, pv_used, 2 * s)
                    for part in range(3):
                        unit = 3 * g + part
                        bank = st_banks[part]
                        wait(pe, exp_done, UN * s + unit - 2)
                        if part < 2:
                            half, j = divmod(2 * g + part, PP)
                            last = mm(bank[:, 0:2 * TP], k_rows[u][:, half, j, 0:P], q_rows[u][:, half, j, :, :],
                                      start=True, stop=True)
                        else:
                            for i in range(2):
                                half, j = divmod(2 * g + i, PP)
                                last = mm(bank[0:T1, i * 2 * P:(i + 1) * 2 * P], k_rows[u][:, half, j, P:TOK],
                                          q_rows[u][:, half, j, :, TP - P:TP], start=i == 0, stop=i == 1)
                        last.then_inc(st_ps, 1)

                if a:
                    wait(pe, xnT_ready, s + 2)
                    if c:
                        wait(pe, oT_ready, s)
                    else:
                        wait(pe, ql_ready, s + 1)
                    project(0, ps6, q_ps)
                    project(1, ps7, k_ps)
                if b:
                    scores(0)
                if a:
                    if c:
                        wait(pe, h2_ready, s)
                    else:
                        wait(pe, h_ready, s + 2)
                    for t, (t0, n) in enumerate(TILES):
                        for k in range(2):
                            last = mm(ps5[0:n, t * D:(t + 1) * D], xnT[v][:, k, t0:t0 + n], w_qkv[:, k, 2 * D:3 * D],
                                      start=k == 0, stop=k == 1)
                    last.then_inc(v_ps, 1)
                if b:
                    scores(1)
                if c:
                    wait(pe, xn2_ready, s)
                    if a:
                        wait(pe, kl_ready, s + 2)
                    else:
                        wait(pe, x2T_ready, s - 1)
                    transposes(ps7, tab[v], TILES).then_inc(x2T_ps, 1)
                if b:
                    scores(2)
                def weighted(half):
                    bank = pv_banks[half]
                    for j in range(HH):
                        hd = half * HH + j
                        if hd == HH:
                            wait(pe, sel_done, UN * s + 7)
                        elif hd % 4 == 0:
                            wait(pe, sel_done, UN * s + 3 * (hd // 4 + 1))
                        mm(bank[0:VW, 0:TOK], vz[u][:, 0, hd, :], pt0[u][:, hd, :], start=j == 0, stop=False)
                        last = mm(bank[0:VW, P:TOK], vz[u][0:T1, 1, hd, :], pt1[u][0:T1, hd, :],
                                  start=False, stop=j == HH - 1)
                    last.then_inc(pv_ps, 1)

                if b:
                    wait(pe, v_ready, s + 1)
                    weighted(0)
                if c:
                    wait(pe, x2T_ready, s)
                    if a:
                        wait(pe, v_ready, s + 2)
                    else:
                        wait(pe, h2_ready, s)
                    for k in range(2):
                        last = mm(ps5[0:E, 0:TOK], w_gate[:, k, :], x2T[v][:, k, :], start=k == 0, stop=k == 1)
                    last.then_inc(lg_ps, 1)
                if b:
                    weighted(1)
                if c:
                    wait_apart(pe, sT_ready, s)
                    if a:
                        wait_apart(pe, ql_ready, s + 2)
                    else:
                        wait(pe, oT_ready, s)
                    for t, (t0, n) in enumerate(TILES):
                        last = nc.tensor.transpose(ps6[0:n, t * E:(t + 1) * E], sT[v][0:E, t0:t0 + n],
                                                   ident[0:E, 0:E])
                    last.then_inc(sT_ps, 1)

            slots(pe, slot)


CH = ST_N
SH_CHUNKS = N // CH
STEPS = 32
GT = (CAP + P - 1) // P
LAST = CAP - (GT - 1) * P
IDX_GROUPS = ((0, 3), (3, 6), (6, 9), (9, 12), (12, GT))
assert SH_CHUNKS == 2 * E and STEPS == 4 * (SH_CHUNKS // 4)


def rows_of(t):
    return P if t < GT - 1 else LAST


XT = 3
WT = 5
PASSES = ((0, 0), (1, 1), (2, 2), (3, 0), (4, 1))
W64 = D - P


def stage_s(nc, dram, idx_all, ws):
    ctx = ExitStack()
    with ctx:
        def sb(name, shape, dt=F32):
            return ctx.enter_context(nc.sbuf_tensor(name, shape, dt))

        def sem(name):
            return ctx.enter_context(nc.semaphore(name))

        w_gu, w_d = ws.gu, ws.d
        xr = [sb(f"xr{u}", [P, XT, CH]) for u in range(2)]
        xs = [sb(f"xs{u}", [P, XT, CH], F32R) for u in range(2)]
        hs = [sb(f"hs{u}", [P, 4, D]) for u in range(2)]
        sg = [sb(f"sg{u}", [P, CH]) for u in range(2)]
        prod = [sb(f"prod{u}", [P, CH]) for u in range(2)]
        hidh = [sb(f"hidh{u}", [P, FS, CH], F32R) for u in range(2)]
        hidl = [sb(f"hidl{u}", [P, FS, CH], F32R) for u in range(2)]
        os_ = [sb(f"os{u}", [P, 4, D]) for u in range(2)]

        s1 = sb("s1", [P, CAP])
        hits = sb("hits", [P, CAP], BF16)
        cnt = sb("cnt", [P, 1])
        thr = sb("thr", [P, 1], I32)
        cand = sb("cand", [P, 1], I32)
        inc = sb("inc", [P, 1], I32)
        bitf = sb("bitf", [P, 1])
        biti = sb("biti", [P, 1], I32)
        same_expert = sb("same_expert", [P, P])
        s2 = sb("s2", [NBLK, E, P])
        thr_b = sb("thr_b", [NBLK, E])
        mask = sb("mask", [NBLK, E * P])
        keep_run = sb("keep_run", [NBLK, E * P])
        g_run = sb("g_run", [NBLK, E * P])
        e_run = sb("e_run", [NBLK, E * P])
        tots = sb("tots", [NBLK, 2 * E])
        before = sb("before", [NBLK, 2 * E])
        need = sb("need", [NBLK, E])
        lo = sb("lo", [NBLK, E])
        hi = sb("hi", [NBLK, E])
        earlier = sb("earlier", [NBLK, NBLK])
        ones = sb("ones", [NBLK, NBLK])
        rank = sb("rank", [NBLK, E, P + 1], F16)
        slot_no = sb("slot_no", [NBLK, CAP], F16)
        ge = sb("ge", [NBLK, CAP], F16)
        onehot = sb("onehot", [NBLK, CAP], F16)
        jcol = sb("jcol", [P, GT])
        junk = sb("junk", [P, GT, P], BF16)
        bcol = sb("bcol", [P, GT])
        acol = sb("acol", [P, GT])

        ps_g = [ctx.enter_context(nc.psum_tensor(f"ps_g{i}", [P, 512], F32)) for i in range(2)]
        ps_u = [ctx.enter_context(nc.psum_tensor(f"ps_u{i}", [P, 512], F32)) for i in range(2)]
        ps_d = [ctx.enter_context(nc.psum_tensor(f"ps_d{i}", [P, 512], F32)) for i in range(2)]
        ps_i = [ctx.enter_context(nc.psum_tensor(f"ps_i{i}", [P, 512], F32)) for i in range(2)]

        wld = sem("wld")
        s_ld = sem("s_ld")
        cst = sem("cst")
        xs_ld = [sem(f"xs_ld{u}") for u in range(2)]
        hs_ld = [sem(f"hs_ld{u}") for u in range(2)]
        g_ps = sem("g_ps")
        sg_ready = sem("sg_ready")
        x1_ready = sem("x1_ready")
        xh_ready = sem("xh_ready")
        xl_ready = sem("xl_ready")
        prod_ready = sem("prod_ready")
        hh_ready = sem("hh_ready")
        hl_ready = sem("hl_ready")
        dn_ps = sem("dn_ps")
        os_ready = sem("os_ready")
        os_out = [sem(f"os_out{u}") for u in range(2)]
        thr_init = sem("thr_init")
        cand_s = sem("cand_s")
        cnt_s = sem("cnt_s")
        cnt_ps = sem("cnt_ps")
        inc_s = sem("inc_s")
        bit_s = sem("bit_s")
        bitf_s = sem("bitf_s")
        thr_s = sem("thr_s")
        thr_st = sem("thr_st")
        thr_ld = sem("thr_ld")
        rk = sem("rk")
        rk_ps = sem("rk_ps")
        oh_ge = sem("oh_ge")
        oh_s = sem("oh_s")
        ix_ps = sem("ix_ps")
        ix_used = sem("ix_used")
        list_s = sem("list_s")
        passed = sem("passed_s")
        CST = 12
        CST_EARLY = 6
        NG = len(IDX_GROUPS)

        def wait_apart(eng, s, value):
            wait(eng, s, value)
            if not isinstance(value, int):
                eng.sem_inc(passed, 1)

        def chunks(eng, chunk, middle):
            half = SH_CHUNKS // 2
            for lo_c, hi_c, second in ((0, half, False), (half, SH_CHUNKS, True)):
                start = lo_c
                if not second:
                    for c in range(2):
                        chunk(c, c % 2, False)
                    start = lo_c + 2
                stop = hi_c - 2 if second else hi_c
                with eng.Fori(0, (stop - start) // 2) as it:
                    for u in range(2):
                        chunk(it * 2 + (start + u), (start + u) % 2, second)
                if second:
                    for c in range(hi_c - 2, hi_c):
                        chunk(c, c % 2, True)
                else:
                    middle()

        block = ctx.enter_context(nc.Block())

        @block.sync
        def _(sp):
            def load_x(c, u):
                for dst, r0, r1 in ((xr[u][:, 0, :], 0, P), (xr[u][0:W64, 1, :], P, D), (xr[u][W64:P, 1, :], 0, W64),
                                    (xr[u][:, 2, :], W64, D)):
                    sp.dma_start(dst, dram["x2T"][r0:r1, bass.ds(c * CH, CH)]).then_inc(xs_ld[u], 16)

            def load_h(c, u):
                for i in range(2):
                    sp.dma_start(hs[u][:, 2 * i, :], dram["h2"][bass.ds(c * CH + i * TOK, P), :])\
                        .then_inc(hs_ld[u], 16)
                    sp.dma_start(hs[u][0:T1, 2 * i + 1, :], dram["h2"][bass.ds(c * CH + i * TOK + P, T1), :])\
                        .then_inc(hs_ld[u], 16)

            load_x(0, 0)
            load_x(1, 1)
            for e in range(E):
                sp.dma_start(s1[e * CHUNKS:(e + 1) * CHUNKS, :],
                             dram["sT"][e, 0:N].rearrange("(c t) -> c t", c=CHUNKS)).then_inc(s_ld, 16)
            sp.dma_start(s2[:], dram["sT"].rearrange("e (a b) -> a e b", b=P)).then_inc(wld, 16)
            load_h(0, 0)

            def chunk(c, u, second):
                more = not (isinstance(c, int) and c + 1 >= SH_CHUNKS)
                if not (isinstance(c, int) and c + 2 >= SH_CHUNKS):
                    wait_apart(sp, xl_ready, c + 1)
                    load_x(c + 2, u)
                if not (isinstance(c, int) and c == 0):
                    for i in range(2):
                        store(c - 1, 1 - u, i)
                if more:
                    load_h(c + 1, 1 - u)

            def store(c, u, i):
                wait_apart(sp, os_ready, 4 * c + 2 * i + 2)
                sp.dma_start(dram["out"][bass.ds(c * CH + i * TOK, P), :], os_[u][:, 2 * i, :])\
                    .then_inc(os_out[u], 16)
                sp.dma_start(dram["out"][bass.ds(c * CH + i * TOK + P, T1), :], os_[u][0:T1, 2 * i + 1, :])\
                    .then_inc(os_out[u], 16)

            def middle():
                sp.wait_ge(thr_s, STEPS)
                sp.dma_start(dram["thr"], thr[0:P:CHUNKS, :].bitcast(F32)).then_inc(thr_st, 16)
                sp.wait_ge(thr_st, 16)
                sp.dma_start(thr_b[:], dram["thr"].rearrange("e one -> one e").to_broadcast([NBLK, E]))\
                    .then_inc(thr_ld, 16)

            chunks(sp, chunk, middle)
            for i in range(2):
                store(SH_CHUNKS - 1, 1, i)
            for u in range(2):
                sp.wait_ge(os_out[u], 64 * SH_CHUNKS // 2)

        @block.gpsimd
        def _(pool):
            made = [0]

            def made_one(ins):
                made[0] += 1
                ins.then_inc(cst, 1)
                pool.wait_ge(cst, made[0])

            made_one(pool.memset(same_expert[:], 1.0))
            v = same_expert[:].rearrange("p (e c) -> p e c", e=E)
            made_one(pool.affine_select(out=v, in_=v, compare_op=ALU.is_ge, fill=0.0, base=0,
                                        pattern=[[-CHUNKS, E], [0, CHUNKS]], channel_multiplier=1))
            made_one(pool.affine_select(out=v, in_=v, compare_op=ALU.is_ge, fill=0.0, base=CHUNKS - 1,
                                        pattern=[[CHUNKS, E], [0, CHUNKS]], channel_multiplier=-1))
            made_one(pool.memset(ones[:], 1.0))
            made_one(pool.memset(earlier[:], 1.0))
            made_one(pool.affine_select(out=earlier[:], in_=earlier[:], compare_op=ALU.is_gt, fill=0.0, base=0,
                                        pattern=[[1, NBLK]], channel_multiplier=-1))
            assert made[0] == CST_EARLY
            def split_x(c, u):
                wait(pool, xh_ready, c + 1)
                if isinstance(c, int) and c == 1:
                    pool.wait_ge(xl_ready, 1)
                elif not isinstance(c, int) or c > 1:
                    wait(pool, hl_ready, FS * (c - 1))
                pool.tensor_tensor(xs[u][W64:P, 1, :], xr[u][W64:P, 1, :], xs[u][W64:P, 1, :].bitcast(F32),
                                   ALU.subtract).then_inc(x1_ready, 1)
                wait(pool, x1_ready, c + 1)
                pool.tensor_tensor(xs[u][:, 2, :], xr[u][:, 2, :], xs[u][:, 2, :].bitcast(F32), ALU.subtract)\
                    .then_inc(xl_ready, 1)

            def low(c, u, f):
                wait(pool, hh_ready, FS * c + f + 1)
                pool.tensor_tensor(hidl[u][:, f, :], prod[(u + f) % 2][:], hidh[u][:, f, :].bitcast(F32),
                                   ALU.subtract).then_inc(hl_ready, 1)

            split_x(0, 0)

            def chunk(c, u, second):
                if not (isinstance(c, int) and c + 1 >= SH_CHUNKS):
                    split_x(c + 1, 1 - u)
                for f in range(FS):
                    low(c, u, f)

            def middle():
                wait(pool, hl_ready, FS * SH_CHUNKS // 2)
                made_one(pool.memset(keep_run[:], 1.0))
                k = keep_run[:].rearrange("p (e b) -> p e b", e=E)
                made_one(pool.affine_select(out=k, in_=k, compare_op=ALU.not_equal, fill=0.0, base=0,
                                            pattern=[[0, E], [1, P]], channel_multiplier=0))
                made_one(pool.iota(rank[:, :, P:P + 1], pattern=[[0, E], [0, 1]], base=0, channel_multiplier=1,
                                   allow_small_or_imprecise_dtypes=True))
                made_one(pool.iota(slot_no[:], pattern=[[1, CAP]], base=0, channel_multiplier=0,
                                   allow_small_or_imprecise_dtypes=True))
                made_one(pool.iota(jcol[:], pattern=[[P, GT]], base=0, channel_multiplier=1,
                                   allow_small_or_imprecise_dtypes=True))
                made_one(pool.memset(idx_all[:], 0))
                assert made[0] == CST

            chunks(pool, chunk, middle)

        @block.scalar
        def _(act):
            def high_x(c, u):
                wait(act, xs_ld[u], (c - u) * 32 + 64)
                wait(act, g_ps, FS * (c - 1))
                act.activation(xs[u][:], xr[u][:], ACT.Copy).then_inc(xh_ready, 1)

            def silu(c, u, f):
                wait(act, g_ps, FS * c + f + 1)
                wait(act, prod_ready, FS * c + f - 1)
                act.activation(sg[(u + f) % 2][:], ps_g[(u + f) % 2][:, 0:CH], ACT.Silu).then_inc(sg_ready, 1)

            def high(c, u, f):
                wait(act, prod_ready, FS * c + f + 1)
                if f == 0:
                    wait(act, dn_ps, 4 * (c - 1))
                act.activation(hidh[u][:, f, :], prod[(u + f) % 2][:], ACT.Copy).then_inc(hh_ready, 1)

            high_x(0, 0)

            def chunk(c, u, second):
                if not (isinstance(c, int) and c + 1 >= SH_CHUNKS):
                    high_x(c + 1, 1 - u)
                silu(c, u, 0)
                silu(c, u, 1)
                high(c, u, 0)
                high(c, u, 1)
                silu(c, u, 2)
                high(c, u, 2)

            chunks(act, chunk, lambda: None)

        @block.vector
        def _(dve):
            vec = nc.vector
            vec.memset(thr[:], 0).then_inc(thr_init, 1)
            vec.memset(bitf[:], float(1 << 30)).then_inc(thr_init, 1)
            dve.wait_ge(thr_init, 2)
            vec.tensor_copy(biti[:], bitf[:]).then_inc(bit_s, 1)
            dve.wait_ge(bit_s, 1)
            dve.wait_ge(s_ld, 16 * E)

            def count(k):
                wait(dve, thr_s, k)
                wait(dve, bit_s, k + 1)
                vec.tensor_tensor(cand[:], thr[:], biti[:], ALU.bitwise_or).then_inc(cand_s, 1)
                wait(dve, cand_s, k + 1)
                vec.tensor_scalar(hits[:], s1[:], cand[:].bitcast(F32), None, ALU.is_ge, ALU.add,
                                  accum_out=cnt[:]).then_inc(cnt_s, 1)

            def settle(k):
                wait(dve, cnt_ps, k + 1)
                vec.tensor_scalar(inc[:], ps_i[0][:, 0:1], CAP - 0.5, bitf[:], ALU.is_ge, ALU.mult)\
                    .then_inc(inc_s, 1)
                wait(dve, inc_s, k + 1)
                vec.tensor_tensor(thr[:], thr[:], inc[:], ALU.bitwise_or).then_inc(thr_s, 1)
                vec.tensor_scalar(bitf[:], bitf[:], 0.5, None, ALU.mult).then_inc(bitf_s, 1)

            def halve(k):
                wait(dve, bitf_s, k + 1)
                vec.tensor_copy(biti[:], bitf[:]).then_inc(bit_s, 1)

            def product(c, u, f):
                wait(dve, sg_ready, FS * c + f + 1)
                wait(dve, hl_ready, FS * c + f - 1)
                vec.tensor_tensor(prod[(u + f) % 2][:], sg[(u + f) % 2][:], ps_u[(u + f) % 2][:, 0:CH], ALU.mult)\
                    .then_inc(prod_ready, 1)

            def outputs(c, u, i):
                for t in range(2 * i, 2 * i + 2):
                    n = TILES[t % 2][1]
                    wait(dve, dn_ps, 4 * c + t + 1)
                    if t == 0:
                        wait(dve, hs_ld[u], (c - u) * 32 + 64)
                        if not isinstance(c, int) or c >= 2:
                            wait(dve, os_out[u], (c - u) * 32)
                    vec.tensor_tensor(os_[u][0:n, t, :], ps_d[t % 2][0:n, 0:D], hs[u][0:n, t, :], ALU.add)\
                        .then_inc(os_ready, 1)

            def block_starts(j):
                wait(dve, oh_s, j)
                vec.tensor_scalar(ge[:], slot_no[:], lo[:, bass.ds(j, 1)], None, ALU.is_ge).then_inc(oh_ge, 1)

            def block_rows(j):
                wait(dve, ix_ps, NG * j)
                wait(dve, oh_ge, j + 1)
                vec.scalar_tensor_tensor(onehot[:], slot_no[:], hi[:, bass.ds(j, 1)], ge[:], ALU.is_lt, ALU.mult)\
                    .then_inc(oh_s, 1)

            def take(j, u, g):
                t0, t1 = IDX_GROUPS[g]
                wait(dve, ix_ps, NG * j + g + 1)
                bank = ps_i[(u + g) % 2]
                for t in range(t0, t1):
                    n, c0 = rows_of(t), (t - t0) * (P + 1)
                    vec.tensor_scalar(junk[0:n, t, :], bank[0:n, c0:c0 + P], jcol[0:n, t:t + 1], None, ALU.is_le,
                                      ALU.add, accum_out=bcol[0:n, t:t + 1])
                n = rows_of(t1 - 1)
                vec.tensor_copy(acol[0:n, t0:t1],
                                bank[0:n, 0:(t1 - t0) * (P + 1)].rearrange("p (t b) -> p t b", b=P + 1)[:, :, P])\
                    .then_inc(ix_used, 1)

            def write_list(j):
                wait(dve, ix_used, NG * (j + 1) + 2)
                vec.scalar_tensor_tensor(idx_all[:, bass.ds(j * GT, GT)], acol[:], float(P), bcol[:], ALU.mult,
                                         ALU.add).then_inc(list_s, 1)

            def chunk(c, u, second):
                has_out = not (isinstance(c, int) and c == 0)
                if second:
                    j = c - E
                    more = not (isinstance(c, int) and c + 1 >= SH_CHUNKS)
                    product(c, u, 0)
                    product(c, u, 1)
                    wait(dve, list_s, j + 1)
                    take(j, u, 0)
                    take(j, u, 1)
                    outputs(c - 1, 1 - u, 0)
                    take(j, u, 2)
                    if more:
                        block_starts(j + 1)
                    product(c, u, 2)
                    take(j, u, 3)
                    outputs(c - 1, 1 - u, 1)
                    take(j, u, 4)
                    if more:
                        block_rows(j + 1)
                    write_list(j)
                else:
                    count(2 * c)
                    product(c, u, 0)
                    product(c, u, 1)
                    settle(2 * c)
                    halve(2 * c)
                    if has_out:
                        outputs(c - 1, 1 - u, 0)
                    count(2 * c + 1)
                    product(c, u, 2)
                    if has_out:
                        outputs(c - 1, 1 - u, 1)
                    settle(2 * c + 1)
                    halve(2 * c + 1)

            def middle():
                n = [0]

                def step(ins):
                    n[0] += 1
                    ins.then_inc(rk, 1)
                    dve.wait_ge(rk, n[0])

                s2v = s2[:].rearrange("p e b -> p (e b)")
                dve.wait_ge(wld, 16)
                dve.wait_ge(cst, CST)
                dve.wait_ge(thr_ld, 16)
                per_block = thr_b[:, :, None].to_broadcast([NBLK, E, P])
                m3 = mask[:].rearrange("p (e b) -> p e b", e=E)
                for run, op, o in ((g_run, ALU.is_gt, 0), (e_run, ALU.is_equal, E)):
                    step(vec.tensor_tensor(m3, s2[:], per_block, op))
                    step(vec.tensor_tensor_scan(run[:], keep_run[:], mask[:], 0.0, ALU.mult, ALU.add))
                    step(vec.tensor_copy(tots[:, o:o + E], run[:].rearrange("p (e b) -> p e b", e=E)[:, :, P - 1]))
                dve.wait_ge(rk_ps, 1)
                step(vec.tensor_copy(before[:], ps_i[1][0:NBLK, 0:2 * E]))
                step(vec.tensor_scalar(need[:], ps_i[1][0:NBLK, 2 * E:3 * E], -1.0, float(CAP), ALU.mult, ALU.add))
                step(vec.tensor_tensor(lo[:], before[:, E:2 * E], need[:], ALU.min))
                step(vec.tensor_tensor(lo[:], lo[:], before[:, 0:E], ALU.add))
                g3 = g_run[:].rearrange("p (e b) -> p e b", e=E)
                e3 = e_run[:].rearrange("p (e b) -> p e b", e=E)
                step(vec.tensor_tensor(g3, g3, before[:, 0:E, None].to_broadcast([NBLK, E, P]), ALU.add))
                step(vec.tensor_tensor(e3, e3, before[:, E:2 * E, None].to_broadcast([NBLK, E, P]), ALU.add))
                step(vec.tensor_tensor(e3, e3, need[:, :, None].to_broadcast([NBLK, E, P]), ALU.min))
                step(vec.tensor_tensor(rank[:, :, 0:P], g3, e3, ALU.add))
                step(vec.tensor_copy(hi[:], rank[:, :, P - 1]))
                step(vec.memset(bcol[:], 0.0))
                vec.memset(acol[:], 0.0).then_inc(ix_used, 2)
                dve.wait_ge(ix_used, 2)
                dve.sem_inc(list_s, 1)
                block_starts(0)
                block_rows(0)

            chunks(dve, chunk, middle)
            for i in range(2):
                outputs(SH_CHUNKS - 1, 1, i)

        @block.tensor
        def _(pe):
            mm = nc.tensor.matmul
            pe.wait_ge(ws.gu_low, 1)
            pe.wait_ge(ws.d_low, 1)
            pe.wait_ge(cst, CST_EARLY)

            def hidden(c, u, f):
                if f == 0:
                    wait(pe, xl_ready, c + 1)
                wait(pe, prod_ready, FS * c + f - 1)
                for m, bank in ((0, ps_g), (1, ps_u)):
                    for wt, xt in PASSES:
                        last = mm(bank[(u + f) % 2][:, 0:CH], w_gu[:, m, wt, f * P:(f + 1) * P], xs[u][:, xt, :],
                                  start=wt == 0, stop=wt == WT - 1)
                last.then_inc(g_ps, 1)

            def down(c, u, i):
                for t in range(2 * i, 2 * i + 2):
                    t0, n = TILES[t % 2]
                    cols = slice(i * TOK + t0, i * TOK + t0 + n)
                    wait(pe, hl_ready, FS * c + FS)
                    wait(pe, os_ready, 4 * c + t - 1)
                    for k in range(FS):
                        for i_, (hid, part) in enumerate(((hidh, 0), (hidh, 1), (hidl, 0))):
                            last = mm(ps_d[t % 2][0:n, 0:D], hid[u][:, k, cols], w_d[:, k, part, :],
                                      start=k == 0 and i_ == 0, stop=k == FS - 1 and i_ == 2)
                    last.then_inc(dn_ps, 1)

            def count(k):
                wait(pe, cnt_s, k + 1)
                mm(ps_i[0][:, 0:1], same_expert[:], cnt[:], start=True, stop=True).then_inc(cnt_ps, 1)

            def lists(j, u, g):
                t0, t1 = IDX_GROUPS[g]
                if g == 0:
                    wait(pe, oh_s, j + 1)
                (wait if g < NG - 1 else wait_apart)(pe, ix_used, NG * j + g + 1)
                for t in range(t0, t1):
                    n, c0 = rows_of(t), (t - t0) * (P + 1)
                    last = mm(ps_i[(u + g) % 2][0:n, c0:c0 + P + 1], onehot[:, t * P:t * P + n],
                              rank[:, bass.ds(j, 1), :].rearrange("p e b -> p (e b)"), start=True, stop=True)
                last.then_inc(ix_ps, 1)

            def chunk(c, u, second):
                has_out = not (isinstance(c, int) and c == 0)
                hidden(c, u, 0)
                hidden(c, u, 1)
                if second:
                    j = c - E
                    lists(j, u, 0)
                    lists(j, u, 1)
                    down(c - 1, 1 - u, 0)
                    lists(j, u, 2)
                    hidden(c, u, 2)
                    lists(j, u, 3)
                    down(c - 1, 1 - u, 1)
                    lists(j, u, 4)
                else:
                    count(2 * c)
                    if has_out:
                        down(c - 1, 1 - u, 0)
                    hidden(c, u, 2)
                    if has_out:
                        down(c - 1, 1 - u, 1)
                    count(2 * c + 1)

            def middle():
                pe.wait_ge(rk, 6)
                mm(ps_i[1][0:NBLK, 0:2 * E], earlier[:], tots[:], start=True, stop=True)
                mm(ps_i[1][0:NBLK, 2 * E:4 * E], ones[:], tots[:], start=True, stop=True).then_inc(rk_ps, 1)
                pe.wait_ge(rk, 16)

            chunks(pe, chunk, middle)
            for i in range(2):
                down(SH_CHUNKS - 1, 1, i)


def stage_e(nc, dram, idx_all):
    ctx = ExitStack()
    with ctx:
        def sb(name, shape, dt=F32):
            return ctx.enter_context(nc.sbuf_tensor(name, shape, dt))

        def sem(name):
            return ctx.enter_context(nc.semaphore(name))

        CT = 3
        CHN = GT // CT
        FIRST = [c * CT * P for c in range(CHN)] + [CAP]
        CMAX = CAP - FIRST[CHN - 1]
        UNITS = CHN * FT
        TAIL = (CHN - 1) * CT

        w_raw = sb("ew_raw", [P, 2, XT, F_EXP])
        w_gu = sb("ew_gu", [P, 2, WT, F_EXP], F32R)
        wd_raw = sb("ewd_raw", [P, FT, D])
        w_d = [sb(f"ew_d{u}", [P, FT, 2, D], F32R) for u in range(2)]
        xg = [sb(f"xg{u}", [P, GT, ROW]) for u in range(2)]
        xT = [sb(f"xT{u}", [P, XT, CAP], F32R) for u in range(2)]
        score = [sb(f"score{u}", [P, GT]) for u in range(2)]
        idx_g = [sb(f"idx_g{u}", [P, GT], I32) for u in range(2)]
        idx_s = [sb(f"idx_s{u}", [P, GT], I32) for u in range(2)]
        sg = [sb(f"esg{u}", [P, CMAX]) for u in range(2)]
        prod = [sb(f"eprod{u}", [P, CMAX]) for u in range(2)]
        hidh = [sb(f"ehidh{u}", [P, FT, CMAX], F32R) for u in range(2)]
        hidl = [sb(f"ehidl{u}", [P, FT, CMAX], F32R) for u in range(2)]
        y_low = [sb(f"y_low{u}", [P, D]) for u in range(2)]
        y = sb("y", [P, GT, D])
        ident = sb("eident", [P, P])

        ps_g = [ctx.enter_context(nc.psum_tensor(f"eps_g{i}", [P, 512], F32)) for i in range(2)]
        ps_u = [ctx.enter_context(nc.psum_tensor(f"eps_u{i}", [P, 512], F32)) for i in range(2)]
        ps_d = [ctx.enter_context(nc.psum_tensor(f"eps_d{i}", [P, 512], F32)) for i in range(2)]
        ps_t = [ctx.enter_context(nc.psum_tensor(f"eps_t{i}", [P, 512], F32)) for i in range(2)]

        cst = sem("e_cst")
        gu_ld = sem("gu_ld")
        d_ld = sem("d_ld")
        wh_ready = sem("wh_ready")
        wl_ready = sem("wl_ready")
        dh_ready = sem("dh_ready")
        dl_ready = sem("dl_ready")
        gathered = [sem(f"gathered{u}") for u in range(2)]
        scattered = [sem(f"scattered{u}") for u in range(2)]
        idxg_ready = sem("idxg_ready")
        idxs_ready = sem("idxs_ready")
        score_ready = sem("score_ready")
        tr_ps = sem("tr_ps")
        xh_ready = sem("exh_ready")
        xl_ready = sem("exl_ready")
        gu_ps = sem("gu_ps")
        sg_ready = sem("esg_ready")
        prod_ready = sem("eprod_ready")
        hh_ready = sem("ehh_ready")
        hl_ready = sem("ehl_ready")
        dn_ps = sem("edn_ps")
        ylow_ready = sem("ylow_ready")
        y_ready = sem("y_ready")
        passed = sem("passed_e")

        def wait_apart(eng, s, value):
            wait(eng, s, value)
            if not isinstance(value, int):
                eng.sem_inc(passed, 1)

        def order():
            downs = [[(1, t) for t in range(TAIL, GT)]] + \
                    [[(0, t) for t in range(CT * c, CT * c + CT)] for c in range(CHN - 1)]
            turn = nxt = 0
            for c in range(CHN):
                for f in range(FT):
                    yield "gu", c, f
                    if 1 <= f <= len(downs[c]):
                        yield ("dn", *downs[c][f - 1])
                    if c >= 1 and turn < GT and (f < 5 or c == 1):
                        yield "tr", 0, turn
                        turn += 1
                    if (c, f) == (2, 4):
                        yield "wd", 0, 0
                    if c >= 1 and f >= 1 and nxt < GT:
                        yield "ga", 0, nxt
                        nxt += 1
            assert turn == GT and nxt == GT

        def before(c, f):
            if f:
                return 0, c, f - 1
            return (0, c - 1, FT - 1) if c else (1, CHN - 1, FT - 1)

        def is_first(e, c, f):
            return isinstance(e, int) and e == 0 and c == 0 and f == 0

        def size(c):
            return FIRST[c + 1] - FIRST[c]

        def experts(eng, expert):
            for e in range(2):
                expert(e, e % 2, True, True)
            with eng.Fori(0, (E - 4) // 2) as it:
                for u in range(2):
                    expert(it * 2 + (2 + u), u, True, True)
            for e in range(E - 2, E):
                expert(e, e % 2, e + 1 < E, False)

        block = ctx.enter_context(nc.Block())

        @block.sync
        def _(sp):
            def load_gu(e):
                sp.dma_start(w_raw[:], dram["WguT"][bass.ds(e, 1)].rearrange("e p m k f -> (e p) m k f"))\
                    .then_inc(gu_ld, 16)

            def load_d(e):
                sp.dma_start(wd_raw[:], dram["WdT"][bass.ds(e, 1)].rearrange("e p k f -> (e p) k f"))\
                    .then_inc(d_ld, 16)

            load_gu(0)
            load_d(0)

            def expert(e, u, more, more2):
                if more:
                    wait_apart(sp, wl_ready, FT * (e + 1))
                    load_gu(e + 1)
                    wait_apart(sp, dl_ready, e + 1)
                    load_d(e + 1)

            experts(sp, expert)

        @block.gpsimd
        def _(pool):
            made = [0]

            def made_one(ins):
                made[0] += 1
                ins.then_inc(cst, 1)
                pool.wait_ge(cst, made[0])

            made_one(pool.memset(ident[:], 0.0))
            made_one(pool.affine_select(out=ident[:], in_=ident[:], compare_op=ALU.not_equal, fill=1.0, base=0,
                                        pattern=[[-1, P]], channel_multiplier=1))
            made_one(pool.memset(xg[0][:, GT - 1, :], 0.0))
            made_one(pool.memset(xg[1][:, GT - 1, :], 0.0))

            def gather(e, u, t):
                if t == 0:
                    wait(pool, idxg_ready, e + 1)
                    wait(pool, tr_ps, GT * (e - 1))
                    wait_apart(pool, score_ready, e - 1)
                n = rows_of(t)
                pool.indirect_dma_start(
                    out=xg[u][0:n, t, :], out_offset=None, in_=dram["tab"],
                    in_offset=bass.IndirectOffsetOnAxis(ap=idx_g[u][0:n, t:t + 1], axis=0))\
                    .then_inc(gathered[u], 16)

            def scatter(e, u, t):
                if t == 0:
                    wait(pool, idxs_ready, e + 1)
                    if not isinstance(e, int) or e >= 1:
                        wait(pool, scattered[1 - u], (e - (1 - u) + 1) * (16 * GT // 2))
                wait_apart(pool, y_ready, GT * e + t + 1)
                n = rows_of(t)
                pool.indirect_dma_start(
                    out=dram["out"], out_offset=bass.IndirectOffsetOnAxis(ap=idx_s[u][0:n, t:t + 1], axis=0),
                    in_=y[0:n, t, :], in_offset=None, compute_op=ALU.add).then_inc(scattered[u], 16)

            def low_gu(e, f):
                cols = slice(f * P, (f + 1) * P)
                wait(pool, wh_ready, FT * e + f + 1)
                pool.tensor_tensor(w_gu[:, :, XT:WT, cols], w_raw[:, :, 0:2, cols],
                                   w_gu[:, :, 0:2, cols].bitcast(F32), ALU.subtract).then_inc(wl_ready, 1)

            def low_d(e, u):
                wait(pool, dh_ready, e + 1)
                pool.tensor_tensor(w_d[u][:, :, 1, :], wd_raw[:], w_d[u][:, :, 0, :].bitcast(F32), ALU.subtract)\
                    .then_inc(dl_ready, 1)

            for e in range(2):
                for t in range(GT):
                    gather(e, e, t)
            low_d(0, 0)

            def expert(e, u, more, more2):
                last_down = None
                for kind, c, t in order():
                    if kind == "gu" and c == 0 and not (isinstance(e, int) and e == 0) and t == 0:
                        low_gu(e, FT - 1)
                    if kind == "gu" and c == CHN - 1 and t >= 1 and more:
                        low_gu(e + 1, t - 1)
                    if kind == "gu" and last_down is not None:
                        scatter(*last_down)
                        last_down = None
                    if kind == "dn" and c == 0:
                        last_down = (e, u, t)
                    elif kind == "dn" and not (isinstance(e, int) and e == 0):
                        last_down = (e - 1, 1 - u, t)
                    elif kind == "ga" and more2:
                        gather(e + 2, u, t)
                    elif kind == "wd" and more:
                        low_d(e + 1, 1 - u)

            experts(pool, expert)
            for t in range(TAIL, GT):
                scatter(E - 1, (E - 1) % 2, t)
            for u in range(2):
                pool.wait_ge(scattered[u], 16 * GT * E // 2)

        @block.scalar
        def _(act):
            def high_x(e, u, t):
                wait(act, tr_ps, GT * e + t + 1)
                n = rows_of(t)
                act.activation(xT[u][:, :, t * P:t * P + n],
                               ps_t[(u + t) % 2][:, 0:XT * P].rearrange("p (k t) -> p k t", k=XT)[:, :, 0:n],
                               ACT.Copy).then_inc(xh_ready, 1)

            def high_d(e, u):
                wait(act, d_ld, 16 * (e + 1))
                wait(act, dn_ps, GT * (e - 1))
                act.activation(w_d[u][:, :, 0, :], wd_raw[:], ACT.Copy).then_inc(dh_ready, 1)

            def high(back, e, c, f):
                n = UNITS * (e - back) + FT * c + f
                wait(act, prod_ready, n + 1)
                act.activation(hidh[c % 2][:, f, 0:size(c)], prod[f % 2][:, 0:size(c)], ACT.Copy)\
                    .then_inc(hh_ready, 1)

            def low_y(e, u, t):
                n = rows_of(t)
                wait(act, dn_ps, GT * e + t + 1)
                if t == 0:
                    wait(act, score_ready, e + 1)
                wait(act, y_ready, GT * e + t - 1)
                act.activation(y_low[(u + t) % 2][0:n, :], ps_d[(u + t) % 2][0:n, D:2 * D], ACT.Copy,
                               scale=score[u][0:n, t:t + 1]).then_inc(ylow_ready, 1)

            for t in range(GT):
                high_x(0, 0, t)
            high_d(0, 0)

            def expert(e, u, more, more2):
                for kind, c, t in order():
                    if kind == "gu":
                        n = UNITS * e + FT * c + t
                        wait(act, gu_ps, n + 1)
                        wait(act, prod_ready, n - 1)
                        act.activation(sg[t % 2][:, 0:size(c)], ps_g[t % 2][:, 0:size(c)], ACT.Silu)\
                            .then_inc(sg_ready, 1)
                        if not is_first(e, c, t):
                            back, pc, pf = before(c, t)
                            high(back, e, pc, pf)
                    elif kind == "dn" and c == 0:
                        low_y(e, u, t)
                    elif kind == "dn" and not (isinstance(e, int) and e == 0):
                        low_y(e - 1, 1 - u, t)
                    elif kind == "tr" and more:
                        high_x(e + 1, 1 - u, t)
                    elif kind == "wd" and more:
                        high_d(e + 1, 1 - u)

            experts(act, expert)
            high(1, E, CHN - 1, FT - 1)
            for t in range(TAIL, GT):
                low_y(E - 1, (E - 1) % 2, t)

        @block.vector
        def _(dve):
            vec = nc.vector

            def copy_g(e, u):
                if not isinstance(e, int) or e >= 2:
                    wait_apart(dve, gathered[u], (e - u) * (16 * GT // 2))
                vec.tensor_copy(idx_g[u][:], idx_all[:, bass.ds(e * GT, GT)]).then_inc(idxg_ready, 1)

            def copy_score(e, u):
                wait_apart(dve, gathered[u], (e - u) * (16 * GT // 2) + 16 * GT)
                vec.tensor_copy(score[u][:, :], xg[u][:, :, bass.ds(e + SC0, 1)].rearrange("p t one -> p (t one)"))\
                    .then_inc(score_ready, 1)

            def low_x(e, u, t):
                n = rows_of(t)
                wait(dve, xh_ready, GT * e + t + 1)
                for rows, k in ((slice(W64, P), 1), (slice(0, P), 2)):
                    dst = xT[u][rows, k, t * P:t * P + n]
                    last = vec.tensor_tensor(dst, ps_t[(u + t) % 2][rows, k * P:k * P + n], dst.bitcast(F32),
                                             ALU.subtract)
                last.then_inc(xl_ready, 1)

            def high_gu(e, f, used):
                cols = slice(f * P, (f + 1) * P)
                if f == 0:
                    wait(dve, gu_ld, 16 * (e + 1))
                wait(dve, gu_ps, used)
                vec.tensor_copy(w_gu[:, :, 0:XT, cols], w_raw[:, :, :, cols]).then_inc(wh_ready, 1)

            def product(e, c, f):
                wait(dve, sg_ready, UNITS * e + FT * c + f + 1)
                wait(dve, hl_ready, UNITS * e + FT * c + f - 1)
                vec.tensor_tensor(prod[f % 2][:, 0:size(c)], sg[f % 2][:, 0:size(c)], ps_u[f % 2][:, 0:size(c)],
                                  ALU.mult).then_inc(prod_ready, 1)

            def low(back, e, c, f):
                wait(dve, hh_ready, UNITS * (e - back) + FT * c + f + 1)
                vec.tensor_tensor(hidl[c % 2][:, f, 0:size(c)], prod[f % 2][:, 0:size(c)],
                                  hidh[c % 2][:, f, 0:size(c)].bitcast(F32), ALU.subtract).then_inc(hl_ready, 1)

            def scaled(e, u, t):
                n = rows_of(t)
                if t == 0:
                    wait(dve, score_ready, e + 1)
                    if not isinstance(e, int) or e >= 1:
                        wait(dve, scattered[1 - u], (e - (1 - u) + 1) * (16 * GT // 2))
                wait(dve, ylow_ready, GT * e + t + 1)
                vec.scalar_tensor_tensor(y[0:n, t, :], ps_d[(u + t) % 2][0:n, 0:D], score[u][0:n, t:t + 1],
                                         y_low[(u + t) % 2][0:n, :], ALU.mult, ALU.add).then_inc(y_ready, 1)

            copy_g(0, 0)
            copy_g(1, 1)
            for f in range(FT):
                high_gu(0, f, 0)
                wait(dve, wh_ready, f + 1)
                cols = slice(f * P, (f + 1) * P)
                vec.tensor_tensor(w_gu[:, :, XT:WT, cols], w_raw[:, :, 0:2, cols],
                                  w_gu[:, :, 0:2, cols].bitcast(F32), ALU.subtract).then_inc(wl_ready, 1)
            dve.wait_ge(cst, 4)
            copy_score(0, 0)
            for t in range(GT):
                low_x(0, 0, t)

            def expert(e, u, more, more2):
                for kind, c, t in order():
                    if kind == "gu":
                        n = UNITS * e + FT * c + t
                        if c == 0 and t == 0 and not (isinstance(e, int) and e == 0):
                            high_gu(e, FT - 1, n)
                        if c == CHN - 1 and t >= 1 and more:
                            high_gu(e + 1, t - 1, n)
                        product(e, c, t)
                        if not is_first(e, c, t):
                            back, pc, pf = before(c, t)
                            low(back, e, pc, pf)
                        if (c, t) == (0, 4):
                            if more2:
                                copy_g(e + 2, u)
                            if not isinstance(e, int) or e >= 2:
                                wait_apart(dve, scattered[u], (e - u) * (16 * GT // 2))
                            vec.tensor_copy(idx_s[u][:], idx_all[:, bass.ds(e * GT, GT)]).then_inc(idxs_ready, 1)
                    elif kind == "dn" and c == 0:
                        scaled(e, u, t)
                    elif kind == "dn" and not (isinstance(e, int) and e == 0):
                        scaled(e - 1, 1 - u, t)
                    elif kind == "tr" and more:
                        if t == 0:
                            copy_score(e + 1, 1 - u)
                        low_x(e + 1, 1 - u, t)

            experts(dve, expert)
            low(1, E, CHN - 1, FT - 1)
            for t in range(TAIL, GT):
                scaled(E - 1, (E - 1) % 2, t)

        @block.tensor
        def _(pe):
            mm = nc.tensor.matmul
            pe.wait_ge(cst, 4)

            def transposes(e, u, t):
                if t == 0:
                    wait(pe, gathered[u], (e - u) * (16 * GT // 2) + 16 * GT)
                (wait if t < GT - 1 else wait_apart)(pe, xl_ready, GT * e + t - 1)
                n = rows_of(t)
                for k, c0 in enumerate((0, P, W64)):
                    last = nc.tensor.transpose(ps_t[(u + t) % 2][:, k * P:k * P + n], xg[u][0:n, t, c0:c0 + P],
                                               ident[0:n, 0:n])
                last.then_inc(tr_ps, 1)

            def down(e, u, t):
                c = min(t // CT, CHN - 1)
                wait(pe, hl_ready, UNITS * e + FT * (c + 1))
                if t == 0:
                    wait(pe, dl_ready, e + 1)
                wait(pe, y_ready, GT * e + t - 1)
                n = rows_of(t)
                cols = slice(t * P - FIRST[c], t * P - FIRST[c] + n)
                bank = ps_d[(u + t) % 2]
                for k in range(FT):
                    mm(bank[0:n, 0:2 * D], hidh[c % 2][:, k, cols], w_d[u][:, k].rearrange("p h n -> p (h n)"),
                       start=k == 0, stop=False)
                    last = mm(bank[0:n, 0:D], hidl[c % 2][:, k, cols], w_d[u][:, k, 0, :],
                              start=False, stop=k == FT - 1)
                last.then_inc(dn_ps, 1)

            for t in range(GT):
                transposes(0, 0, t)

            def expert(e, u, more, more2):
                for kind, c, t in order():
                    if kind == "gu":
                        n = UNITS * e + FT * c + t
                        if c == 0 and t == 0:
                            wait(pe, xl_ready, GT * (e + 1))
                        if c == 0:
                            wait(pe, wl_ready, FT * e + t + 1)
                        wait(pe, prod_ready, n - 1)
                        for m, bank in ((0, ps_g), (1, ps_u)):
                            for wt, xt in PASSES:
                                last = mm(bank[t % 2][:, 0:size(c)], w_gu[:, m, wt, t * P:(t + 1) * P],
                                          xT[u][:, xt, FIRST[c]:FIRST[c + 1]], start=wt == 0, stop=wt == WT - 1)
                        last.then_inc(gu_ps, 1)
                    elif kind == "dn" and c == 0:
                        down(e, u, t)
                    elif kind == "dn" and not (isinstance(e, int) and e == 0):
                        down(e - 1, 1 - u, t)
                    elif kind == "tr" and more:
                        transposes(e + 1, 1 - u, t)

            experts(pe, expert)
            for t in range(TAIL, GT):
                down(E - 1, (E - 1) % 2, t)


SCRATCH = {"h2": (N, D), "tab": (N, ROW), "x2T": (D, N), "sT": (E, NPAD), "thr": (E, 1)}


def program(nc, dram):
    with nc.sbuf_tensor("idx_all", [P, E * GT], I32) as idx_all:
        with ExitStack() as ctx:
            ws = SharedWeights(nc, ctx)
            stage_a(nc, dram, ws)
            stage_s(nc, dram, idx_all, ws)
        stage_e(nc, dram, idx_all)


def layouts(i):
    import numpy as np

    def stacked(w):
        return np.stack([w[..., 0:P, :], np.concatenate([w[..., P:D, :], w[..., 0:D - P, :]], -2),
                         w[..., D - P:D, :]], -2)

    x = np.asarray(i["x"]).reshape(IMAGES, GRID, PATCH, GRID, PATCH, 3).transpose(0, 2, 4, 5, 1, 3)
    patches = np.zeros((IMAGES, KC * P, TOK), x.dtype)
    patches[:, :, 1:] = x.reshape(IMAGES, DPATCH, GRID * GRID)
    a = {k: np.asarray(v) for k, v in i.items()}
    return {
        "patches": patches.reshape(IMAGES, KC, P, TOK).transpose(0, 2, 1, 3),
        "tok_W": a["L0_tok_W"], "tok_b": a["L0_tok_b"], "cls": a["L0_tok_class_token"],
        "pos": a["L0_tok_pos_emb"], "Wqkv": a["L0_attn_Wqkv"], "bqkv": a["L0_attn_bqkv"],
        "Wout": a["L0_attn_Wout"], "bout": a["L0_attn_bout"], "gateT": a["L0_ffn_gate_weight"].T,
        "WguT": np.stack([stacked(a["L0_ffn_Wg"].transpose(0, 2, 1)), stacked(a["L0_ffn_Wu"].transpose(0, 2, 1))], 2),
        "WdT": a["L0_ffn_Wd"].reshape(E, D, FT, P).transpose(0, 3, 2, 1),
        "WsgT": stacked(a["L0_ffn_Ws_g"].T), "WsuT": stacked(a["L0_ffn_Ws_u"].T),
        "WsdT": a["L0_ffn_Ws_d"].reshape(D, FS, P).transpose(2, 1, 0),
    }


def kernel(**inputs):
    import numpy as np
    import concourse.bacc as bacc
    from concourse.bass_utils import run_bass_kernel_spmd

    nc = bacc.Bacc("TRN2", target_bir_lowering=False, num_devices=1)
    arrays, dram = {}, {}
    for name, a in layouts(inputs).items():
        arrays[f"in_{name}"] = np.ascontiguousarray(a)
        dram[name] = nc.dram_tensor(f"in_{name}", a.shape, mybir.dt.from_np(a.dtype), kind="ExternalInput").ap()
    for name, shape in SCRATCH.items():
        dram[name] = nc.dram_tensor(f"scratch_{name}", shape, F32, kind="Internal").ap()
    dram["out"] = nc.dram_tensor("out", (N, D), F32, kind="ExternalOutput").ap()
    program(nc, dram)
    got = run_bass_kernel_spmd(nc, [arrays], core_ids=[0]).results[0]["out"]
    return got.reshape(IMAGES, TOK, D)
```
